# Optimizing a Trainium2 kernel written in Bass

```python
import numpy as np
import jax
import jax.numpy as jnp

def _softmax(x, axis=-1):
    return jax.nn.softmax(x, axis=axis)

def _gelu(x):
    return jax.nn.gelu(x, approximate=True)

def _silu(x):
    return jax.nn.silu(x)

def _sigmoid(x):
    return jax.nn.sigmoid(x)

def _layernorm(x, axis=-1, eps=1e-05):
    m = jnp.mean(x, axis=axis, keepdims=True)
    v = jnp.var(x, axis=axis, keepdims=True)
    return (x - m) / jnp.sqrt(v + eps)

def _scatter_add(tgt, idx, src, axis=0):
    return tgt.at[idx].add(src)

def _segment_sum(src, seg, n):
    return jax.ops.segment_sum(src, seg, n)
kernel_name = 'mk_adj_ffn_d2_adj_r2_e55379'

def setup_inputs(seed: int=0):
    np.random.seed(seed)
    _w = jnp.asarray

    def _rec_inputs():
        import jax
        import jax.numpy as jnp
        _gk = jax.random.key(seed)
        x = -0.000929 + 1 * jax.random.normal(jax.random.fold_in(_gk, 1), (4096, 128), jnp.float32)
        _a = jax.random.bernoulli(jax.random.fold_in(_gk, 2), 0.000488281, (4096, 4096))
        _a = jnp.logical_or(_a, jnp.eye(4096, dtype=bool))
        _af = _a.astype(jnp.float32)
        _af = _af * jax.random.uniform(jax.random.fold_in(_gk, 3), (4096, 4096), jnp.float32, 0.05, 1)
        adj = _af
        return (x, adj)
    x, adj = _rec_inputs()

    def _L0_gnn_setup():
        import jax, jax.numpy as jnp
        import numpy as np
        N, H, HEADS = (2048, 128, 3)
        ALPHA = 0.2
        NEG_INF = -9000000000000000.0

        def _sign_adj(key, n, density):
            k1, k2 = jax.random.split(key)
            mask = jax.random.uniform(k1, (n, n)) < density
            sign = jnp.where(jax.random.uniform(k2, (n, n)) < 0.5, -1.0, 1.0)
            adj = jnp.where(mask, sign, 0.0).astype(jnp.float32)
            idx = jnp.arange(n)
            return adj.at[idx, idx].set(1.0)

        def _gru_cell(x, hstate, Wih, Whh, bih, bhh):
            gi = x @ Wih.T + bih
            gh = hstate @ Whh.T + bhh
            ir, iz, inn = jnp.split(gi, 3, axis=1)
            hr, hz, hn = jnp.split(gh, 3, axis=1)
            r = jax.nn.sigmoid(ir + hr)
            z = jax.nn.sigmoid(iz + hz)
            n = jnp.tanh(inn + r * hn)
            return (1.0 - z) * n + z * hstate

        def _gat_head(h, node_adj, edge_adj, W, a):
            hW = h @ W
            hp = (node_adj > 0).astype(hW.dtype) @ hW
            hm = (node_adj < 0).astype(hW.dtype) @ hW
            e_plus = jax.nn.leaky_relu(jnp.concatenate([hp, hm], axis=1) @ a, ALPHA)[:, 0]
            e_minus = jax.nn.leaky_relu(jnp.concatenate([hm, hp], axis=1) @ a, ALPHA)[:, 0]
            att = jnp.where(edge_adj > 0, e_plus[None, :], NEG_INF)
            att = jnp.where(edge_adj < 0, e_minus[None, :], att)
            att = jax.nn.softmax(att, axis=1)
            return att * edge_adj @ hW
        key = jax.random.key(seed)
        ks = jax.random.split(key, 16)
        std = 0.01
        gain = 1.414
        return {'h': jax.random.normal(ks[0], (N, H), jnp.float32), 'node_adj': _sign_adj(ks[1], N, 0.005), 'edge_adj': _sign_adj(ks[2], N, 0.005), 'gat_W': jax.random.normal(ks[3], (HEADS, H, H), jnp.float32) * (gain / np.sqrt(H, dtype=np.float32)), 'gat_a': jax.random.normal(ks[4], (HEADS, 2 * H, 1), jnp.float32) * 0.1, 'edge_Wih': jax.random.normal(ks[5], (3 * H, H), jnp.float32) * std, 'edge_Whh': jax.random.normal(ks[6], (3 * H, H), jnp.float32) * std, 'edge_bih': jnp.zeros((3 * H,), jnp.float32), 'edge_bhh': jnp.zeros((3 * H,), jnp.float32), 'node_Wih': jax.random.normal(ks[7], (3 * H, H), jnp.float32) * std, 'node_Whh': jax.random.normal(ks[8], (3 * H, H), jnp.float32) * std, 'node_bih': jnp.zeros((3 * H,), jnp.float32), 'node_bhh': jnp.zeros((3 * H,), jnp.float32)}
    _L0_gnn_all = _L0_gnn_setup()
    _L0_gnn_in = {k: v for k, v in _L0_gnn_all.items() if k in ('gat_W', 'gat_a', 'edge_Wih', 'edge_Whh', 'edge_bih', 'edge_bhh', 'node_Wih', 'node_Whh', 'node_bih', 'node_bhh')}
    del _L0_gnn_all

    def _L0_ffn_setup():
        import jax, jax.numpy as jnp
        import numpy as np
        C = 128
        EPS = 1e-05
        N_ITERS = 30

        def _layernorm(x, w, bias):
            mu = jnp.mean(x, axis=-1, keepdims=True)
            var = jnp.mean(jnp.square(x - mu), axis=-1, keepdims=True)
            return (x - mu) * jax.lax.rsqrt(var + EPS) * w + bias
        key = jax.random.key(seed)
        kx, kw, kb, klw, klb = jax.random.split(key, 5)
        x = jax.random.normal(kx, (8, 1024, C), dtype=jnp.float32)
        bound = 1.0 / np.sqrt(C)
        W = jax.random.uniform(kw, (C, C), minval=-bound, maxval=bound, dtype=jnp.float32)
        b = jax.random.uniform(kb, (C,), minval=-bound, maxval=bound, dtype=jnp.float32)
        ln_w = jnp.ones((C,), dtype=jnp.float32)
        ln_b = jnp.zeros((C,), dtype=jnp.float32)
        return {'x': x, 'ln_w': ln_w, 'ln_b': ln_b, 'W': W, 'b': b}
    _L0_ffn_all = _L0_ffn_setup()
    _L0_ffn_in = {k: v for k, v in _L0_ffn_all.items() if k in ('ln_w', 'ln_b', 'W', 'b')}
    del _L0_ffn_all

    def _L1_gnn_setup():
        import jax, jax.numpy as jnp
        import numpy as np
        N = 10000
        D = 128
        F = 128
        K = F // 8
        key = jax.random.key(seed)
        k1, k2, k3, k4, k5 = jax.random.split(key, 5)
        h = jax.random.normal(k1, (N, D), dtype=jnp.float32)
        adj = jax.random.uniform(k2, (N, N), dtype=jnp.float32)
        W1 = jax.random.normal(k3, (D, K), dtype=jnp.float32) * 0.05
        W2 = jax.random.normal(k4, (K, D, F), dtype=jnp.float32) * 0.05
        b = jax.random.normal(k5, (K, F), dtype=jnp.float32) * 0.05
        return {'h': h, 'adj': adj, 'W1': W1, 'W2': W2, 'b': b}
    _L1_gnn_all = _L1_gnn_setup()
    _L1_gnn_in = {k: v for k, v in _L1_gnn_all.items() if k in ('W1', 'W2', 'b')}
    del _L1_gnn_all

    def _L1_ffn_setup():
        import jax, jax.numpy as jnp
        import numpy as np
        NUM_EXPERTS = 8
        TOP_K = 2
        B, S, D = (8, 4096, 128)

        def _moe(tokens, router_w, w1, b1, w2, b2):
            N = tokens.shape[0]
            E = router_w.shape[0]
            logits = tokens.astype(jnp.float32) @ router_w.astype(jnp.float32).T
            probs = jax.nn.softmax(logits, axis=-1)
            rw, re = jax.lax.top_k(probs, TOP_K)
            if TOP_K > 1:
                rw = rw / jnp.maximum(rw.sum(-1, keepdims=True), 1e-12)
            rw = rw.astype(tokens.dtype)
            combine = jnp.zeros((N, E), tokens.dtype).at[jnp.arange(N)[:, None], re].set(rw)
            out = tokens
            for e in range(E):
                h = jax.nn.gelu(tokens @ w1[e] + b1[e], approximate=False)
                y = h @ w2[e] + b2[e]
                out = out + combine[:, e:e + 1] * y
            return out
        key = jax.random.key(seed)
        ks = jax.random.split(key, 4)
        scale = 1.0 / np.sqrt(D).astype(np.float32)
        return {'input_embeddings': jax.random.normal(ks[0], (B, S, D), jnp.float32), 'router_w': jax.random.normal(ks[1], (NUM_EXPERTS, D), jnp.float32) * scale, 'w1': jax.random.normal(ks[2], (NUM_EXPERTS, D, D), jnp.float32) * scale, 'b1': jnp.zeros((NUM_EXPERTS, D), jnp.float32), 'w2': jax.random.normal(ks[3], (NUM_EXPERTS, D, D), jnp.float32) * scale, 'b2': jnp.zeros((NUM_EXPERTS, D), jnp.float32)}
    _L1_ffn_all = _L1_ffn_setup()
    _L1_ffn_in = {k: v for k, v in _L1_ffn_all.items() if k in ('router_w', 'w1', 'b1', 'w2', 'b2')}
    del _L1_ffn_all
    return {'x': x, 'adj': adj, 'L0_gnn_gat_W': _L0_gnn_in['gat_W'], 'L0_gnn_gat_a': _L0_gnn_in['gat_a'], 'L0_gnn_edge_Wih': _L0_gnn_in['edge_Wih'], 'L0_gnn_edge_Whh': _L0_gnn_in['edge_Whh'], 'L0_gnn_edge_bih': _L0_gnn_in['edge_bih'], 'L0_gnn_edge_bhh': _L0_gnn_in['edge_bhh'], 'L0_gnn_node_Wih': _L0_gnn_in['node_Wih'], 'L0_gnn_node_Whh': _L0_gnn_in['node_Whh'], 'L0_gnn_node_bih': _L0_gnn_in['node_bih'], 'L0_gnn_node_bhh': _L0_gnn_in['node_bhh'], 'L0_ffn_ln_w': _L0_ffn_in['ln_w'], 'L0_ffn_ln_b': _L0_ffn_in['ln_b'], 'L0_ffn_W': _L0_ffn_in['W'], 'L0_ffn_b': _L0_ffn_in['b'], 'L1_gnn_W1': _L1_gnn_in['W1'], 'L1_gnn_W2': _L1_gnn_in['W2'], 'L1_gnn_b': _L1_gnn_in['b'], 'L1_ffn_router_w': _L1_ffn_in['router_w'], 'L1_ffn_w1': _L1_ffn_in['w1'], 'L1_ffn_b1': _L1_ffn_in['b1'], 'L1_ffn_w2': _L1_ffn_in['w2'], 'L1_ffn_b2': _L1_ffn_in['b2']}

def reference(x, adj, L0_gnn_gat_W, L0_gnn_gat_a, L0_gnn_edge_Wih, L0_gnn_edge_Whh, L0_gnn_edge_bih, L0_gnn_edge_bhh, L0_gnn_node_Wih, L0_gnn_node_Whh, L0_gnn_node_bih, L0_gnn_node_bhh, L0_ffn_ln_w, L0_ffn_ln_b, L0_ffn_W, L0_ffn_b, L1_gnn_W1, L1_gnn_W2, L1_gnn_b, L1_ffn_router_w, L1_ffn_w1, L1_ffn_b1, L1_ffn_w2, L1_ffn_b2):
    import jax
    import jax.numpy as jnp

    def _L0_gnn_ref(h, node_adj, edge_adj, gat_W, gat_a, edge_Wih, edge_Whh, edge_bih, edge_bhh, node_Wih, node_Whh, node_bih, node_bhh):
        import jax, jax.numpy as jnp
        import numpy as np
        N, H, HEADS = (2048, 128, 3)
        ALPHA = 0.2
        NEG_INF = -9000000000000000.0

        def _sign_adj(key, n, density):
            k1, k2 = jax.random.split(key)
            mask = jax.random.uniform(k1, (n, n)) < density
            sign = jnp.where(jax.random.uniform(k2, (n, n)) < 0.5, -1.0, 1.0)
            adj = jnp.where(mask, sign, 0.0).astype(jnp.float32)
            idx = jnp.arange(n)
            return adj.at[idx, idx].set(1.0)

        def _gru_cell(x, hstate, Wih, Whh, bih, bhh):
            gi = x @ Wih.T + bih
            gh = hstate @ Whh.T + bhh
            ir, iz, inn = jnp.split(gi, 3, axis=1)
            hr, hz, hn = jnp.split(gh, 3, axis=1)
            r = jax.nn.sigmoid(ir + hr)
            z = jax.nn.sigmoid(iz + hz)
            n = jnp.tanh(inn + r * hn)
            return (1.0 - z) * n + z * hstate

        def _gat_head(h, node_adj, edge_adj, W, a):
            hW = h @ W
            hp = (node_adj > 0).astype(hW.dtype) @ hW
            hm = (node_adj < 0).astype(hW.dtype) @ hW
            e_plus = jax.nn.leaky_relu(jnp.concatenate([hp, hm], axis=1) @ a, ALPHA)[:, 0]
            e_minus = jax.nn.leaky_relu(jnp.concatenate([hm, hp], axis=1) @ a, ALPHA)[:, 0]
            att = jnp.where(edge_adj > 0, e_plus[None, :], NEG_INF)
            att = jnp.where(edge_adj < 0, e_minus[None, :], att)
            att = jax.nn.softmax(att, axis=1)
            return att * edge_adj @ hW
        dn = jnp.diag(node_adj)
        de = jnp.diag(edge_adj)
        idx = jnp.arange(node_adj.shape[0])
        node_adj_norm = node_adj.at[idx, idx].add(-dn)
        edge_adj_norm = edge_adj.at[idx, idx].add(-de)
        node_support = node_adj_norm @ h
        edge_output = _gru_cell(node_support, h, edge_Wih, edge_Whh, edge_bih, edge_bhh)
        edge_support = _gat_head(h, node_adj_norm, edge_adj_norm, gat_W[0], gat_a[0])
        for i in range(1, HEADS):
            edge_support = edge_support + _gat_head(h, node_adj_norm, edge_adj_norm, gat_W[i], gat_a[i])
        edge_support = edge_support / HEADS
        node_output = _gru_cell(edge_support, h, node_Wih, node_Whh, node_bih, node_bhh)
        return de[:, None] * edge_output + dn[:, None] * node_output

    def _L0_ffn_ref(x, ln_w, ln_b, W, b):
        import jax, jax.numpy as jnp
        import numpy as np
        C = 128
        EPS = 1e-05
        N_ITERS = 30

        def _layernorm(x, w, bias):
            mu = jnp.mean(x, axis=-1, keepdims=True)
            var = jnp.mean(jnp.square(x - mu), axis=-1, keepdims=True)
            return (x - mu) * jax.lax.rsqrt(var + EPS) * w + bias

        def step(h, _):
            h = h + 0.01 * jnp.tanh(h)
            h = h * jax.nn.sigmoid(h)
            h = _layernorm(h, ln_w, ln_b)
            h = jnp.einsum('bsc,dc->bsd', h, W) + b
            return (h, None)
        x, _ = jax.lax.scan(step, x, None, length=N_ITERS)
        return x

    def _L1_gnn_ref(h, adj, W1, W2, b):
        import jax, jax.numpy as jnp
        import numpy as np
        N = 10000
        D = 128
        F = 128
        K = F // 8
        node = h @ W1
        hw = jnp.einsum('nc,kcf->nkf', h, W2)
        x = jnp.einsum('nk,nkf->nf', node, hw)
        x = adj @ x
        x = x + node @ b
        return jax.nn.relu(x)

    def _L1_ffn_ref(input_embeddings, router_w, w1, b1, w2, b2):
        import jax, jax.numpy as jnp
        import numpy as np
        NUM_EXPERTS = 8
        TOP_K = 2
        B, S, D = (8, 4096, 128)

        def _moe(tokens, router_w, w1, b1, w2, b2):
            N = tokens.shape[0]
            E = router_w.shape[0]
            logits = tokens.astype(jnp.float32) @ router_w.astype(jnp.float32).T
            probs = jax.nn.softmax(logits, axis=-1)
            rw, re = jax.lax.top_k(probs, TOP_K)
            if TOP_K > 1:
                rw = rw / jnp.maximum(rw.sum(-1, keepdims=True), 1e-12)
            rw = rw.astype(tokens.dtype)
            combine = jnp.zeros((N, E), tokens.dtype).at[jnp.arange(N)[:, None], re].set(rw)
            out = tokens
            for e in range(E):
                h = jax.nn.gelu(tokens @ w1[e] + b1[e], approximate=False)
                y = h @ w2[e] + b2[e]
                out = out + combine[:, e:e + 1] * y
            return out
        b, s, d = input_embeddings.shape
        tokens = input_embeddings.reshape(b * s, d)
        return _moe(tokens, router_w, w1, b1, w2, b2).reshape(b, s, d)
    x = x + _L0_gnn_ref(_layernorm(x, axis=-1), adj, adj, L0_gnn_gat_W, L0_gnn_gat_a, L0_gnn_edge_Wih, L0_gnn_edge_Whh, L0_gnn_edge_bih, L0_gnn_edge_bhh, L0_gnn_node_Wih, L0_gnn_node_Whh, L0_gnn_node_bih, L0_gnn_node_bhh)
    x = x + _L0_ffn_ref(_layernorm(x, axis=-1)[None], L0_ffn_ln_w, L0_ffn_ln_b, L0_ffn_W, L0_ffn_b)[0]
    x = x + _L1_gnn_ref(_layernorm(x, axis=-1), adj, L1_gnn_W1, L1_gnn_W2, L1_gnn_b)
    x = x + _L1_ffn_ref(_layernorm(x, axis=-1)[None], L1_ffn_router_w, L1_ffn_w1, L1_ffn_b1, L1_ffn_w2, L1_ffn_b2)[0]
    return x

_drawn_inputs = setup_inputs


def setup_inputs(seed=0):
    import zlib

    import numpy as np

    out = dict(_drawn_inputs(seed))
    spreads = {'L0_gnn_edge_bih': (0.0, 0.1),
     'L0_gnn_edge_bhh': (0.0, 0.1),
     'L0_gnn_node_bih': (0.0, 0.1),
     'L0_gnn_node_bhh': (0.0, 0.267),
     'L0_ffn_ln_w': (1.0, 0.2),
     'L0_ffn_ln_b': (0.0, 0.1),
     'L1_ffn_b1': (0.0, 0.463),
     'L1_ffn_b2': (0.0, 0.315)}
    factors = {'L0_gnn_gat_W': 2.83, 'L0_gnn_gat_a': 5.397, 'L0_gnn_node_Wih': 2.758}
    for name, (base, spread) in spreads.items():
        noise = np.random.default_rng([zlib.crc32(name.encode()), seed]).standard_normal(out[name].shape)
        drawn = base * np.exp(spread * noise) if base else spread * noise
        out[name] = jnp.asarray(drawn.astype(out[name].dtype))
    for name, factor in factors.items():
        out[name] = (out[name] * factor).astype(out[name].dtype)
    return out
```

```python
from contextlib import ExitStack, contextmanager

import concourse.bass as bass
from concourse import mybir

ALU = mybir.AluOpType
ACT = mybir.ActivationFunctionType
AX_X = mybir.AxisListType.X
F32 = mybir.dt.float32
BF16 = mybir.dt.bfloat16
U32 = mybir.dt.uint32
I32 = mybir.dt.int32
U8 = mybir.dt.uint8

P = 128
NODES = 4096
C = 128
TILES = NODES // P
QUAD = 4
QUADS = TILES // QUAD
BANK = QUAD * C
HEADS = 3
SLOTS = 8
WIDE = C + 2 * HEADS
EPS = 1e-5
ALPHA = 0.2
NEG_INF = -9000000000000000.0
FAR = -1.0e30
KPOLY = 16
EXPERTS = 8
ITERS = 30


class Core:

    def __init__(self, nc, stack):
        self.nc, self.stack = nc, stack

    def sb(self, name, shape, dtype=F32, stack=None):
        return (stack or self.stack).enter_context(self.nc.sbuf_tensor(name, shape, dtype))

    def ps(self, name, shape, stack, dtype=F32):
        return stack.enter_context(self.nc.psum_tensor(name, shape, dtype))

    def sem(self, name):
        return self.stack.enter_context(self.nc.semaphore(name))


class Link:

    def __init__(self, engine, sem, base=0):
        self.engine, self.sem, self.base, self.n = engine, sem, base, 0

    def __call__(self, ins):
        self.n += 1
        ins.then_inc(self.sem, 1)
        self.engine.wait_ge(self.sem, self.base + self.n)


def one(t):
    return bass.ds(t, 1)


def prepare(k, d):
    nc = k.nc
    st = ExitStack()
    with st:
        x = k.sb("x_in", [P, TILES, C], stack=st)
        k.t1 = k.sb("t1", [P, TILES, WIDE], stack=st)
        tile_no = k.sb("tile_no", [1, TILES], I32, stack=st)
        gat_wt = k.sb("gat_wt", [P, HEADS, C], stack=st)
        gat_at = k.sb("gat_at", [P, 2 * HEADS], stack=st)
        wa = k.sb("wa", [P, 2 * HEADS], stack=st)
        h4 = k.sb("h4", [P, QUAD, C], stack=st)
        h4t = k.sb("h4t", [P, BANK], stack=st)
        bank_w = [k.ps(f"bank_w{i}", [P, 512], st) for i in range(HEADS)]
        bank_a = k.ps("bank_a", [P, 512], st)
        bank_t = k.ps("bank_t", [P, 512], st)
        bank_p = k.ps("bank_p", [P, QUAD, 8], st)

        x_in, w_in = k.sem("x_in_s"), k.sem("w_in")
        pool0, made, rsd = k.sem("p0_pool"), k.sem("consts_made"), k.sem("p0_rstd")
        dve, scaled = k.sem("p0_dve"), k.sem("p0_scaled")
        folded, wa_put, ww_put = k.sem("folded"), k.sem("wa_put"), k.sem("ww_put")
        normed, turned, put_t, put_h, prod, put_p = (
            k.sem("p0_normed"), k.sem("p0_turned"), k.sem("p0_put_t"), k.sem("p0_put_h"),
            k.sem("p0_prod"), k.sem("p0_put_p"))
        brow0, table = k.sem("brow_zero"), k.sem("t1_stored")
        stats_in = k.sem("p0_var")

        block = st.enter_context(nc.Block())

        @block.sync
        def _(sp):
            sp.dma_start(x[:, :, :], d["x"].rearrange("(p t) c -> p t c", t=TILES)).then_inc(x_in, 16)
            loads = [
                (gat_wt[:, :, :], d["gat_wt"]), (gat_at[:, :], d["gat_at"]),
                (k.wih_e[:, :], d["wih_e"]), (k.whh_e[:, :], d["whh_e"]),
                (k.wih_n[:, :], d["wih_n"]), (k.whh_n[:, :], d["whh_n"]),
            ]
            for to, of in loads:
                sp.dma_start(to, of).then_inc(w_in, 16)
            sp.wait_ge(brow0, 1)
            for row, bih, bhh in ((k.brow_e, "bih_e", "bhh_e"), (k.brow_n, "bih_n", "bhh_n")):
                sp.dma_start(row[0:1, 0:3 * C], d[bih]).then_inc(w_in, 16)
                sp.dma_start(row[1:2, 0:2 * C], d[bhh][:, 0:2 * C]).then_inc(w_in, 16)
                sp.dma_start(row[1:2, 3 * C:4 * C], d[bhh][:, 2 * C:3 * C]).then_inc(w_in, 16)
            with nc.allow_non_contiguous_dma("the diagonal"):
                diagonal = bass.AP(d["adj"].tensor, 0, [[TILES * (NODES + 1), P], [NODES + 1, TILES]])
                sp.dma_start(k.dcol[:, :], diagonal).then_inc(w_in, 16)
            sp.wait_ge(put_h, QUADS + 1)
            sp.wait_ge(put_p, QUADS)
            sp.dma_start(k.t1_dram.rearrange("(p t) c -> p t c", t=TILES), k.t1[:, :, :]).then_inc(table, 16)
            sp.wait_ge(w_in, 16 * (len(loads) + 7))
            sp.wait_ge(table, 16)

        @block.gpsimd
        def _(pool):
            nc.gpsimd.memset(k.ident[:, :], 0.0).then_inc(pool0, 1)
            pool.wait_ge(pool0, 1)
            nc.gpsimd.affine_select(out=k.ident[:, :], in_=k.ident[:, :], compare_op=ALU.not_equal, fill=1.0,
                                    base=0, pattern=[[-1, P]], channel_multiplier=1).then_inc(made, 1)
            nc.gpsimd.memset(k.minus_half[:, :], -0.5).then_inc(pool0, 1)
            nc.gpsimd.iota(tile_no[:, :], pattern=[[1, TILES]], base=0, channel_multiplier=0).then_inc(pool0, 1)
            pool.wait_ge(pool0, 3)
            nc.gpsimd.tensor_scalar(k.tiles_left[:, :], tile_no[:, :], -1.0, float(TILES), ALU.mult, ALU.add)
            pool.wait_ge(stats_in, 1)
            nc.gpsimd.tensor_tensor(k.rstd[:, :], k.var[:, :], k.minus_half[:, :], ALU.pow).then_inc(rsd, 1)

        @block.vector
        def _(dve_):
            link = Link(dve_, dve)
            nc.vector.memset(k.brow_e[:, :], 0.0)
            nc.vector.memset(k.brow_n[:, :], 0.0).then_inc(brow0, 1)
            nc.vector.memset(k.ones[:, :], 1.0)
            nc.vector.memset(k.tiny[:, :], -1e-30)
            dve_.wait_ge(made, 1)
            link(nc.vector.tensor_scalar(k.not_ident[:, :], k.ident[:, :], -1.0, 1.0, ALU.mult, ALU.add))
            dve_.wait_ge(x_in, 16)
            layer_stats(k, dve_, link, x, stats_in)
            dve_.wait_ge(rsd, 1)
            dve_.wait_ge(folded, 1)
            nc.vector.tensor_copy(wa[:, :], bank_a[:, 0:2 * HEADS]).then_inc(wa_put, 1)
            dve_.sem_inc(turned, 1)
            dve_.sem_inc(put_h, 1)
            with dve_.Fori(0, QUADS) as g:
                dve_.wait_ge(turned, g + 1)
                dve_.wait_ge(put_h, g + 1)
                for j in range(QUAD):
                    ins = nc.vector.tensor_scalar(h4[:, j, :], x[:, one(g * QUAD + j), :],
                                                  k.mean[:, one(g * QUAD + j)], k.rstd[:, one(g * QUAD + j)],
                                                  ALU.subtract, ALU.mult)
                ins.then_inc(normed, 1)
                dve_.wait_ge(prod, g + 1)
                nc.vector.tensor_copy(k.t1[:, bass.ts(g, QUAD), C:WIDE],
                                      bank_p[:, :, 0:2 * HEADS]).then_inc(put_p, 1)

        @block.tensor
        def _(pe):
            pe.wait_ge(w_in, 16 * 13)
            for half in range(2):
                for h in range(HEADS):
                    c = half * HEADS + h
                    mm = nc.tensor.matmul(bank_a[:, c:c + 1], gat_wt[:, h, :], gat_at[:, c:c + 1],
                                          start=True, stop=True)
            mm.then_inc(folded, 1)
            for h in range(HEADS):
                mm = nc.tensor.matmul(bank_w[h][:, 0:3 * C], gat_wt[:, h, :], k.wih_n[:, :],
                                      start=True, stop=True)
            mm.then_inc(folded, 1)
            pe.wait_ge(made, 1)
            pe.wait_ge(wa_put, 1)
            with pe.Fori(0, QUADS) as g:
                pe.wait_ge(normed, g + 1)
                for j in range(QUAD):
                    mm = nc.tensor.transpose(bank_t[:, j * C:(j + 1) * C], h4[:, j, :], k.ident[:, :])
                mm.then_inc(turned, 1)
                pe.wait_ge(put_t, g + 1)
                for j in range(QUAD):
                    mm = nc.tensor.matmul(bank_p[:, j, 0:2 * HEADS], h4t[:, j * C:(j + 1) * C], wa[:, :],
                                          start=True, stop=True)
                mm.then_inc(prod, 1)

        @block.scalar
        def _(act):
            act.wait_ge(folded, 2)
            for h in range(HEADS):
                nc.scalar.activation(k.ww[:, h, :], bank_w[h][:, 0:3 * C], ACT.Copy,
                                     scale=1.0 / HEADS).then_inc(ww_put, 1)
            with act.Fori(0, QUADS) as g:
                act.wait_ge(normed, g + 1)
                nc.scalar.activation(k.t1[:, bass.ts(g, QUAD), 0:C], h4[:, :, :], ACT.Copy).then_inc(put_h, 1)
                act.wait_ge(turned, g + 2)
                nc.scalar.activation(h4t[:, :], bank_t[:, :], ACT.Copy).then_inc(put_t, 1)


def layer_stats(k, eng, link, x, ready):
    nc = k.nc
    stats, dif, sq = k.stats, k.dif, k.sq
    with eng.Fori(0, QUADS) as g:
        for j in range(QUAD):
            ins = nc.vector.bn_stats(stats[:, one(g * QUAD + j), :], x[:, one(g * QUAD + j), :])
        ins.then_inc(k.stats_s, 1)
    k.stats_n += QUADS
    eng.wait_ge(k.stats_s, k.stats_n)
    even_m, even_v, odd_m, odd_v = stats[:, :, 1], stats[:, :, 2], stats[:, :, 4], stats[:, :, 5]
    nc.vector.tensor_tensor(dif[:, :], even_m, odd_m, ALU.subtract)
    nc.vector.tensor_tensor(k.mean[:, :], even_m, odd_m, ALU.add)
    link(nc.vector.scalar_tensor_tensor(k.var[:, :], even_v, C * EPS, odd_v, ALU.add, ALU.add))
    nc.vector.tensor_scalar(k.mean[:, :], k.mean[:, :], 0.5, None, ALU.mult)
    link(nc.vector.scalar_tensor_tensor(sq[:, :], dif[:, :], 0.25, dif[:, :], ALU.mult, ALU.mult))
    nc.vector.scalar_tensor_tensor(k.var[:, :], k.var[:, :], 1.0 / C, sq[:, :],
                                   ALU.mult, ALU.add).then_inc(ready, 1)


def extract(k, d):
    nc = k.nc
    st = ExitStack()
    with st:
        a = [k.sb(f"adj_rows{i}", [P, NODES], stack=st) for i in range(2)]
        signs = k.sb("signs", [P, NODES], BF16, stack=st)
        top = [k.sb(f"top{i}", [P, SLOTS], stack=st) for i in range(2)]
        raw = [k.sb(f"raw_index{i}", [P, SLOTS], U32, stack=st) for i in range(2)]
        off = [k.sb(f"off{i}", [P, SLOTS], stack=st) for i in range(2)]
        cnt = k.sb("cnt", [P, 2, TILES], stack=st)
        found = k.sb("found", [P, TILES, SLOTS], stack=st)
        nfound = k.sb("nfound", [P, TILES], stack=st)
        twice = k.sb("twice", [P, TILES], stack=st)
        bad = k.sb("bad", [P, 2, TILES], stack=st)
        sixes = k.sb("sixes", [P, TILES, 2 * HEADS], stack=st)
        good = k.sb("good", [P, TILES], stack=st)
        keys = [k.sb(f"flag_keys{i}", [1, TILES], stack=st) for i in range(2)]
        order = k.sb("flag_order", [1, TILES], stack=st)
        countf = k.sb("flag_count", [1, 1], stack=st)
        bank = k.ps("bank_flags", [P, 512], st)

        loaded = [k.sem(f"adj_loaded{i}") for i in range(2)]
        undiag, maxed, indexed, off_s, idx_ready = (
            k.sem("undiag"), k.sem("maxed"), k.sem("indexed"), k.sem("off_s"), k.sem("idx_ready"))
        counted, zeroed, dve, summed = k.sem("counted"), k.sem("g_zeroed"), k.sem("p1_dve"), k.sem("bad_summed")
        half_counted, bad_made = k.sem("half_counted"), k.sem("bad_made")
        rows = d["adj"].rearrange("(p t) j -> t p j", t=TILES)
        block = st.enter_context(nc.Block())

        @block.sync
        def _(sp):
            for b in range(2):
                sp.dma_start(a[b][:, :], rows[b]).then_inc(loaded[b], 16)
            for t in range(2, TILES):
                sp.wait_ge(indexed, t - 1)
                sp.wait_ge(counted, t)
                sp.dma_start(a[t % 2][:, :], rows[t]).then_inc(loaded[t % 2], 16)

        @block.scalar
        def _(act):
            act.sem_inc(counted, 1)
            with act.Fori(0, TILES // 2) as i:
                for b in range(2):
                    t = i * 2 + b
                    act.wait_ge(undiag, t + 1)
                    act.wait_ge(counted, t + 1)
                    nc.scalar.activation(signs[:, :], a[b][:, :], ACT.Sign,
                                         accum_out=cnt[:, 0, one(t)]).then_inc(half_counted, 1)
                    act.wait_ge(half_counted, t + 1)
                    nc.scalar.activation(signs[:, :], a[b][:, :], ACT.Sign, bias=k.tiny[:, 0:1],
                                         accum_out=cnt[:, 1, one(t)]).then_inc(counted, 1)

        @block.vector
        def _(dve_):
            def zero_diagonal(i, b):
                dve_.wait_ge(loaded[b], i * 16 + 16)
                diag = a[b][:, :].rearrange("p (q t) -> p q t", t=TILES)[:, :, one(i * 2 + b)]
                nc.vector.tensor_tensor(diag, diag, k.not_ident[:, :].rearrange("p (q o) -> p q o", o=1),
                                        ALU.mult).then_inc(undiag, 1)

            def put_index(t, b):
                dve_.wait_ge(indexed, t + 1)
                dve_.wait_ge(off_s, t + 1)
                nc.vector.tensor_tensor(k.idx[:, one(t), :].rearrange("p a s -> p (a s)"), raw[b][:, :],
                                        off[b][:, :], ALU.add).then_inc(idx_ready, 1)

            def search(t, b):
                nc.vector.max(top[b][:, :], a[b][:, :]).then_inc(maxed, 1)
                dve_.wait_ge(maxed, t + 1)
                nc.vector.tensor_copy(k.val[:, one(t), :].rearrange("p a s -> p (a s)"), top[b][:, :])
                nc.vector.max_index(raw[b][:, :], top[b][:, :], a[b][:, :]).then_inc(indexed, 1)
                nc.vector.tensor_scalar(off[b][:, :], top[b][:, :], 0.0, 2.0 * NODES,
                                        ALU.is_le, ALU.mult).then_inc(off_s, 1)

            zero_diagonal(0, 0)
            dve_.wait_ge(undiag, 1)
            search(0, 0)
            zero_diagonal(0, 1)
            dve_.wait_ge(undiag, 2)
            put_index(0, 0)
            search(1, 1)
            with dve_.Fori(1, TILES // 2) as i:
                for b in range(2):
                    zero_diagonal(i, b)
                    dve_.wait_ge(undiag, i * 2 + (b + 1))
                    put_index(i * 2 + (b - 1), 1 - b)
                    search(i * 2 + b, b)
            put_index(TILES - 1, 1)
            link = Link(dve_, dve)
            link(nc.vector.tensor_scalar(found[:, :, :], k.val[:, :, :], 0.0, None, ALU.is_gt))
            nc.vector.tensor_scalar(k.far[:, :, :], k.val[:, :, :], 0.0, FAR, ALU.is_le, ALU.mult)
            link(nc.vector.tensor_reduce(nfound[:, :], found[:, :, :], AX_X, ALU.add))
            link(nc.vector.tensor_scalar(twice[:, :], nfound[:, :], 2.0, -float(NODES), ALU.mult, ALU.add))
            dve_.wait_ge(counted, TILES + 1)
            nc.vector.tensor_tensor(bad[:, 0, :], cnt[:, 0, :], nfound[:, :], ALU.not_equal)
            nc.vector.tensor_tensor(bad[:, 1, :], cnt[:, 1, :], twice[:, :], ALU.not_equal).then_inc(bad_made, 1)
            dve_.wait_ge(summed, 1)
            link(nc.vector.tensor_scalar(good[:, :], bank[:, 0:TILES], 0.5, None, ALU.is_lt))
            nc.vector.tensor_tensor(k.val[:, :, :], k.val[:, :, :],
                                    good[:, :].rearrange("p (t o) -> p t o", o=1).broadcast_to([P, TILES, SLOTS]),
                                    ALU.mult)
            link(nc.vector.tensor_scalar(keys[0][:, :], good[0:1, :], -1.0, 1.0, ALU.mult, ALU.add))
            link(nc.vector.tensor_reduce(countf[:, :], keys[0][:, :], AX_X, ALU.add))
            nc.vector.tensor_copy(k.count[:, :], countf[:, :])
            link(nc.vector.tensor_tensor(keys[0][:, :], keys[0][:, :], k.tiles_left[:, :], ALU.mult))
            for r in range(TILES // 8):
                eight = order[:, 8 * r:8 * r + 8]
                link(nc.vector.max(eight, keys[r % 2][:, :]))
                if r < TILES // 8 - 1:
                    link(nc.vector.match_replace(out=keys[1 - r % 2][:, :], in_to_replace=eight,
                                                 in_values=keys[r % 2][:, :], imm_value=0.0))
            link(nc.vector.tensor_scalar(k.order[:, :], order[:, :], -1.0, float(TILES), ALU.mult, ALU.add))
            dve_.wait_ge(k.gathered, 16 * TILES * SLOTS)
            quarter = TILES // 4
            for q in range(4):
                ts = slice(q * quarter, (q + 1) * quarter)
                link(nc.vector.tensor_reduce(sixes[:, ts, :], k.g[:, ts, :, C:WIDE].rearrange("p t s c -> p t c s"),
                                             AX_X, ALU.add))
            link(nc.vector.scalar_tensor_tensor(k.e6[:, :, :], sixes[:, :, :], ALPHA, sixes[:, :, :],
                                                ALU.mult, ALU.max))

        @block.tensor
        def _(pe):
            pe.wait_ge(bad_made, 1)
            for i in range(2):
                mm = nc.tensor.matmul(bank[:, 0:TILES], k.ones[:, :], bad[:, i, :], start=(i == 0), stop=(i == 1))
            mm.then_inc(summed, 1)

        @block.gpsimd
        def _(pool):
            nc.gpsimd.memset(k.g[:, :, :, :], 0.0).then_inc(zeroed, 1)
            pool.wait_ge(zeroed, 1)
            for t in range(TILES):
                pool.wait_ge(idx_ready, t + 1)
                for s in range(SLOTS):
                    gather(nc, k.g[:, t, s, :], k.t1_dram, k.idx[:, t, s:s + 1]).then_inc(k.gathered, 16)


def gather(nc, to, table, index):
    return nc.gpsimd.indirect_dma_start(
        out=to, out_offset=None, in_=table, in_offset=bass.IndirectOffsetOnAxis(ap=index, axis=0),
        bounds_check=NODES - 1, oob_is_err=False)


class Turning:

    GROUPS = TILES // 4
    CREDIT = 2

    def __init__(self, k, stack, name, calls):
        self.k, self.calls = k, calls
        self.banks = [k.ps(f"{name}_turn{i}", [P, BANK], stack) for i in range(2)]
        self.turned_sb = [k.sb(f"{name}_turned{i}", [P, BANK], stack=stack) for i in range(2)]
        self.turned, self.copied, self.used = (
            k.sem(f"{name}_turned_s"), k.sem(f"{name}_copied_s"), k.sem(f"{name}_used_s"))

    def start(self, act):
        act.sem_inc(self.copied, self.CREDIT)
        act.sem_inc(self.used, self.CREDIT)

    def base(self, rank, call):
        return rank * (self.calls * self.GROUPS) + call * self.GROUPS

    def done(self, rank, call):
        return rank * (self.calls * self.GROUPS) + ((call + 1) * self.GROUPS + self.CREDIT)

    def multiply(self, pe, rank, call, rows, table, out):
        nc = self.k.nc
        r = rank * (self.calls * self.GROUPS)
        blocks = rows.rearrange("p (q t) -> p q t", t=TILES)
        for g in range(self.GROUPS + 1):
            n = call * self.GROUPS + g
            if g < self.GROUPS:
                pe.wait_ge(self.copied, r + (n + 1))
                for j in range(4):
                    mm = nc.tensor.transpose(self.banks[g % 2][:, j * P:(j + 1) * P], blocks[:, :, 4 * g + j],
                                             self.k.ident[:, :])
                mm.then_inc(self.turned, 1)
            if g >= 1:
                pe.wait_ge(self.copied, r + (n - 1 + 1 + self.CREDIT))
                for j in range(4):
                    b = 4 * (g - 1) + j
                    mm = nc.tensor.matmul(out, self.turned_sb[(g - 1) % 2][:, j * P:(j + 1) * P], table(b),
                                          start=(b == 0), stop=(b == TILES - 1))
                mm.then_inc(self.used, 1)

    def copy(self, act, rank, call):
        nc = self.k.nc
        r = rank * (self.calls * self.GROUPS)
        for g in range(self.GROUPS):
            n = call * self.GROUPS + g
            act.wait_ge(self.turned, r + (n + 1))
            act.wait_ge(self.used, r + (n + 1))
            nc.scalar.activation(self.turned_sb[g % 2][:, :], self.banks[g % 2][:, :], ACT.Copy).then_inc(self.copied, 1)


@contextmanager
def flagged(k, eng):
    count = eng.value_load(k.count[0:1, 0:1], min_val=0, max_val=TILES)
    with eng.If(count > 0):
        with eng.Fori(0, count) as rank:
            yield eng.value_load(k.order[0:1, one(rank)], min_val=0, max_val=TILES - 1), rank
        eng.sem_inc(k.after_flagged, 1)


def dense_logits(k, d):
    nc = k.nc
    st = ExitStack()
    with st:
        rows_sb = k.sb("d1_rows", [P, NODES], stack=st)
        mask = k.sb("d1_mask", [P, NODES], stack=st)
        hwa = k.sb("d1_hwa", [P, TILES, 2 * HEADS], stack=st)
        pos = k.sb("d1_pos", [P, 2 * HEADS], stack=st)
        six = k.sb("d1_six", [P, 2 * HEADS], stack=st)
        acc = [k.ps(f"d1_acc{i}", [P, 512], st) for i in range(2)]
        turning = Turning(k, st, "d1", calls=2)
        table_in, loaded, free = k.sem("d1_table_in"), k.sem("d1_loaded"), k.sem("d1_free")
        undiag, masked, dve = k.sem("d1_undiag"), k.sem("d1_masked"), k.sem("d1_dve")
        rows = d["adj"].rearrange("(p t) j -> t p j", t=TILES)
        block = st.enter_context(nc.Block())

        @block.sync
        def _(sp):
            t1 = k.t1_dram.rearrange("(p t) c -> p t c", t=TILES)
            sp.dma_start(hwa[:, :, :], t1[:, :, C:WIDE]).then_inc(table_in, 16)
            sp.wait_ge(table_in, 16)
            with flagged(k, sp) as (t, rank):
                sp.wait_ge(free, rank + 1)
                sp.wait_ge(table_in, 16)
                sp.dma_start(rows_sb[:, :], rows[one(t)].rearrange("a p j -> p (a j)")).then_inc(loaded, 16)

        @block.vector
        def _(dve_):
            dve_.sem_inc(free, 1)
            with flagged(k, dve_) as (t, rank):
                dve_.wait_ge(loaded, rank * 16 + 16)
                diag = rows_sb[:, :].rearrange("p (q t) -> p q t", t=TILES)[:, :, one(t)]
                nc.vector.tensor_tensor(diag, diag, k.not_ident[:, :].rearrange("p (q o) -> p q o", o=1),
                                        ALU.mult).then_inc(undiag, 1)
                dve_.wait_ge(undiag, rank + 1)
                nc.vector.tensor_scalar(mask[:, :], rows_sb[:, :], 0.0, None, ALU.is_gt).then_inc(masked, 1)
                dve_.wait_ge(turning.used, turning.done(rank, 0))
                nc.vector.tensor_scalar(mask[:, :], rows_sb[:, :], 0.0, None, ALU.is_lt).then_inc(masked, 1)
                link = Link(dve_, dve, rank * 4)
                link(nc.vector.tensor_copy(pos[:, :], acc[0][:, 0:2 * HEADS]))
                dve_.wait_ge(turning.used, turning.done(rank, 1))
                nc.vector.tensor_tensor(six[:, 0:HEADS], pos[:, 0:HEADS], acc[1][:, HEADS:2 * HEADS], ALU.add)
                link(nc.vector.tensor_tensor(six[:, HEADS:], pos[:, HEADS:], acc[1][:, 0:HEADS], ALU.add))
                link(nc.vector.scalar_tensor_tensor(k.e6[:, one(t), :].rearrange("p a c -> p (a c)"), six[:, :],
                                                    ALPHA, six[:, :], ALU.mult, ALU.max))
                link(nc.vector.memset(mask[:, 0:1], 0.0))
                nc.vector.memset(mask[:, 1:2], 0.0).then_inc(free, 1)

        @block.tensor
        def _(pe):
            pe.wait_ge(table_in, 16)
            with flagged(k, pe) as (t, rank):
                for call in range(2):
                    pe.wait_ge(masked, rank * 2 + (call + 1))
                    turning.multiply(pe, rank, call, mask[:, :], lambda b: hwa[:, b, :], acc[call][:, 0:2 * HEADS])

        @block.scalar
        def _(act):
            turning.start(act)
            with flagged(k, act) as (t, rank):
                for call in range(2):
                    turning.copy(act, rank, call)


QUAD_GATHERS = 16 * QUAD * SLOTS


def gather_all(k, pool, to, table, gathered, freed=None):
    for g in range(QUADS):
        if freed is not None:
            freed(g)
        if g >= 2:
            pool.wait_ge(gathered[g % 2], QUAD_GATHERS * (g // 2))
        for t in range(g * QUAD, (g + 1) * QUAD):
            for s in range(SLOTS):
                gather(k.nc, to(t, s), table, k.idx[:, t, s:s + 1]).then_inc(gathered[g % 2], 16)


def attend(k):
    nc = k.nc
    st = ExitStack()
    with st:
        e_pack = k.sb("e_pack", [P, TILES, HEADS], stack=st)
        e_col = k.sb("e_col", [P, 2 * HEADS, TILES], stack=st)
        eg = k.sb("eg", [P, TILES, SLOTS, HEADS], stack=st)
        logit = [k.sb(f"logit{i}", [P, QUAD, HEADS, SLOTS], stack=st) for i in range(2)]
        prob = [k.sb(f"prob{i}", [P, QUAD, HEADS, SLOTS], stack=st) for i in range(2)]
        top = k.sb("row_max", [P, QUAD, HEADS], stack=st)
        den = k.sb("row_sum", [P, QUAD, HEADS], stack=st)
        rden = k.sb("row_rsum", [P, QUAD, HEADS], stack=st)
        weight = k.sb("weight", [P, QUAD, HEADS, SLOTS], stack=st)
        acc = [k.sb(f"sums{i}", [P, BANK], stack=st) for i in range(QUAD)]
        packed, stored, eg0 = k.sem("e_packed"), k.sem("e_stored"), k.sem("eg_zeroed")
        dve, shifted, exped, rounds = k.sem("p2_dve"), k.sem("p2_shifted"), k.sem("p2_exped"), k.sem("p2_rounds")
        tiled = k.sem("p2_tiled")
        out_s = [k.sem(f"p2_out{i}") for i in range(QUAD)]
        gathered = [k.sem(f"e_gathered{i}") for i in range(2)]
        block = st.enter_context(nc.Block())

        @block.sync
        def _(sp):
            sp.wait_ge(packed, 2)
            sp.dma_start(k.e_dram.rearrange("(p t) c -> p t c", t=TILES), e_pack[:, :, :]).then_inc(stored, 16)
            sp.dma_start(k.ecol_dram.rearrange("c (p t) -> p c t", t=TILES), e_col[:, :, :]).then_inc(stored, 16)
            for t in range(TILES):
                sp.wait_ge(tiled, t // 2 + 1)
                sp.dma_start(k.st_dram[t], acc[t % QUAD][:, :]).then_inc(out_s[t % QUAD], 16)
            sp.wait_ge(stored, 32)
            for j in range(QUAD):
                sp.wait_ge(out_s[j], 16 * QUADS + 16)

        @block.gpsimd
        def _(pool):
            nc.gpsimd.memset(eg[:, :, :, :], 0.0).then_inc(eg0, 1)
            pool.wait_ge(eg0, 1)
            pool.wait_ge(stored, 32)
            gather_all(k, pool, lambda t, s: eg[:, t, s, :], k.e_dram, gathered)

        @block.scalar
        def _(act):
            with act.Fori(0, QUADS // 2) as i:
                for b in range(2):
                    act.wait_ge(shifted, i * 2 + (b + 1))
                    nc.scalar.activation(prob[b][:, :, :, :], logit[b][:, :, :, :], ACT.Exp).then_inc(exped, 1)

        @block.vector
        def _(dve_):
            nc.vector.tensor_copy(e_pack[:, :, :], k.e6[:, :, 0:HEADS]).then_inc(packed, 1)
            nc.vector.tensor_copy(e_col[:, :, :], k.e6[:, :, :].rearrange("p t c -> p c t")).then_inc(packed, 1)

            def wide(x):
                return x.rearrange("p t (c o) -> p t c o", o=1).broadcast_to([P, QUAD, HEADS, SLOTS])

            def over_heads(x, g):
                return x[:, bass.ts(g, QUAD), :].rearrange("p t (o s) -> p t o s", o=1).broadcast_to(
                    [P, QUAD, HEADS, SLOTS])

            for j in range(QUAD):
                dve_.sem_inc(out_s[j], 16)
            with dve_.Fori(0, QUADS // 2) as i:
                for b in range(2):
                    g = i * 2 + b
                    link = Link(dve_, dve, g * 6)
                    dve_.wait_ge(gathered[b], i * QUAD_GATHERS + QUAD_GATHERS)
                    lg, pr = logit[b][:, :, :, :], prob[b][:, :, :, :]
                    link(nc.vector.tensor_tensor(lg, eg[:, bass.ts(g, QUAD), :, :].rearrange("p t s c -> p t c s"),
                                                 over_heads(k.far, g), ALU.add))
                    link(nc.vector.tensor_reduce(top[:, :, :], lg, AX_X, ALU.max))
                    nc.vector.tensor_tensor(lg, lg, wide(top[:, :, :]), ALU.subtract).then_inc(shifted, 1)
                    dve_.wait_ge(exped, g + 1)
                    link(nc.vector.tensor_reduce(den[:, :, :], pr, AX_X, ALU.add))
                    link(nc.vector.reciprocal(rden[:, :, :], den[:, :, :]))
                    link(nc.vector.tensor_tensor(weight[:, :, :, :], pr, wide(rden[:, :, :]), ALU.mult))
                    link(nc.vector.tensor_tensor(weight[:, :, :, :], weight[:, :, :, :], over_heads(k.val, g), ALU.mult))
                    for pair in range(2):
                        for j in (2 * pair, 2 * pair + 1):
                            dve_.wait_ge(out_s[j], g * 16 + 16)
                        for s in range(SLOTS):
                            for j in (2 * pair, 2 * pair + 1):
                                t = g * QUAD + j
                                if s > 0:
                                    dve_.wait_ge(rounds, g * (QUAD * SLOTS) + (pair * 2 * SLOTS + 2 * s + j % 2 - 1))
                                row = k.g[:, one(t), s, 0:C].rearrange("p a c -> p (a c)")
                                for h in range(1 + HEADS):
                                    w = (k.val[:, one(t), s] if h == 0 else weight[:, j, h - 1, s:s + 1])
                                    to = acc[j][:, h * C:(h + 1) * C]
                                    if s == 0:
                                        ins = nc.vector.tensor_scalar(to, row, w, None, ALU.mult)
                                    else:
                                        ins = nc.vector.scalar_tensor_tensor(to, row, w, to, ALU.mult, ALU.add)
                                if s == SLOTS - 1 and j % 2:
                                    ins.then_inc(rounds, 1)
                                    nc.vector.drain().then_inc(tiled, 1)
                                else:
                                    ins.then_inc(rounds, 1)


def dense_attend(k, d):
    nc = k.nc
    st = ExitStack()
    with st:
        rows_sb = k.sb("d2_rows", [P, NODES], stack=st)
        e_wide = k.sb("d2_e", [P, NODES], stack=st)
        att = k.sb("d2_att", [P, NODES], stack=st)
        positive = k.sb("d2_pos", [P, NODES], U8, stack=st)
        negative = k.sb("d2_neg", [P, NODES], U8, stack=st)
        h = k.sb("d2_h", [P, TILES, C], stack=st)
        top = k.sb("d2_top", [P, HEADS], stack=st)
        minus_top = k.sb("d2_minus_top", [P, HEADS], stack=st)
        carrier = k.sb("d2_carrier", [P, 2], stack=st)
        den = k.sb("d2_den", [P, HEADS], stack=st)
        rden = k.sb("d2_rden", [P, HEADS], stack=st)
        sums = k.sb("d2_sums", [P, BANK], stack=st)
        acc = [k.ps(f"d2_acc{i}", [P, 512], st) for i in range(2)]
        turning = Turning(k, st, "d2", calls=1 + HEADS)
        table_in, loaded, stored = k.sem("d2_table_in"), k.sem("d2_loaded"), k.sem("d2_stored")
        e_in, e_used, undiag, ready, dve = (
            k.sem("d2_e_in"), k.sem("d2_e_used"), k.sem("d2_undiag"), k.sem("d2_ready"), k.sem("d2_dve"))
        topped, exped, summed = k.sem("d2_topped"), k.sem("d2_exped"), k.sem("d2_summed")
        tile_done = k.sem("d2_tile_done")
        rows = d["adj"].rearrange("(p t) j -> t p j", t=TILES)
        block = st.enter_context(nc.Block())

        @block.sync
        def _(sp):
            t1 = k.t1_dram.rearrange("(p t) c -> p t c", t=TILES)
            sp.dma_start(h[:, :, :], t1[:, :, 0:C]).then_inc(table_in, 16)
            sp.sem_inc(stored, 16)
            with flagged(k, sp) as (t, rank):
                sp.wait_ge(stored, rank * 16 + 16)
                sp.wait_ge(table_in, 16)
                sp.dma_start(rows_sb[:, :], rows[one(t)].rearrange("a p j -> p (a j)")).then_inc(loaded, 16)
                for n in range(2 * HEADS):
                    sp.wait_ge(e_used, rank * (2 * HEADS) + (n + 1))
                    sp.wait_ge(table_in, 16)
                    c = n // 2 + HEADS * (n % 2)
                    sp.dma_start(e_wide[:, :], k.ecol_dram[c:c + 1, :].broadcast_to([P, NODES])).then_inc(e_in, 16)
                sp.wait_ge(summed, rank + 1)
                sp.wait_ge(table_in, 16)
                sp.dma_start(k.st_dram[one(t)].rearrange("a p c -> p (a c)"), sums[:, :]).then_inc(stored, 16)
                sp.wait_ge(stored, rank * 16 + 32)
                sp.sem_inc(tile_done, 1)

        @block.vector
        def _(dve_):
            dve_.sem_inc(e_used, 1)
            with flagged(k, dve_) as (t, rank):
                dve_.wait_ge(loaded, rank * 16 + 16)
                diag = rows_sb[:, :].rearrange("p (q t) -> p q t", t=TILES)[:, :, one(t)]
                nc.vector.tensor_tensor(diag, diag, k.not_ident[:, :].rearrange("p (q o) -> p q o", o=1),
                                        ALU.mult).then_inc(undiag, 1)
                dve_.wait_ge(undiag, rank + 1)
                link = Link(dve_, dve, rank * (2 + 3 * HEADS))
                link(nc.vector.tensor_scalar(positive[:, :], rows_sb[:, :], 0.0, None, ALU.is_gt))
                link(nc.vector.tensor_scalar(negative[:, :], rows_sb[:, :], 0.0, None, ALU.is_lt))
                for n in range(HEADS):
                    if n > 0:
                        dve_.wait_ge(turning.used, turning.done(rank, n))
                    link(nc.vector.memset(att[:, :], NEG_INF))
                    for half, mask in enumerate((positive, negative)):
                        dve_.wait_ge(e_in, rank * (32 * HEADS) + (32 * n + 16 * half + 16))
                        nc.vector.memset(carrier[:, half:half + 1], 0.0)
                        nc.vector.copy_predicated(att[:, :], mask[:, :], e_wide[:, :]).then_inc(e_used, 1)
                        dve_.wait_ge(e_used, rank * (2 * HEADS) + (2 * n + half + 2))
                    link(nc.vector.tensor_reduce(top[:, n:n + 1], att[:, :], AX_X, ALU.max))
                    nc.vector.tensor_scalar(minus_top[:, n:n + 1], top[:, n:n + 1], -1.0, None,
                                            ALU.mult).then_inc(topped, 1)
                    dve_.wait_ge(exped, rank * HEADS + (n + 1))
                    nc.vector.tensor_tensor(att[:, :], att[:, :], rows_sb[:, :], ALU.mult).then_inc(ready, 1)
                    link(nc.vector.reciprocal(rden[:, n:n + 1], den[:, n:n + 1]))
                    if n == 0:
                        dve_.wait_ge(turning.used, turning.done(rank, 0))
                        nc.vector.tensor_copy(sums[:, 0:C], acc[0][:, 0:C])
                    dve_.wait_ge(turning.used, turning.done(rank, n + 1))
                    ins = nc.vector.tensor_scalar(sums[:, (n + 1) * C:(n + 2) * C], acc[(n + 1) % 2][:, 0:C],
                                                  rden[:, n:n + 1], None, ALU.mult)
                ins.then_inc(summed, 1)

        @block.scalar
        def _(act):
            turning.start(act)
            with flagged(k, act) as (t, rank):
                turning.copy(act, rank, 0)
                for n in range(HEADS):
                    act.wait_ge(topped, rank * HEADS + (n + 1))
                    nc.scalar.activation(att[:, :], att[:, :], ACT.Exp, bias=minus_top[:, n:n + 1],
                                         accum_out=den[:, n:n + 1]).then_inc(exped, 1)
                    turning.copy(act, rank, n + 1)

        @block.tensor
        def _(pe):
            pe.wait_ge(table_in, 16)
            with flagged(k, pe) as (t, rank):
                pe.wait_ge(undiag, rank + 1)
                turning.multiply(pe, rank, 0, rows_sb[:, :], lambda b: h[:, b, :], acc[0][:, 0:C])
                for n in range(HEADS):
                    pe.wait_ge(ready, rank * HEADS + (n + 1))
                    turning.multiply(pe, rank, n + 1, att[:, :], lambda b: h[:, b, :], acc[(n + 1) % 2][:, 0:C])


def gates(k, d):
    nc = k.nc
    st = ExitStack()
    with st:
        h = k.sb("gru_h", [P, TILES, C], stack=st)
        sums = [k.sb(f"gru_in{i}", [P, BANK], stack=st) for i in range(2)]
        h1 = [k.sb(f"gru_h{i}", [P, C], stack=st) for i in range(2)]
        sums_t = [k.sb(f"gru_in_t{i}", [P, BANK], stack=st) for i in range(2)]
        h_t = [k.sb(f"gru_h_t{i}", [P, C], stack=st) for i in range(2)]
        rz = [k.sb(f"gru_rz{i}", [P, 2, 2 * C], stack=st) for i in range(2)]
        n_in = [k.sb(f"gru_n_in{i}", [P, 2, C], stack=st) for i in range(2)]
        new = [k.sb(f"gru_new{i}", [P, 2, C], stack=st) for i in range(2)]
        dif = k.sb("gru_dif", [P, 2, C], stack=st)
        both = k.sb("gru_both", [P, C], stack=st)
        bank_s = [k.ps(f"gru_bank_s{i}", [P, BANK], st) for i in range(2)]
        bank_h = [k.ps(f"gru_bank_h{i}", [P, 512], st) for i in range(2)]
        bank_g = [k.ps(f"gru_bank_g{i}", [P, 2, BANK], st) for i in range(2)]
        h_in, x_in = k.sem("gru_h_in"), k.sem("gru_x_in")
        s_in = [k.sem(f"gru_s_in{i}") for i in range(2)]
        picked, turned, copied_s, copied_h, gated = (
            k.sem("gru_picked"), k.sem("gru_turned"), k.sem("gru_copied_s"), k.sem("gru_copied_h"), k.sem("gru_gated"))
        squashed, pre, newed, dve, done = (
            k.sem("gru_squashed"), k.sem("gru_pre"), k.sem("gru_newed"), k.sem("gru_dve"), k.sem("gru_done"))
        block = st.enter_context(nc.Block())

        @block.sync
        def _(sp):
            t1 = k.t1_dram.rearrange("(p t) c -> p t c", t=TILES)
            sp.dma_start(h[:, :, :], t1[:, :, 0:C]).then_inc(h_in, 16)
            sp.dma_start(k.x[:, :, :], d["x"].rearrange("(p t) c -> p t c", t=TILES)).then_inc(x_in, 16)
            for t in range(TILES):
                if t >= 2:
                    sp.wait_ge(turned, t + 1)
                sp.dma_start(sums[t % 2][:, :], k.st_dram[t]).then_inc(s_in[t % 2], 16)

        @block.gpsimd
        def _(pool):
            pool.wait_ge(h_in, 16)
            pool.sem_inc(turned, 2)
            with pool.Fori(0, TILES // 2) as i:
                for b in range(2):
                    t = i * 2 + b
                    pool.wait_ge(turned, t + 1)
                    nc.gpsimd.tensor_copy(h1[b][:, :], h[:, one(t), :].rearrange("p a c -> p (a c)")).then_inc(picked, 1)

        @block.tensor
        def _(pe):
            pe.sem_inc(copied_s, 2)
            pe.sem_inc(copied_h, 2)
            pe.sem_inc(newed, 2)
            pe.sem_inc(pre, 2)

            def turn(i, b):
                t = i * 2 + b
                pe.wait_ge(copied_s, t + 1)
                pe.wait_ge(copied_h, t + 1)
                pe.wait_ge(s_in[b], i * 16 + 16)
                pe.wait_ge(picked, t + 1)
                for j in range(4):
                    nc.tensor.transpose(bank_s[b][:, j * C:(j + 1) * C], sums[b][:, j * C:(j + 1) * C], k.ident[:, :])
                nc.tensor.transpose(bank_h[b][:, 0:C], h1[b][:, :], k.ident[:, :]).then_inc(turned, 1)

            def products(i, b):
                t = i * 2 + b
                pe.wait_ge(copied_s, t + 3)
                pe.wait_ge(copied_h, t + 3)
                pe.wait_ge(pre, t + 1)
                pe.wait_ge(newed, t + 1)
                for cell, (brow, whh) in enumerate(((k.brow_e, k.whh_e), (k.brow_n, k.whh_n))):
                    out = bank_g[b][:, cell, :]
                    nc.tensor.matmul(out[:, 0:BANK], k.ones[0:2, :], brow[:, :], start=True, stop=False)
                    if cell == 0:
                        nc.tensor.matmul(out[:, 0:3 * C], sums_t[b][:, 0:C], k.wih_e[:, :], start=False, stop=False)
                    else:
                        for h_ in range(HEADS):
                            nc.tensor.matmul(out[:, 0:3 * C], sums_t[b][:, (1 + h_) * C:(2 + h_) * C], k.ww[:, h_, :],
                                             start=False, stop=False)
                    nc.tensor.matmul(out[:, 0:2 * C], h_t[b][:, :], whh[:, 0:2 * C], start=False, stop=False)
                    mm = nc.tensor.matmul(out[:, 3 * C:4 * C], h_t[b][:, :], whh[:, 2 * C:3 * C], start=False, stop=True)
                mm.then_inc(gated, 1)

            with pe.Fori(0, TILES // 2) as i:
                turn(i, 0)
                turn(i, 1)
                products(i, 0)
                products(i, 1)

        @block.scalar
        def _(act):
            act.sem_inc(gated, 2)
            with act.Fori(0, TILES // 2) as i:
                for b in range(2):
                    t = i * 2 + b
                    act.wait_ge(turned, t + 3)
                    act.wait_ge(gated, t + 1)
                    nc.scalar.activation(sums_t[b][:, :], bank_s[b][:, :], ACT.Copy).then_inc(copied_s, 1)
                for b in range(2):
                    t = i * 2 + b
                    act.wait_ge(gated, t + 3)
                    act.wait_ge(done, t + 1)
                    nc.scalar.activation(rz[b][:, :, :], bank_g[b][:, :, 0:2 * C], ACT.Sigmoid).then_inc(squashed, 1)
                for b in range(2):
                    t = i * 2 + b
                    act.wait_ge(pre, t + 3)
                    nc.scalar.activation(new[b][:, :, :], n_in[b][:, :, :], ACT.Tanh).then_inc(newed, 1)

        @block.vector
        def _(dve_):
            dve_.wait_ge(x_in, 16)
            dve_.sem_inc(done, 2)
            with dve_.Fori(0, TILES // 2) as i:
                link = Link(dve_, dve, i * 10)
                for b in range(2):
                    t = i * 2 + b
                    dve_.wait_ge(turned, t + 3)
                    dve_.wait_ge(gated, t + 1)
                    nc.vector.tensor_copy(h_t[b][:, :], bank_h[b][:, 0:C]).then_inc(copied_h, 1)
                for b in range(2):
                    t = i * 2 + b
                    dve_.wait_ge(squashed, t + 1)
                    link(nc.vector.tensor_tensor(n_in[b][:, :, :], rz[b][:, :, 0:C], bank_g[b][:, :, 3 * C:4 * C], ALU.mult))
                    nc.vector.tensor_tensor(n_in[b][:, :, :], n_in[b][:, :, :], bank_g[b][:, :, 2 * C:3 * C],
                                            ALU.add).then_inc(pre, 1)
                for b in range(2):
                    t = i * 2 + b
                    dve_.wait_ge(newed, t + 3)
                    hb = h[:, one(t), :].broadcast_to([P, 2, C])
                    link(nc.vector.tensor_tensor(dif[:, :, :], hb, new[b][:, :, :], ALU.subtract))
                    link(nc.vector.tensor_tensor(dif[:, :, :], dif[:, :, :], rz[b][:, :, C:2 * C], ALU.mult))
                    link(nc.vector.tensor_tensor(dif[:, :, :], dif[:, :, :], new[b][:, :, :], ALU.add))
                    link(nc.vector.tensor_tensor(both[:, :], dif[:, 0, :], dif[:, 1, :], ALU.add))
                    xt = k.x[:, one(t), :].rearrange("p a c -> p (a c)")
                    nc.vector.scalar_tensor_tensor(xt, both[:, :], k.dcol[:, one(t)], xt, ALU.mult, ALU.add).then_inc(done, 1)


def ffn_weights(k, d):
    nc = k.nc
    st = ExitStack()
    with st:
        wt = k.sb("ffn_wt_in", [P, C], stack=st)
        w_scaled = k.sb("ffn_w_scaled", [P, C], stack=st)
        ln_w, ln_b = k.sb("ffn_ln_w", [P, 1], stack=st), k.sb("ffn_ln_b", [P, 1], stack=st)
        b_row = k.sb("ffn_b_in", [1, C], stack=st)
        mean_row = k.sb("ffn_ones_mean", [P, P], stack=st)
        bank = k.ps("ffn_w_bank", [P, 512], st)
        bank_b = k.ps("ffn_b_bank", [1, 512], st)
        w_in, scaled, averaged, put = k.sem("ffn_w_in"), k.sem("ffn_w_scaled_s"), k.sem("ffn_averaged"), k.sem("ffn_put")
        rsd, ready, dve = k.sem("ln1_rstd"), k.sem("ln1_var"), k.sem("ln1_dve")
        block = st.enter_context(nc.Block())

        @block.sync
        def _(sp):
            for to, of in ((wt, "ffn_wt"), (ln_w, "ln_w"), (ln_b, "ln_b"), (b_row, "ffn_b")):
                sp.dma_start(to[:, :], d[of]).then_inc(w_in, 16)

        @block.tensor
        def _(pe):
            pe.wait_ge(w_in, 64)
            pe.wait_ge(scaled, 2)
            nc.tensor.matmul(bank[:, 0:C], mean_row[:, :], w_scaled[:, :], start=True, stop=True).then_inc(averaged, 1)
            nc.tensor.matmul(bank_b[:, 0:C], ln_b[:, :], wt[:, :], start=True, stop=False)
            nc.tensor.matmul(bank_b[:, 0:C], k.ones[0:1, 0:1], b_row[:, :], start=False, stop=True).then_inc(averaged, 1)

        @block.gpsimd
        def _(pool):
            pool.wait_ge(ready, 1)
            nc.gpsimd.tensor_tensor(k.rstd[:, :], k.var[:, :], k.minus_half[:, :], ALU.pow).then_inc(rsd, 1)

        @block.vector
        def _(dve_):
            dve_.wait_ge(w_in, 64)
            nc.vector.tensor_scalar(w_scaled[:, :], wt[:, :], ln_w[:, 0:1], None, ALU.mult).then_inc(scaled, 1)
            nc.vector.memset(mean_row[:, :], 1.0 / C).then_inc(scaled, 1)
            link = Link(dve_, dve)
            layer_stats(k, dve_, link, k.x, ready)
            dve_.wait_ge(averaged, 2)
            nc.vector.tensor_tensor(k.ffn_wc[:, :], w_scaled[:, :], bank[:, 0:C], ALU.subtract)
            nc.vector.tensor_copy(k.ffn_bias[:, :], bank_b[:, 0:C])
            dve_.wait_ge(rsd, 1)
            normalise(k, dve_, k.x, k.f0, put, 0)


def normalise(k, eng, x, to, done, base):
    with eng.Fori(0, QUADS) as g:
        for j in range(QUAD):
            t = g * QUAD + j
            ins = k.nc.vector.tensor_scalar(to[:, one(t), :], x[:, one(t), :], k.mean[:, one(t)], k.rstd[:, one(t)],
                                            ALU.subtract, ALU.mult)
        ins.then_inc(done, 1)


def feed_forward(k):
    nc = k.nc
    st = ExitStack()
    with st:
        act_out = [k.sb(f"ffn_silu{i}", [P, QUAD, C], stack=st) for i in range(QUADS)]
        diag = [k.sb(f"ffn_diag{i}", [P, QUAD, C], stack=st) for i in range(QUADS)]
        tanh = [k.sb(f"ffn_tanh{i}", [P, QUAD, C], stack=st) for i in range(2)]
        blend = [k.sb(f"ffn_blend{i}", [P, QUAD, C], stack=st) for i in range(2)]
        turned_sb = [k.sb(f"ffn_turned{i}", [P, BANK], stack=st) for i in range(2)]
        stats = [k.sb(f"ffn_stats{i}", [P, QUAD, 6], stack=st) for i in range(2)]
        dif = k.sb("ffn_dif", [P, QUAD], stack=st)
        sq = k.sb("ffn_sq", [P, QUAD], stack=st)
        both = k.sb("ffn_both", [P, QUAD], stack=st)
        var = [k.sb(f"ffn_var{i}", [P, QUAD], stack=st) for i in range(4)]
        rstd = k.sb("ffn_rstd", [P, QUAD], stack=st)
        bank_t = [k.ps(f"ffn_bank_t{i}", [P, BANK], st) for i in range(4)]
        bank_z = [k.ps(f"ffn_bank_z{i}", [P, BANK], st) for i in range(4)]
        s_tanh, s_blend, s_silu, s_var, s_rstd, s_diag, s_turn, s_copy, s_z, dve = (
            k.sem("ffn_s_tanh"), k.sem("ffn_s_blend"), k.sem("ffn_s_silu"), k.sem("ffn_s_var"), k.sem("ffn_s_rstd"),
            k.sem("ffn_s_diag"), k.sem("ffn_s_turn"), k.sem("ffn_s_copy"), k.sem("ffn_s_z"), k.sem("ffn_dve"))
        ITEMS = ITERS * QUADS
        LINKS = 3
        block = st.enter_context(nc.Block())

        def schedule(eng, stages, first):
            def step(s, base):
                for stage, lag in stages:
                    j = s - lag
                    if base is not None or 0 <= j < ITEMS:
                        stage(j, base)
            last = ITEMS + max(lag for _, lag in stages)
            head = 2 * QUADS
            tail = ITEMS - QUADS
            for s in range(0, head):
                step(s, None)
            with eng.Fori(head // QUADS, tail // QUADS) as it:
                base = it * QUADS
                for g in range(QUADS):
                    step(g, base)
            for s in range(tail, last + 1):
                step(s, None)

        def at(j, base, n):
            return (j + n) if base is None else base + (j + n)

        def wait(eng, sem, j, base, n):
            if base is not None or j + n >= 1:
                eng.wait_ge(sem, at(j, base, n))

        def source(j, base):
            if base is None and j < QUADS:
                return k.f0[:, j * QUAD:(j + 1) * QUAD, :]
            return bank_z[j % 4][:, :].rearrange("p (q c) -> p q c", q=QUAD)

        T_TANH, T_SILU, T_BLEND, T_STATS, T_DIAG = 0, 1, 0, 2, 2
        T_TURN, T_COPY, T_PRODUCT = 5, 5, 6

        @block.scalar
        def _(act):
            def do_tanh(j, base):
                if base is not None or j >= QUADS:
                    wait(act, s_z, j, base, 1 - QUADS)
                wait(act, s_blend, j, base, -1)
                nc.scalar.activation(tanh[j % 2][:, :, :], source(j, base), ACT.Tanh).then_inc(s_tanh, 1)

            def do_silu(j, base):
                wait(act, s_blend, j, base, 1)
                wait(act, s_turn, j, base, 1 - QUADS)
                nc.scalar.activation(act_out[j % QUADS][:, :, :], blend[j % 2][:, :, :], ACT.Silu).then_inc(s_silu, 1)

            def do_copy(j, base):
                wait(act, s_turn, j, base, 1)
                wait(act, s_z, j, base, -1)
                nc.scalar.activation(turned_sb[j % 2][:, :], bank_t[j % 4][:, :], ACT.Copy).then_inc(s_copy, 1)

            schedule(act, [(do_copy, T_COPY), (do_tanh, T_TANH), (do_silu, T_SILU)], 0)

        @block.vector
        def _(dve_):
            def do_blend(j, base):
                wait(dve_, s_tanh, j, base, 1)
                wait(dve_, s_silu, j, base, -1)
                nc.vector.scalar_tensor_tensor(blend[j % 2][:, :, :], tanh[j % 2][:, :, :], 0.01, source(j, base),
                                               ALU.mult, ALU.add).then_inc(s_blend, 1)

            def do_stats(j, base):
                wait(dve_, s_silu, j, base, 1)
                stats_ = stats[j % 2]
                for q in range(QUAD):
                    ins = nc.vector.bn_stats(stats_[:, q, :], act_out[j % QUADS][:, q, :])
                ins.then_inc(dve, 1)
                n = at(j, base, 0) * LINKS
                dve_.wait_ge(dve, n + 1)
                nc.vector.tensor_tensor(dif[:, :], stats_[:, :, 1], stats_[:, :, 4], ALU.subtract)
                nc.vector.scalar_tensor_tensor(both[:, :], stats_[:, :, 2], C * EPS, stats_[:, :, 5],
                                               ALU.add, ALU.add).then_inc(dve, 1)
                dve_.wait_ge(dve, n + 2)
                nc.vector.scalar_tensor_tensor(sq[:, :], dif[:, :], 0.25, dif[:, :], ALU.mult, ALU.mult).then_inc(dve, 1)
                dve_.wait_ge(dve, n + 3)
                wait(dve_, s_rstd, j, base, -3)
                nc.vector.scalar_tensor_tensor(var[j % 4][:, :], both[:, :], 1.0 / C, sq[:, :],
                                               ALU.mult, ALU.add).then_inc(s_var, 1)

            schedule(dve_, [(do_blend, T_BLEND), (do_stats, T_STATS)], 0)
            for g in range(QUADS):
                dve_.wait_ge(s_z, ITEMS - QUADS + g + 1)
                xg = k.x[:, g * QUAD:(g + 1) * QUAD, :]
                nc.vector.tensor_tensor(xg, xg, bank_z[g % 4][:, :].rearrange("p (q c) -> p q c", q=QUAD),
                                        ALU.add).then_inc(s_blend, 1)

        @block.gpsimd
        def _(pool):
            ident = k.ident[:, :].rearrange("p (o c) -> p o c", o=1).broadcast_to([P, QUAD, C])

            def do_diag(j, base):
                wait(pool, s_var, j, base, 1)
                wait(pool, s_diag, j, base, 0)
                nc.gpsimd.tensor_tensor(rstd[:, :], var[j % 4][:, :], k.minus_half[:, 0:QUAD], ALU.pow).then_inc(s_rstd, 1)
                wait(pool, s_rstd, j, base, 1)
                wait(pool, s_turn, j, base, 1 - QUADS)
                nc.gpsimd.tensor_tensor(diag[j % QUADS][:, :, :], ident,
                                        rstd[:, :].rearrange("p (q o) -> p q o", o=1).broadcast_to([P, QUAD, C]),
                                        ALU.mult).then_inc(s_diag, 1)

            schedule(pool, [(do_diag, T_DIAG)], 0)

        @block.tensor
        def _(pe):
            def do_turn(j, base):
                wait(pe, s_diag, j, base, 1)
                wait(pe, s_copy, j, base, -3)
                for q in range(QUAD):
                    mm = nc.tensor.matmul(bank_t[j % 4][:, q * C:(q + 1) * C], act_out[j % QUADS][:, q, :],
                                          diag[j % QUADS][:, q, :], start=True, stop=True)
                mm.then_inc(s_turn, 1)

            def do_product(j, base):
                wait(pe, s_copy, j, base, 1)
                wait(pe, s_blend, j, base, QUADS - 3)
                for q in range(QUAD):
                    out = bank_z[j % 4][:, q * C:(q + 1) * C]
                    nc.tensor.matmul(out, k.ones[0:1, :], k.ffn_bias[:, :], start=True, stop=False)
                    mm = nc.tensor.matmul(out, turned_sb[j % 2][:, q * C:(q + 1) * C], k.ffn_wc[:, :],
                                          start=False, stop=True)
                mm.then_inc(s_z, 1)

            schedule(pe, [(do_turn, T_TURN), (do_product, T_PRODUCT)], 0)


def poly_weights(k, d):
    nc = k.nc
    st = ExitStack()
    with st:
        w1t, bk = k.sb("poly_w1t", [KPOLY, C], stack=st), k.sb("poly_bk", [KPOLY, C], stack=st)
        bank = k.ps("poly_w_bank", [P, 512], st)
        w_in, made, ready, rsd, dve = (
            k.sem("poly_w_in"), k.sem("poly_w_made"), k.sem("ln2_var"), k.sem("ln2_rstd"), k.sem("ln2_dve"))
        block = st.enter_context(nc.Block())

        @block.sync
        def _(sp):
            sp.dma_start(k.poly_w1[:, 0:KPOLY], d["w1"]).then_inc(w_in, 16)
            sp.dma_start(w1t[:, :], d["w1t"]).then_inc(w_in, 16)
            sp.dma_start(bk[:, :], d["bk"]).then_inc(w_in, 16)
            sp.dma_start(k.poly_w2[:, :, :], d["w2"]).then_inc(w_in, 16)

        @block.tensor
        def _(pe):
            pe.wait_ge(w_in, 64)
            nc.tensor.matmul(bank[:, 0:C], w1t[:, :], bk[:, :], start=True, stop=True).then_inc(made, 1)

        @block.gpsimd
        def _(pool):
            pool.wait_ge(ready, 1)
            nc.gpsimd.tensor_tensor(k.rstd[:, :], k.var[:, :], k.minus_half[:, :], ALU.pow).then_inc(rsd, 1)

        @block.vector
        def _(dve_):
            layer_stats(k, dve_, Link(dve_, dve), k.x, ready)
            dve_.wait_ge(made, 1)
            nc.vector.tensor_copy(k.poly_w1[:, KPOLY:], bank[:, 0:C])
            dve_.wait_ge(rsd, 1)


def poly(k):
    nc = k.nc
    st = ExitStack()
    with st:
        h4 = [k.sb(f"poly_h{i}", [P, QUAD, C], stack=st) for i in range(2)]
        h4t = [k.sb(f"poly_ht{i}", [P, BANK], stack=st) for i in range(2)]
        node = [k.sb(f"poly_node{i}", [P, KPOLY], stack=st) for i in range(2)]
        sums = [[k.sb(f"poly_sum{i}_{j}", [P, C], stack=st) for j in range(4)] for i in range(2)]
        bank_t = [k.ps(f"poly_bank_t{i}", [P, BANK], st) for i in range(2)]
        bank_n = [k.ps(f"poly_bank_n{i}", [P, 512], st) for i in range(2)]
        bank_w = [k.ps(f"poly_bank_w{i}", [P, BANK], st) for i in range(4)]
        normed, turned, copied, noded, put, wide, summed, done, stored, zeroed = (
            k.sem("poly_normed"), k.sem("poly_turned"), k.sem("poly_copied"), k.sem("poly_noded"), k.sem("poly_put"),
            k.sem("poly_wide"), k.sem("poly_summed"), k.sem("poly_done"), k.sem("poly_stored"), k.sem("poly_zeroed"))
        block = st.enter_context(nc.Block())

        @block.sync
        def _(sp):
            sp.wait_ge(done, TILES + 2)
            sp.dma_start(k.y_dram.rearrange("(p t) c -> p t c", t=TILES), k.y[:, :, :]).then_inc(stored, 16)
            sp.wait_ge(stored, 16)

        @block.gpsimd
        def _(pool):
            nc.gpsimd.memset(k.yg[:, :, :, :], 0.0).then_inc(zeroed, 1)

        QUAD_WIDE = QUAD * 4
        STEPS = KPOLY + 2

        @block.scalar
        def _(act):
            act.sem_inc(wide, 2 * QUAD_WIDE)
            with act.Fori(0, QUADS // 2) as i:
                for b in range(2):
                    act.wait_ge(turned, i * 2 + (b + 3))
                    act.wait_ge(wide, i * (2 * QUAD_WIDE) + (b + 1) * QUAD_WIDE)
                    nc.scalar.activation(h4t[b][:, :], bank_t[b][:, :], ACT.Copy).then_inc(copied, 1)
                for jj in range(2 * QUAD):
                    t = i * (2 * QUAD) + jj
                    act.wait_ge(noded, t + 1)
                    nc.scalar.activation(k.z[:, one(t), :].rearrange("p a c -> p (a c)"),
                                         bank_n[jj % 2][:, KPOLY:KPOLY + C], ACT.Copy)
                    act.wait_ge(done, t + 1)
                    nc.scalar.activation(node[jj % 2][:, :], bank_n[jj % 2][:, 0:KPOLY], ACT.Copy).then_inc(put, 1)

        @block.vector
        def _(dve_):
            dve_.sem_inc(turned, 2)
            dve_.sem_inc(done, 2)
            dve_.sem_inc(summed, STEPS)
            with dve_.Fori(0, QUADS // 2) as i:
                for b in range(2):
                    dve_.wait_ge(turned, i * 2 + (b + 1))
                    for j in range(QUAD):
                        t = i * (2 * QUAD) + (b * QUAD + j)
                        ins = nc.vector.tensor_scalar(h4[b][:, j, :], k.x[:, one(t), :], k.mean[:, one(t)],
                                                      k.rstd[:, one(t)], ALU.subtract, ALU.mult)
                    ins.then_inc(normed, 1)
                for jj in range(2 * QUAD):
                    t = i * (2 * QUAD) + jj
                    values, part = node[jj % 2], sums[jj % 2]
                    dve_.wait_ge(done, t + 1)
                    dve_.wait_ge(put, t + 3)
                    for m in range(KPOLY):
                        n, c = m // 4, m % 4
                        if c == 0:
                            dve_.wait_ge(wide, t * 4 + (n + 1 + 2 * QUAD_WIDE))
                        product, w, to = bank_w[n][:, c * C:(c + 1) * C], values[:, m:m + 1], part[c][:, :]
                        if n == 0:
                            ins = nc.vector.tensor_scalar(to, product, w, None, ALU.mult)
                        else:
                            dve_.wait_ge(summed, t * STEPS + (STEPS + m - 3))
                            ins = nc.vector.scalar_tensor_tensor(to, product, w, to, ALU.mult, ALU.add)
                        ins.then_inc(summed, 1)
                    dve_.wait_ge(summed, t * STEPS + (STEPS + KPOLY - 2))
                    nc.vector.tensor_tensor(part[0][:, :], part[0][:, :], part[1][:, :], ALU.add).then_inc(summed, 1)
                    dve_.wait_ge(summed, t * STEPS + (STEPS + KPOLY))
                    nc.vector.tensor_tensor(part[2][:, :], part[2][:, :], part[3][:, :], ALU.add).then_inc(summed, 1)
                    dve_.wait_ge(summed, t * STEPS + (STEPS + KPOLY + 2))
                    nc.vector.tensor_tensor(k.y[:, one(t), :].rearrange("p a c -> p (a c)"), part[0][:, :],
                                            part[2][:, :], ALU.add).then_inc(done, 1)

        @block.tensor
        def _(pe):
            pe.sem_inc(copied, 2)
            pe.sem_inc(put, 2)
            with pe.Fori(0, QUADS // 2) as i:
                for b in range(2):
                    pe.wait_ge(normed, i * 2 + (b + 1))
                    pe.wait_ge(copied, i * 2 + (b + 1))
                    for j in range(QUAD):
                        mm = nc.tensor.transpose(bank_t[b][:, j * C:(j + 1) * C], h4[b][:, j, :], k.ident[:, :])
                    mm.then_inc(turned, 1)
                for jj in range(2 * QUAD):
                    b, j = jj // QUAD, jj % QUAD
                    t = i * (2 * QUAD) + jj
                    if j == 0:
                        pe.wait_ge(copied, i * 2 + (b + 3))
                    lhs = h4t[b][:, j * C:(j + 1) * C]
                    pe.wait_ge(put, t + 1)
                    nc.tensor.matmul(bank_n[jj % 2][:, 0:KPOLY + C], lhs, k.poly_w1[:, :], start=True,
                                     stop=True).then_inc(noded, 1)
                    for n in range(4):
                        pe.wait_ge(summed, t * STEPS + 4 * (n + 1))
                        nc.tensor.matmul(bank_w[n][:, :], lhs, k.poly_w2[:, 4 * n:4 * n + 4, :], start=True,
                                         stop=True).then_inc(wide, 1)


RING = 4


def spread(k):
    nc = k.nc
    st = ExitStack()
    with st:
        gathered = [k.sem(f"y_gathered{i}") for i in range(2)]
        rounds = k.sem("z_rounds")
        block = st.enter_context(nc.Block())

        @block.gpsimd
        def _(pool):
            def freed(g):
                if g >= RING:
                    pool.wait_ge(rounds, (g - RING + 1) * QUAD * (SLOTS + 1))

            gather_all(k, pool, lambda t, s: k.yg[:, t % (RING * QUAD), s, :], k.y_dram, gathered, freed)

        @block.vector
        def _(dve_):
            with dve_.Fori(0, QUADS // RING) as i:
                for b in range(RING):
                    dve_.wait_ge(gathered[b % 2], i * (RING // 2 * QUAD_GATHERS) + (b // 2 + 1) * QUAD_GATHERS)
                    for s in range(-1, SLOTS):
                        for j in range(QUAD):
                            n = (i * RING + b) * (QUAD * (SLOTS + 1)) + (s + 1) * QUAD + j
                            t = i * (RING * QUAD) + (b * QUAD + j)
                            slot = b * QUAD + j
                            to = k.z[:, one(t), :].rearrange("p a c -> p (a c)")
                            if s < 0:
                                row, w = k.y[:, one(t), :].rearrange("p a c -> p (a c)"), k.dcol[:, one(t)]
                            else:
                                row, w = k.yg[:, slot, s, :], k.val[:, one(t), s]
                                dve_.wait_ge(rounds, n - 3)
                            nc.vector.scalar_tensor_tensor(to, row, w, to, ALU.mult, ALU.add).then_inc(rounds, 1)


def dense_spread(k, d):
    nc = k.nc
    st = ExitStack()
    with st:
        rows_sb = k.sb("d3_rows", [P, NODES], stack=st)
        acc = k.ps("d3_acc", [P, 512], st)
        turning = Turning(k, st, "d3", calls=1)
        loaded, free, undiag = k.sem("d3_loaded"), k.sem("d3_free"), k.sem("d3_undiag")
        rows = d["adj"].rearrange("(p t) j -> t p j", t=TILES)
        block = st.enter_context(nc.Block())

        @block.sync
        def _(sp):
            with flagged(k, sp) as (t, rank):
                sp.wait_ge(free, rank + 1)
                sp.sem_inc(k.sp_ticks, 1)
                sp.dma_start(rows_sb[:, :], rows[one(t)].rearrange("a p j -> p (a j)")).then_inc(loaded, 16)

        @block.vector
        def _(dve_):
            dve_.sem_inc(free, 1)
            with flagged(k, dve_) as (t, rank):
                z = k.z[:, one(t), :].rearrange("p a c -> p (a c)")
                dve_.wait_ge(loaded, rank * 16 + 16)
                diag = rows_sb[:, :].rearrange("p (q t) -> p q t", t=TILES)[:, :, one(t)]
                nc.vector.tensor_tensor(diag, diag, k.not_ident[:, :].rearrange("p (q o) -> p q o", o=1),
                                        ALU.mult).then_inc(undiag, 1)
                dve_.wait_ge(turning.used, turning.done(rank, 0))
                nc.vector.tensor_tensor(z, acc[:, 0:C], z, ALU.add).then_inc(free, 1)

        @block.tensor
        def _(pe):
            with flagged(k, pe) as (t, rank):
                pe.wait_ge(undiag, rank + 1)
                turning.multiply(pe, rank, 0, rows_sb[:, :], lambda b: k.y[:, b, :], acc[:, 0:C])

        @block.scalar
        def _(act):
            turning.start(act)
            with flagged(k, act) as (t, rank):
                turning.copy(act, rank, 0)


def settle(k, d):
    nc = k.nc
    st = ExitStack()
    with st:
        w_in, ready, rsd, dve = k.sem("moe_w_in"), k.sem("ln3_var"), k.sem("ln3_rstd"), k.sem("ln3_dve")
        block = st.enter_context(nc.Block())

        @block.sync
        def _(sp):
            loads = [(k.router, "router_t"), (k.e_w1, "e_w1"), (k.e_w2, "e_w2"), (k.e_b1, "e_b1"), (k.e_b2, "e_b2")]
            for to, of in loads:
                sp.dma_start(to[(slice(None),) * len(to.shape)], d[of]).then_inc(w_in, 16)
            sp.wait_ge(w_in, 16 * len(loads))

        @block.gpsimd
        def _(pool):
            nc.gpsimd.iota(k.expert_no_i[:, :], pattern=[[1, EXPERTS]], base=0, channel_multiplier=0).then_inc(rsd, 1)
            pool.wait_ge(rsd, 1)
            nc.gpsimd.tensor_copy(k.expert_no[:, :], k.expert_no_i[:, :])
            pool.wait_ge(ready, 1)
            nc.gpsimd.tensor_tensor(k.rstd[:, :], k.var[:, :], k.minus_half[:, :], ALU.pow).then_inc(rsd, 1)

        @block.vector
        def _(dve_):
            link = Link(dve_, dve)
            link(nc.vector.scalar_tensor_tensor(k.x[:, :, :], k.z[:, :, :], 0.0, k.x[:, :, :], ALU.max, ALU.add))
            layer_stats(k, dve_, link, k.x, ready)


def route(k):
    nc = k.nc
    st = ExitStack()
    with st:
        h4 = [k.sb(f"moe_h{i}", [P, QUAD, C], stack=st) for i in range(2)]
        h4t = [k.sb(f"moe_ht{i}", [P, BANK], stack=st) for i in range(2)]
        wide = [P, TILES, EXPERTS]
        logit, prob, sorted_p, mask = (k.sb(f"moe_{n}", wide, stack=st) for n in ("logit", "prob", "sorted", "mask"))
        index = k.sb("moe_index", wide, U32, stack=st)
        index_f = k.sb("moe_index_f", [P, TILES, 2], stack=st)
        top, den, rden = (k.sb(f"moe_{n}", [P, TILES], stack=st) for n in ("top", "den", "rden"))
        bank_t = [k.ps(f"moe_bank_t{i}", [P, BANK], st) for i in range(2)]
        bank_l = [k.ps(f"moe_bank_l{i}", [P, QUAD, EXPERTS], st) for i in range(2)]
        normed, turned, copied, kept, routed, taken, dve, shifted, exped, added = (
            k.sem("moe_normed"), k.sem("moe_turned"), k.sem("moe_copied"), k.sem("moe_kept"), k.sem("moe_routed"),
            k.sem("moe_taken"), k.sem("moe_dve"), k.sem("moe_shifted"), k.sem("moe_exped"), k.sem("moe_added"))
        block = st.enter_context(nc.Block())

        @block.scalar
        def _(act):
            act.sem_inc(routed, 2)
            act.sem_inc(kept, 2)
            with act.Fori(0, QUADS // 2) as i:
                for b in range(2):
                    act.wait_ge(turned, i * 2 + (b + 3))
                    act.wait_ge(routed, i * 2 + (b + 1))
                    act.wait_ge(kept, i * 2 + (b + 1))
                    nc.scalar.activation(h4t[b][:, :], bank_t[b][:, :], ACT.Copy).then_inc(copied, 1)
            act.wait_ge(shifted, 1)
            nc.scalar.activation(prob[:, :, :], prob[:, :, :], ACT.Exp).then_inc(exped, 1)

        @block.gpsimd
        def _(pool):
            with pool.Fori(0, QUADS // 2) as i:
                for b in range(2):
                    pool.wait_ge(copied, i * 2 + (b + 3))
                    nc.gpsimd.tensor_copy(k.ht[:, one(i * 2 + b), :].rearrange("p a c -> p (a c)"),
                                          h4t[b][:, :]).then_inc(kept, 1)

        @block.tensor
        def _(pe):
            pe.sem_inc(copied, 2)
            pe.sem_inc(taken, 2)
            with pe.Fori(0, QUADS // 2) as i:
                for b in range(2):
                    pe.wait_ge(normed, i * 2 + (b + 1))
                    pe.wait_ge(copied, i * 2 + (b + 1))
                    for j in range(QUAD):
                        mm = nc.tensor.transpose(bank_t[b][:, j * C:(j + 1) * C], h4[b][:, j, :], k.ident[:, :])
                    mm.then_inc(turned, 1)
                for b in range(2):
                    pe.wait_ge(copied, i * 2 + (b + 3))
                    pe.wait_ge(taken, i * 2 + (b + 1))
                    for j in range(QUAD):
                        mm = nc.tensor.matmul(bank_l[b][:, j, :], h4t[b][:, j * C:(j + 1) * C], k.router[:, :],
                                              start=True, stop=True)
                    mm.then_inc(routed, 1)

        @block.vector
        def _(dve_):
            dve_.sem_inc(turned, 2)
            dve_.sem_inc(added, 2)
            with dve_.Fori(0, QUADS // 2) as i:
                for b in range(2):
                    dve_.wait_ge(turned, i * 2 + (b + 1))
                    dve_.wait_ge(added, i * 2 + (b + 1))
                    for j in range(QUAD):
                        t = i * (2 * QUAD) + (b * QUAD + j)
                        ins = nc.vector.tensor_scalar(h4[b][:, j, :], k.x[:, one(t), :], k.mean[:, one(t)],
                                                      k.rstd[:, one(t)], ALU.subtract, ALU.mult)
                    ins.then_inc(normed, 1)
                for b in range(2):
                    dve_.wait_ge(normed, i * 2 + (b + 1))
                    xg = k.x[:, bass.ts(i * 2 + b, QUAD), :]
                    nc.vector.tensor_tensor(xg, xg, h4[b][:, :, :], ALU.add).then_inc(added, 1)
                for b in range(2):
                    dve_.wait_ge(routed, i * 2 + (b + 3))
                    nc.vector.tensor_copy(logit[:, bass.ts(i * 2 + b, QUAD), :], bank_l[b][:, :, :]).then_inc(taken, 1)
            dve_.wait_ge(taken, QUADS + 2)
            link = Link(dve_, dve)

            def wide_of(x):
                return x.rearrange("p (t o) -> p t o", o=1).broadcast_to(wide)

            link(nc.vector.tensor_reduce(top[:, :], logit[:, :, :], AX_X, ALU.max))
            nc.vector.tensor_tensor(prob[:, :, :], logit[:, :, :], wide_of(top[:, :]), ALU.subtract).then_inc(shifted, 1)
            dve_.wait_ge(exped, 1)
            link(nc.vector.tensor_reduce(den[:, :], prob[:, :, :], AX_X, ALU.add))
            link(nc.vector.reciprocal(rden[:, :], den[:, :]))
            link(nc.vector.tensor_tensor(prob[:, :, :], prob[:, :, :], wide_of(rden[:, :]), ALU.mult))
            for t in range(TILES):
                ins = nc.vector.max(sorted_p[:, t, :], prob[:, t, :])
            link(ins)
            for t in range(TILES):
                ins = nc.vector.max_index(index[:, t, :], sorted_p[:, t, :], prob[:, t, :])
            link(ins)
            link(nc.vector.tensor_copy(index_f[:, :, :], index[:, :, 0:2]))
            link(nc.vector.tensor_tensor(den[:, :], sorted_p[:, :, 0], sorted_p[:, :, 1], ALU.add))
            link(nc.vector.tensor_scalar(den[:, :], den[:, :], 1e-12, None, ALU.max))
            link(nc.vector.reciprocal(rden[:, :], den[:, :]))
            number = k.expert_no[:, :].rearrange("p (o e) -> p o e", o=1).broadcast_to(wide)
            link(nc.vector.tensor_tensor(k.combine[:, :, :], number, wide_of(index_f[:, :, 0]), ALU.is_equal))
            link(nc.vector.tensor_tensor(mask[:, :, :], number, wide_of(index_f[:, :, 1]), ALU.is_equal))
            link(nc.vector.tensor_tensor(mask[:, :, :], mask[:, :, :], k.combine[:, :, :], ALU.add))
            link(nc.vector.tensor_tensor(mask[:, :, :], mask[:, :, :], prob[:, :, :], ALU.mult))
            nc.vector.tensor_tensor(k.combine[:, :, :], mask[:, :, :], wide_of(rden[:, :]), ALU.mult)


def experts(k, out):
    nc = k.nc
    st = ExitStack()
    with st:
        hidden = [k.sb(f"moe_hidden{i}", [P, BANK], stack=st) for i in range(2)]
        bank_1 = [k.ps(f"moe_bank_1{i}", [P, BANK], st) for i in range(2)]
        bank_2 = [k.ps(f"moe_bank_2{i}", [P, BANK], st) for i in range(4)]
        first, gelued, second, mixed = k.sem("moe_first"), k.sem("moe_gelued"), k.sem("moe_second"), k.sem("moe_mixed")
        stored = k.sem("out_stored")
        out_rows = out.rearrange("(p t) c -> p t c", t=TILES)
        FREE_1, FREE_2 = 2, 4 * QUAD
        block = st.enter_context(nc.Block())

        @block.sync
        def _(sp):
            for g in range(QUADS):
                sp.wait_ge(mixed, FREE_2 + QUAD * EXPERTS * (g + 1))
                ts = slice(g * QUAD, (g + 1) * QUAD)
                sp.dma_start(out_rows[:, ts, :], k.x[:, ts, :]).then_inc(stored, 16)
            sp.wait_ge(stored, 16 * QUADS)

        @block.tensor
        def _(pe):
            pe.sem_inc(gelued, FREE_1)
            pe.sem_inc(mixed, FREE_2)
            with pe.Fori(0, QUADS) as g:
                n0 = g * EXPERTS
                for e in range(EXPERTS + 1):
                    if e < EXPERTS:
                        pe.wait_ge(gelued, n0 + (e + 1))
                        nc.tensor.matmul(bank_1[e % 2][:, :], k.e_w1[:, e, :],
                                         k.ht[:, one(g), :].rearrange("p a c -> p (a c)"),
                                         start=True, stop=True).then_inc(first, 1)
                    if e >= 1:
                        m = e - 1
                        pe.wait_ge(gelued, n0 + (m + 1 + FREE_1))
                        pe.wait_ge(mixed, g * (QUAD * EXPERTS) + QUAD * (m + 1))
                        for j in range(QUAD):
                            to = bank_2[m % 4][:, j * C:(j + 1) * C]
                            nc.tensor.matmul(to, k.ones[0:1, :], k.e_b2[0:1, m * C:(m + 1) * C], start=True, stop=False)
                            mm = nc.tensor.matmul(to, hidden[m % 2][:, j * C:(j + 1) * C], k.e_w2[:, m, :],
                                                  start=False, stop=True)
                        mm.then_inc(second, 1)

        @block.scalar
        def _(act):
            act.sem_inc(second, 2)
            with act.Fori(0, QUADS) as g:
                for e in range(EXPERTS):
                    act.wait_ge(first, g * EXPERTS + (e + 1))
                    act.wait_ge(second, g * EXPERTS + (e + 1))
                    nc.scalar.activation(hidden[e % 2][:, :], bank_1[e % 2][:, :], ACT.Gelu,
                                         bias=k.e_b1[:, e:e + 1]).then_inc(gelued, 1)

        @block.vector
        def _(dve_):
            with dve_.Fori(0, QUADS) as g:
                for e in range(EXPERTS):
                    dve_.wait_ge(second, g * EXPERTS + (e + 3))
                    for j in range(QUAD):
                        t = g * QUAD + j
                        n = e * QUAD + j
                        xt = k.x[:, one(t), :].rearrange("p a c -> p (a c)")
                        if e > 0:
                            dve_.wait_ge(mixed, g * (QUAD * EXPERTS) + (n - 3 + FREE_2))
                        nc.vector.scalar_tensor_tensor(xt, bank_2[e % 4][:, j * C:(j + 1) * C],
                                                       k.combine[:, one(t), e], xt, ALU.mult, ALU.add).then_inc(mixed, 1)


def program(nc, d, out):
    stack = ExitStack()
    with stack:
        k = Core(nc, stack)
        k.t1_dram = nc.dram_tensor("t1_rows", (NODES, WIDE), F32).ap()
        k.e_dram = nc.dram_tensor("e_rows", (NODES, HEADS), F32).ap()
        k.ecol_dram = nc.dram_tensor("e_columns", (2 * HEADS, NODES), F32).ap()
        k.st_dram = nc.dram_tensor("neighbour_sums", (TILES, P, BANK), F32).ap()
        k.y_dram = nc.dram_tensor("y_rows", (NODES, C), F32).ap()
        k.ident = k.sb("ident", [P, P])
        k.not_ident = k.sb("not_ident", [P, P])
        k.ones = k.sb("ones", [P, P])
        k.tiny = k.sb("tiny", [P, 1])
        k.minus_half = k.sb("minus_half", [P, TILES])
        k.mean, k.var, k.rstd = k.sb("mean", [P, TILES]), k.sb("var", [P, TILES]), k.sb("rstd", [P, TILES])
        k.dif, k.sq = k.sb("dif", [P, TILES]), k.sb("sq", [P, TILES])
        k.stats = k.sb("stats", [P, TILES, 6])
        k.stats_s, k.stats_n = k.sem("stats_s"), 0
        k.dcol = k.sb("dcol", [P, TILES])
        k.val = k.sb("val", [P, TILES, SLOTS])
        k.idx = k.sb("idx", [P, TILES, SLOTS], U32)
        k.far = k.sb("far", [P, TILES, SLOTS])
        k.e6 = k.sb("e6", [P, TILES, 2 * HEADS])
        k.tiles_left = k.sb("tiles_left", [1, TILES])
        k.order = k.sb("order", [1, TILES], I32)
        k.count = k.sb("count", [1, 1], I32)
        k.after_flagged = k.sem("after_flagged")
        k.sp_ticks = k.sem("sp_ticks")
        k.gathered = k.sem("gathered")
        with ExitStack() as gnn:
            k.wih_e, k.whh_e = k.sb("wih_e", [P, 3 * C], stack=gnn), k.sb("whh_e", [P, 3 * C], stack=gnn)
            k.wih_n, k.whh_n = k.sb("wih_n", [P, 3 * C], stack=gnn), k.sb("whh_n", [P, 3 * C], stack=gnn)
            k.ww = k.sb("ww", [P, HEADS, 3 * C], stack=gnn)
            k.brow_e = k.sb("brow_e", [2, BANK], stack=gnn)
            k.brow_n = k.sb("brow_n", [2, BANK], stack=gnn)
            prepare(k, d)
            with ExitStack() as gat:
                k.g = k.sb("g", [P, TILES, SLOTS, WIDE], stack=gat)
                extract(k, d)
                dense_logits(k, d)
                attend(k)
            dense_attend(k, d)
            k.x = k.sb("x", [P, TILES, C], stack=gnn)
            gates(k, d)
            k.ffn_wc = k.sb("ffn_wc", [P, C], stack=gnn)
            k.ffn_bias = k.sb("ffn_bias", [1, C], stack=gnn)
            with ExitStack() as ffn:
                k.f0 = k.sb("f0", [P, TILES, C], stack=ffn)
                ffn_weights(k, d)
                feed_forward(k)
            with ExitStack() as gnn2:
                k.z = k.sb("z", [P, TILES, C], stack=gnn2)
                with ExitStack() as nbs:
                    k.y = k.sb("y", [P, TILES, C], stack=nbs)
                    k.yg = k.sb("yg", [P, RING * QUAD, SLOTS, C], stack=nbs)
                    k.poly_w1 = k.sb("poly_w1", [P, KPOLY + C], stack=nbs)
                    k.poly_w2 = k.sb("poly_w2", [P, KPOLY, C], stack=nbs)
                    poly_weights(k, d)
                    poly(k)
                    spread(k)
                    dense_spread(k, d)
                k.router = k.sb("router", [P, EXPERTS], stack=gnn2)
                k.e_w1 = k.sb("e_w1", [P, EXPERTS, C], stack=gnn2)
                k.e_w2 = k.sb("e_w2", [P, EXPERTS, C], stack=gnn2)
                k.e_b1 = k.sb("e_b1", [P, EXPERTS], stack=gnn2)
                k.e_b2 = k.sb("e_b2", [1, EXPERTS * C], stack=gnn2)
                k.expert_no_i = k.sb("expert_no_i", [P, EXPERTS], I32, stack=gnn2)
                k.expert_no = k.sb("expert_no", [P, EXPERTS], stack=gnn2)
                k.combine = k.sb("combine", [P, TILES, EXPERTS], stack=gnn2)
                k.ht = k.sb("ht", [P, QUADS, BANK], stack=gnn2)
                settle(k, d)
                route(k)
                experts(k, out)


def kernel(**inputs):
    import numpy as _np
    import concourse.bacc as _bacc
    from concourse import mybir as _mybir
    from concourse.bass_utils import run_bass_kernel_spmd as _run

    nc = _bacc.Bacc("TRN2", target_bir_lowering=False, num_devices=1)
    arrays = lay_out(inputs)
    d = {}
    for name, a in arrays.items():
        d[name] = nc.dram_tensor(f"in_{name}", a.shape, _mybir.dt.from_np(a.dtype), kind="ExternalInput").ap()
    out = nc.dram_tensor("out_0", (NODES, C), F32, kind="ExternalOutput").ap()
    program(nc, d, out)
    r = _run(nc, [{f"in_{n}": a for n, a in arrays.items()}], core_ids=[0])
    return r.results[0]["out_0"]


def lay_out(inputs):
    import numpy as np

    i = {n: np.asarray(a) for n, a in inputs.items()}
    row = lambda a: a.reshape(1, -1)
    laid = {
        "x": i["x"],
        "adj": i["adj"],
        "gat_wt": i["L0_gnn_gat_W"].transpose(2, 0, 1),
        "gat_at": i["L0_gnn_gat_a"].reshape(HEADS, 2, C).transpose(2, 1, 0).reshape(C, 2 * HEADS),
        "wih_e": i["L0_gnn_edge_Wih"].T,
        "whh_e": i["L0_gnn_edge_Whh"].T,
        "wih_n": i["L0_gnn_node_Wih"].T,
        "whh_n": i["L0_gnn_node_Whh"].T,
        "bih_e": row(i["L0_gnn_edge_bih"]),
        "bhh_e": row(i["L0_gnn_edge_bhh"]),
        "bih_n": row(i["L0_gnn_node_bih"]),
        "bhh_n": row(i["L0_gnn_node_bhh"]),
        "ln_w": i["L0_ffn_ln_w"].reshape(C, 1),
        "ln_b": i["L0_ffn_ln_b"].reshape(C, 1),
        "ffn_wt": i["L0_ffn_W"].T,
        "ffn_b": row(i["L0_ffn_b"]),
        "w1": i["L1_gnn_W1"],
        "w1t": i["L1_gnn_W1"].T,
        "w2": i["L1_gnn_W2"].transpose(1, 0, 2),
        "bk": i["L1_gnn_b"],
        "router_t": i["L1_ffn_router_w"].T,
        "e_w1": i["L1_ffn_w1"].transpose(1, 0, 2),
        "e_b1": i["L1_ffn_b1"].T,
        "e_w2": i["L1_ffn_w2"].transpose(1, 0, 2),
        "e_b2": row(i["L1_ffn_b2"]),
    }
    return {n: np.ascontiguousarray(a) for n, a in laid.items()}
```

```python
from contextlib import ExitStack, contextmanager

import concourse.bass as bass
from concourse import mybir

ALU = mybir.AluOpType
ACT = mybir.ActivationFunctionType
AX_X = mybir.AxisListType.X
F32 = mybir.dt.float32
BF16 = mybir.dt.bfloat16
U32 = mybir.dt.uint32
I32 = mybir.dt.int32
U8 = mybir.dt.uint8

P = 128
NODES = 4096
C = 128
TILES = NODES // P
QUAD = 4
QUADS = TILES // QUAD
BANK = QUAD * C
HEADS = 3
SLOTS = 8
WIDE = C + 2 * HEADS
EPS = 1e-5
ALPHA = 0.2
NEG_INF = -9000000000000000.0
FAR = -1.0e30
KPOLY = 16
EXPERTS = 8
ITERS = 30


class Core:

    def __init__(self, nc, stack):
        self.nc, self.stack = nc, stack

    def sb(self, name, shape, dtype=F32, stack=None):
        return (stack or self.stack).enter_context(self.nc.sbuf_tensor(name, shape, dtype))

    def ps(self, name, shape, stack, dtype=F32):
        return stack.enter_context(self.nc.psum_tensor(name, shape, dtype))

    def sem(self, name):
        return self.stack.enter_context(self.nc.semaphore(name))


class Link:

    def __init__(self, engine, sem, base=0):
        self.engine, self.sem, self.base, self.n = engine, sem, base, 0

    def __call__(self, ins):
        self.n += 1
        ins.then_inc(self.sem, 1)
        self.engine.wait_ge(self.sem, self.base + self.n)


def one(t):
    return bass.ds(t, 1)


def wait_from(eng, sem, value):
    if not isinstance(value, int) or value > 0:
        eng.wait_ge(sem, value)


def by_quads(eng, step):
    step(0, 0)
    step(1, 1)
    with eng.Fori(1, QUADS // 2) as i:
        for b in range(2):
            step(i * 2 + b, b)


def three_parts(k, link, name, source, out, stack):
    nc = k.nc
    rows, n = source.shape[0], source.shape[1]
    hi, mid = (k.sb(f"{name}_{part}", [rows, n], BF16, stack=stack) for part in ("hi", "mid"))
    rest = k.sb(f"{name}_rest", [rows, n], stack=stack)
    of_three = [k.of_three[0:rows, j:j + 1] for j in range(3)]
    link(nc.vector.tensor_copy(hi[:, :], source))
    link(nc.vector.tensor_tensor(rest[:, :], source, hi[:, :], ALU.subtract))
    link(nc.vector.tensor_copy(mid[:, :], rest[:, :]))
    link(nc.vector.tensor_tensor(rest[:, :], rest[:, :], mid[:, :], ALU.subtract))
    link(nc.vector.tensor_scalar(hi[:, :], hi[:, :], of_three[0], None, ALU.mult))
    link(nc.vector.scalar_tensor_tensor(mid[:, :], mid[:, :], of_three[1], hi[:, :], ALU.mult, ALU.add))
    link(nc.vector.scalar_tensor_tensor(out, rest[:, :], of_three[2], mid[:, :], ALU.mult, ALU.add))


def prepare(k, d):
    nc = k.nc
    st = ExitStack()
    with st:
        x = k.sb("x_in", [P, TILES, C], stack=st)
        k.t1 = k.sb("t1", [P, TILES, WIDE], stack=st)
        wih_n = k.sb("wih_n", [P, 3 * C], stack=st)
        tile_no = k.sb("tile_no", [1, TILES], I32, stack=st)
        gat_wt = k.sb("gat_wt", [P, HEADS, C], stack=st)
        gat_at = k.sb("gat_at", [P, 2 * HEADS], stack=st)
        wa = k.sb("wa", [P, 2 * HEADS], stack=st)
        h4 = k.sb("h4", [P, QUAD, C], stack=st)
        h4t = k.sb("h4t", [P, BANK], stack=st)
        bank_w = [k.ps(f"bank_w{i}", [P, 512], st) for i in range(HEADS)]
        bank_a = k.ps("bank_a", [P, 512], st)
        bank_t = k.ps("bank_t", [P, 512], st)
        bank_p = k.ps("bank_p", [P, QUAD, 8], st)

        x_in, w_in = k.sem("x_in_s"), k.sem("w_in")
        pool0, made, rsd = k.sem("p0_pool"), k.sem("consts_made"), k.sem("p0_rstd")
        dve, scaled = k.sem("p0_dve"), k.sem("p0_scaled")
        folded, wa_put, ww_put = k.sem("folded"), k.sem("wa_put"), k.sem("ww_put")
        normed, turned, put_t, put_h, prod, put_p = (
            k.sem("p0_normed"), k.sem("p0_turned"), k.sem("p0_put_t"), k.sem("p0_put_h"),
            k.sem("p0_prod"), k.sem("p0_put_p"))
        table = k.sem("t1_stored")
        stats_in = k.sem("p0_var")

        block = st.enter_context(nc.Block())

        @block.sync
        def _(sp):
            sp.dma_start(x[:, :, :], d["x"].rearrange("(p t) c -> p t c", t=TILES)).then_inc(x_in, 16)
            loads = [
                (gat_wt[:, :, :], d["gat_wt"]), (gat_at[:, :], d["gat_at"]),
                (wih_n[:, :], d["wih_n"]),
            ]
            for to, of in loads:
                sp.dma_start(to, of).then_inc(w_in, 16)
            with nc.allow_non_contiguous_dma("the diagonal"):
                diagonal = bass.AP(d["adj"].tensor, 0, [[TILES * (NODES + 1), P], [NODES + 1, TILES]])
                sp.dma_start(k.dcol[:, :], diagonal).then_inc(w_in, 16)
            sp.wait_ge(put_h, QUADS + 1)
            sp.wait_ge(put_p, QUADS)
            sp.dma_start(k.t1_dram.rearrange("(p t) c -> p t c", t=TILES), k.t1[:, :, :]).then_inc(table, 16)
            sp.wait_ge(w_in, 16 * (len(loads) + 1))
            sp.wait_ge(table, 16)

        @block.gpsimd
        def _(pool):
            nc.gpsimd.memset(k.ident[:, :], 0.0).then_inc(pool0, 1)
            pool.wait_ge(pool0, 1)
            nc.gpsimd.affine_select(out=k.ident[:, :], in_=k.ident[:, :], compare_op=ALU.not_equal, fill=1.0,
                                    base=0, pattern=[[-1, P]], channel_multiplier=1).then_inc(made, 1)
            nc.gpsimd.memset(k.minus_half[:, :], -0.5).then_inc(pool0, 1)
            nc.gpsimd.iota(tile_no[:, :], pattern=[[1, TILES]], base=0, channel_multiplier=0).then_inc(pool0, 1)
            pool.wait_ge(pool0, 3)
            nc.gpsimd.tensor_scalar(k.tiles_left[:, :], tile_no[:, :], -1.0, float(TILES), ALU.mult, ALU.add)
            pool.wait_ge(stats_in, 1)
            nc.gpsimd.tensor_tensor(k.rstd[:, :], k.var[:, :], k.minus_half[:, :], ALU.pow).then_inc(rsd, 1)

        @block.vector
        def _(dve_):
            link = Link(dve_, dve)
            nc.vector.memset(k.ones[:, :], 1.0)
            nc.vector.memset(k.ones_bf[:, :], 1.0)
            nc.vector.memset(k.tiny[:, :], -1e-30)
            dve_.wait_ge(made, 1)
            link(nc.vector.tensor_scalar(k.not_ident[:, :], k.ident[:, :], -1.0, 1.0, ALU.mult, ALU.add))
            nc.vector.tensor_tensor(k.of_three[:, :], k.ident[:, 0:3], k.ident[:, 3:6], ALU.add)
            dve_.wait_ge(x_in, 16)
            layer_stats(k, dve_, link, x, stats_in)
            dve_.wait_ge(rsd, 1)
            dve_.wait_ge(folded, 1)
            nc.vector.tensor_copy(wa[:, :], bank_a[:, 0:2 * HEADS]).then_inc(wa_put, 1)
            dve_.sem_inc(turned, 1)
            dve_.sem_inc(put_h, 1)
            with dve_.Fori(0, QUADS) as g:
                dve_.wait_ge(turned, g + 1)
                dve_.wait_ge(put_h, g + 1)
                for j in range(QUAD):
                    ins = nc.vector.tensor_scalar(h4[:, j, :], x[:, one(g * QUAD + j), :],
                                                  k.mean[:, one(g * QUAD + j)], k.rstd[:, one(g * QUAD + j)],
                                                  ALU.subtract, ALU.mult)
                ins.then_inc(normed, 1)
                dve_.wait_ge(prod, g + 1)
                nc.vector.tensor_copy(k.t1[:, bass.ts(g, QUAD), C:WIDE],
                                      bank_p[:, :, 0:2 * HEADS]).then_inc(put_p, 1)

        @block.tensor
        def _(pe):
            pe.wait_ge(w_in, 16 * 4)
            for half in range(2):
                for h in range(HEADS):
                    c = half * HEADS + h
                    mm = nc.tensor.matmul(bank_a[:, c:c + 1], gat_wt[:, h, :], gat_at[:, c:c + 1],
                                          start=True, stop=True)
            mm.then_inc(folded, 1)
            for h in range(HEADS):
                mm = nc.tensor.matmul(bank_w[h][:, 0:3 * C], gat_wt[:, h, :], wih_n[:, :],
                                      start=True, stop=True)
            mm.then_inc(folded, 1)
            pe.wait_ge(made, 1)
            pe.wait_ge(wa_put, 1)
            with pe.Fori(0, QUADS) as g:
                pe.wait_ge(normed, g + 1)
                for j in range(QUAD):
                    mm = nc.tensor.transpose(bank_t[:, j * C:(j + 1) * C], h4[:, j, :], k.ident[:, :])
                mm.then_inc(turned, 1)
                pe.wait_ge(put_t, g + 1)
                for j in range(QUAD):
                    mm = nc.tensor.matmul(bank_p[:, j, 0:2 * HEADS], h4t[:, j * C:(j + 1) * C], wa[:, :],
                                          start=True, stop=True)
                mm.then_inc(prod, 1)

        @block.scalar
        def _(act):
            act.wait_ge(folded, 2)
            for h in range(HEADS):
                nc.scalar.activation(k.ww[:, h, :], bank_w[h][:, 0:3 * C], ACT.Copy,
                                     scale=1.0 / HEADS).then_inc(ww_put, 1)
            with act.Fori(0, QUADS) as g:
                act.wait_ge(normed, g + 1)
                nc.scalar.activation(k.t1[:, bass.ts(g, QUAD), 0:C], h4[:, :, :], ACT.Copy).then_inc(put_h, 1)
                act.wait_ge(turned, g + 2)
                nc.scalar.activation(h4t[:, :], bank_t[:, :], ACT.Copy).then_inc(put_t, 1)


def layer_stats(k, eng, link, x, ready):
    nc = k.nc
    stats, dif, sq = k.stats, k.dif, k.sq
    with eng.Fori(0, QUADS) as g:
        for j in range(QUAD):
            ins = nc.vector.bn_stats(stats[:, one(g * QUAD + j), :], x[:, one(g * QUAD + j), :])
        ins.then_inc(k.stats_s, 1)
    k.stats_n += QUADS
    eng.wait_ge(k.stats_s, k.stats_n)
    even_m, even_v, odd_m, odd_v = stats[:, :, 1], stats[:, :, 2], stats[:, :, 4], stats[:, :, 5]
    nc.vector.tensor_tensor(dif[:, :], even_m, odd_m, ALU.subtract)
    nc.vector.tensor_tensor(k.mean[:, :], even_m, odd_m, ALU.add)
    link(nc.vector.scalar_tensor_tensor(k.var[:, :], even_v, C * EPS, odd_v, ALU.add, ALU.add))
    nc.vector.tensor_scalar(k.mean[:, :], k.mean[:, :], 0.5, None, ALU.mult)
    link(nc.vector.scalar_tensor_tensor(sq[:, :], dif[:, :], 0.25, dif[:, :], ALU.mult, ALU.mult))
    nc.vector.scalar_tensor_tensor(k.var[:, :], k.var[:, :], 1.0 / C, sq[:, :],
                                   ALU.mult, ALU.add).then_inc(ready, 1)


def extract(k, d):
    nc = k.nc
    st = ExitStack()
    with st:
        a = [k.sb(f"adj_rows{i}", [P, NODES], stack=st) for i in range(2)]
        signs = k.sb("signs", [P, NODES], BF16, stack=st)
        top = [k.sb(f"top{i}", [P, SLOTS], stack=st) for i in range(2)]
        raw = [k.sb(f"raw_index{i}", [P, SLOTS], U32, stack=st) for i in range(2)]
        off = [k.sb(f"off{i}", [P, SLOTS], stack=st) for i in range(2)]
        cnt = k.sb("cnt", [P, 2, TILES], stack=st)
        found = k.sb("found", [P, TILES, SLOTS], stack=st)
        nfound = k.sb("nfound", [P, TILES], stack=st)
        twice = k.sb("twice", [P, TILES], stack=st)
        bad = k.sb("bad", [P, 2, TILES], stack=st)
        sixes = k.sb("sixes", [P, TILES, 2 * HEADS], stack=st)
        good = k.sb("good", [P, TILES], stack=st)
        keys = [k.sb(f"flag_keys{i}", [1, TILES], stack=st) for i in range(2)]
        order = k.sb("flag_order", [1, TILES], stack=st)
        countf = k.sb("flag_count", [1, 1], stack=st)
        bank = k.ps("bank_flags", [P, 512], st)

        loaded = [k.sem(f"adj_loaded{i}") for i in range(2)]
        undiag, maxed, indexed, off_s, idx_ready = (
            k.sem("undiag"), k.sem("maxed"), k.sem("indexed"), k.sem("off_s"), k.sem("idx_ready"))
        counted, zeroed, dve, summed = k.sem("counted"), k.sem("g_zeroed"), k.sem("p1_dve"), k.sem("bad_summed")
        half_counted, bad_made = k.sem("half_counted"), k.sem("bad_made")
        rows = d["adj"].rearrange("(p t) j -> t p j", t=TILES)
        block = st.enter_context(nc.Block())

        @block.sync
        def _(sp):
            for b in range(2):
                sp.dma_start(a[b][:, :], rows[b]).then_inc(loaded[b], 16)
            for t in range(2, TILES):
                sp.wait_ge(indexed, t - 1)
                sp.wait_ge(counted, t)
                sp.dma_start(a[t % 2][:, :], rows[t]).then_inc(loaded[t % 2], 16)

        @block.scalar
        def _(act):
            act.sem_inc(counted, 1)
            with act.Fori(0, TILES // 2) as i:
                for b in range(2):
                    t = i * 2 + b
                    act.wait_ge(undiag, t + 1)
                    act.wait_ge(counted, t + 1)
                    nc.scalar.activation(signs[:, :], a[b][:, :], ACT.Sign,
                                         accum_out=cnt[:, 0, one(t)]).then_inc(half_counted, 1)
                    act.wait_ge(half_counted, t + 1)
                    nc.scalar.activation(signs[:, :], a[b][:, :], ACT.Sign, bias=k.tiny[:, 0:1],
                                         accum_out=cnt[:, 1, one(t)]).then_inc(counted, 1)

        @block.vector
        def _(dve_):
            def zero_diagonal(i, b):
                dve_.wait_ge(loaded[b], i * 16 + 16)
                diag = a[b][:, :].rearrange("p (q t) -> p q t", t=TILES)[:, :, one(i * 2 + b)]
                nc.vector.tensor_tensor(diag, diag, k.not_ident[:, :].rearrange("p (q o) -> p q o", o=1),
                                        ALU.mult).then_inc(undiag, 1)

            def put_index(t, b):
                dve_.wait_ge(indexed, t + 1)
                dve_.wait_ge(off_s, t + 1)
                nc.vector.tensor_tensor(k.idx[:, one(t), :].rearrange("p a s -> p (a s)"), raw[b][:, :],
                                        off[b][:, :], ALU.add).then_inc(idx_ready, 1)

            def search(t, b):
                nc.vector.max(top[b][:, :], a[b][:, :]).then_inc(maxed, 1)
                dve_.wait_ge(maxed, t + 1)
                nc.vector.tensor_copy(k.val[:, one(t), :].rearrange("p a s -> p (a s)"), top[b][:, :])
                nc.vector.max_index(raw[b][:, :], top[b][:, :], a[b][:, :]).then_inc(indexed, 1)
                nc.vector.tensor_scalar(off[b][:, :], top[b][:, :], 0.0, 2.0 * NODES,
                                        ALU.is_le, ALU.mult).then_inc(off_s, 1)

            zero_diagonal(0, 0)
            dve_.wait_ge(undiag, 1)
            search(0, 0)
            zero_diagonal(0, 1)
            dve_.wait_ge(undiag, 2)
            put_index(0, 0)
            search(1, 1)
            with dve_.Fori(1, TILES // 2) as i:
                for b in range(2):
                    zero_diagonal(i, b)
                    dve_.wait_ge(undiag, i * 2 + (b + 1))
                    put_index(i * 2 + (b - 1), 1 - b)
                    search(i * 2 + b, b)
            put_index(TILES - 1, 1)
            link = Link(dve_, dve)
            link(nc.vector.tensor_scalar(found[:, :, :], k.val[:, :, :], 0.0, None, ALU.is_gt))
            link(nc.vector.tensor_reduce(nfound[:, :], found[:, :, :], AX_X, ALU.add))
            link(nc.vector.tensor_scalar(twice[:, :], nfound[:, :], 2.0, -float(NODES), ALU.mult, ALU.add))
            dve_.wait_ge(counted, TILES + 1)
            nc.vector.tensor_tensor(bad[:, 0, :], cnt[:, 0, :], nfound[:, :], ALU.not_equal)
            nc.vector.tensor_tensor(bad[:, 1, :], cnt[:, 1, :], twice[:, :], ALU.not_equal).then_inc(bad_made, 1)
            dve_.wait_ge(summed, 1)
            link(nc.vector.tensor_scalar(good[:, :], bank[:, 0:TILES], 0.5, None, ALU.is_lt))
            nc.vector.tensor_tensor(k.val[:, :, :], k.val[:, :, :],
                                    good[:, :].rearrange("p (t o) -> p t o", o=1).broadcast_to([P, TILES, SLOTS]),
                                    ALU.mult)
            link(nc.vector.tensor_scalar(keys[0][:, :], good[0:1, :], -1.0, 1.0, ALU.mult, ALU.add))
            link(nc.vector.tensor_reduce(countf[:, :], keys[0][:, :], AX_X, ALU.add))
            nc.vector.tensor_copy(k.count[:, :], countf[:, :])
            link(nc.vector.tensor_tensor(keys[0][:, :], keys[0][:, :], k.tiles_left[:, :], ALU.mult))
            for r in range(TILES // 8):
                eight = order[:, 8 * r:8 * r + 8]
                link(nc.vector.max(eight, keys[r % 2][:, :]))
                if r < TILES // 8 - 1:
                    link(nc.vector.match_replace(out=keys[1 - r % 2][:, :], in_to_replace=eight,
                                                 in_values=keys[r % 2][:, :], imm_value=0.0))
            link(nc.vector.tensor_scalar(k.order[:, :], order[:, :], -1.0, float(TILES), ALU.mult, ALU.add))
            dve_.wait_ge(k.gathered, 16 * TILES * SLOTS)
            quarter = TILES // 4
            for q in range(4):
                ts = slice(q * quarter, (q + 1) * quarter)
                link(nc.vector.tensor_reduce(sixes[:, ts, :], k.g[:, ts, :, C:WIDE].rearrange("p t s c -> p t c s"),
                                             AX_X, ALU.add))
            link(nc.vector.scalar_tensor_tensor(k.e6[:, :, :], sixes[:, :, :], ALPHA, sixes[:, :, :],
                                                ALU.mult, ALU.max))

        @block.tensor
        def _(pe):
            pe.wait_ge(bad_made, 1)
            for i in range(2):
                mm = nc.tensor.matmul(bank[:, 0:TILES], k.ones[:, :], bad[:, i, :], start=(i == 0), stop=(i == 1))
            mm.then_inc(summed, 1)

        @block.gpsimd
        def _(pool):
            nc.gpsimd.memset(k.g[:, :, :, :], 0.0).then_inc(zeroed, 1)
            pool.wait_ge(zeroed, 1)
            for t in range(TILES):
                pool.wait_ge(idx_ready, t + 1)
                for s in range(SLOTS):
                    gather(nc, k.g[:, t, s, :], k.t1_dram, k.idx[:, t, s:s + 1]).then_inc(k.gathered, 16)


def gather(nc, to, table, index):
    return nc.gpsimd.indirect_dma_start(
        out=to, out_offset=None, in_=table, in_offset=bass.IndirectOffsetOnAxis(ap=index, axis=0),
        bounds_check=NODES - 1, oob_is_err=False)


class Turning:

    GROUPS = TILES // 4
    CREDIT = 2

    def __init__(self, k, stack, name, calls, banks=None):
        self.k, self.calls = k, calls
        self.banks = banks or [k.ps(f"{name}_turn{i}", [P, BANK], stack) for i in range(2)]
        self.turned_sb = [k.sb(f"{name}_turned{i}", [P, BANK], stack=stack) for i in range(2)]
        self.turned, self.copied, self.used = (
            k.sem(f"{name}_turned_s"), k.sem(f"{name}_copied_s"), k.sem(f"{name}_used_s"))

    def start(self, act):
        act.sem_inc(self.copied, self.CREDIT)
        act.sem_inc(self.used, self.CREDIT)

    def base(self, rank, call):
        return rank * (self.calls * self.GROUPS) + call * self.GROUPS

    def done(self, rank, call):
        return rank * (self.calls * self.GROUPS) + ((call + 1) * self.GROUPS + self.CREDIT)

    def multiply(self, pe, rank, call, rows, table, out):
        nc = self.k.nc
        r = rank * (self.calls * self.GROUPS)
        blocks = rows.rearrange("p (q t) -> p q t", t=TILES)
        for g in range(self.GROUPS + 1):
            n = call * self.GROUPS + g
            if g < self.GROUPS:
                pe.wait_ge(self.copied, r + (n + 1))
                for j in range(4):
                    mm = nc.tensor.transpose(self.banks[g % 2][:, j * P:(j + 1) * P], blocks[:, :, 4 * g + j],
                                             self.k.ident[:, :])
                mm.then_inc(self.turned, 1)
            if g >= 1:
                pe.wait_ge(self.copied, r + (n - 1 + 1 + self.CREDIT))
                for j in range(4):
                    b = 4 * (g - 1) + j
                    mm = nc.tensor.matmul(out, self.turned_sb[(g - 1) % 2][:, j * P:(j + 1) * P], table(b),
                                          start=(b == 0), stop=(b == TILES - 1))
                mm.then_inc(self.used, 1)

    def copy(self, act, rank, call):
        nc = self.k.nc
        r = rank * (self.calls * self.GROUPS)
        for g in range(self.GROUPS):
            n = call * self.GROUPS + g
            act.wait_ge(self.turned, r + (n + 1))
            act.wait_ge(self.used, r + (n + 1))
            nc.scalar.activation(self.turned_sb[g % 2][:, :], self.banks[g % 2][:, :], ACT.Copy).then_inc(self.copied, 1)


@contextmanager
def flagged(k, eng):
    count = eng.value_load(k.count[0:1, 0:1], min_val=0, max_val=TILES)
    with eng.If(count > 0):
        with eng.Fori(0, count) as rank:
            yield eng.value_load(k.order[0:1, one(rank)], min_val=0, max_val=TILES - 1), rank
        eng.sem_inc(k.after_flagged, 1)


def plain_sums(k, eng, first, last):
    steps = QUAD * SLOTS
    with eng.Fori(first, last) as g:
        for s in range(SLOTS):
            for j in range(QUAD):
                to = k.x[:, one(g * QUAD + j), :].rearrange("p a c -> p (a c)")
                row = k.g[:, one(g * QUAD + j), s, 0:C].rearrange("p a c -> p (a c)")
                w = k.val[:, one(g * QUAD + j), s]
                if s == 0:
                    ins = k.nc.vector.tensor_scalar(to, row, w, None, ALU.mult)
                else:
                    eng.wait_ge(k.plain, g * steps + (s * QUAD + j - 3))
                    ins = k.nc.vector.scalar_tensor_tensor(to, row, w, to, ALU.mult, ALU.add)
                ins.then_inc(k.plain, 1)


def dense_logits(k, d):
    nc = k.nc
    st = ExitStack()
    with st:
        rows_sb = k.sb("d1_rows", [P, NODES], stack=st)
        mask = k.sb("d1_mask", [P, NODES], stack=st)
        hwa = k.sb("d1_hwa", [P, TILES, 2 * HEADS], stack=st)
        pos = k.sb("d1_pos", [P, 2 * HEADS], stack=st)
        six = k.sb("d1_six", [P, 2 * HEADS], stack=st)
        acc = [k.ps(f"d1_acc{i}", [P, 512], st) for i in range(2)]
        turning = Turning(k, st, "d1", calls=2)
        brow = [k.sb(f"gru_bias_rows{i}", [6, BANK], stack=st) for i in range(2)]
        zeroed, rows_in, split = k.sem("gru_bias_zeroed"), k.sem("gru_bias_in"), k.sem("gru_bias_split")
        table_in, loaded, free = k.sem("d1_table_in"), k.sem("d1_loaded"), k.sem("d1_free")
        undiag, masked, dve = k.sem("d1_undiag"), k.sem("d1_masked"), k.sem("d1_dve")
        rows = d["adj"].rearrange("(p t) j -> t p j", t=TILES)
        block = st.enter_context(nc.Block())

        @block.sync
        def _(sp):
            with flagged(k, sp) as (t, rank):
                sp.wait_ge(free, rank + 1)
                sp.sem_inc(k.sp_ticks, 1)
                sp.dma_start(rows_sb[:, :], rows[one(t)].rearrange("a p j -> p (a j)")).then_inc(loaded, 16)

        @block.vector
        def _(dve_):
            for cell in range(2):
                nc.vector.memset(brow[cell][:, :], 0.0).then_inc(zeroed, 1)
            dve_.sem_inc(free, 1)
            plain_sums(k, dve_, 0, QUADS // 2)
            dve_.wait_ge(rows_in, 16 * 6)
            link = Link(dve_, split)
            for cell in range(2):
                with ExitStack() as parts:
                    three_parts(k, link, f"gru_bias{cell}", brow[cell][:, :], k.gru_bias[cell][:, :], parts)
            with flagged(k, dve_) as (t, rank):
                dve_.wait_ge(loaded, rank * 16 + 16)
                diag = rows_sb[:, :].rearrange("p (q t) -> p q t", t=TILES)[:, :, one(t)]
                nc.vector.tensor_tensor(diag, diag, k.not_ident[:, :].rearrange("p (q o) -> p q o", o=1),
                                        ALU.mult).then_inc(undiag, 1)
                dve_.wait_ge(undiag, rank + 1)
                nc.vector.tensor_scalar(mask[:, :], rows_sb[:, :], 0.0, None, ALU.is_gt).then_inc(masked, 1)
                dve_.wait_ge(turning.used, turning.done(rank, 0))
                nc.vector.tensor_scalar(mask[:, :], rows_sb[:, :], 0.0, None, ALU.is_lt).then_inc(masked, 1)
                link = Link(dve_, dve, rank * 4)
                link(nc.vector.tensor_copy(pos[:, :], acc[0][:, 0:2 * HEADS]))
                dve_.wait_ge(turning.used, turning.done(rank, 1))
                nc.vector.tensor_tensor(six[:, 0:HEADS], pos[:, 0:HEADS], acc[1][:, HEADS:2 * HEADS], ALU.add)
                link(nc.vector.tensor_tensor(six[:, HEADS:], pos[:, HEADS:], acc[1][:, 0:HEADS], ALU.add))
                link(nc.vector.scalar_tensor_tensor(k.e6[:, one(t), :].rearrange("p a c -> p (a c)"), six[:, :],
                                                    ALPHA, six[:, :], ALU.mult, ALU.max))
                link(nc.vector.memset(mask[:, 0:1], 0.0))
                nc.vector.memset(mask[:, 1:2], 0.0).then_inc(free, 1)

        @block.tensor
        def _(pe):
            pe.wait_ge(table_in, 16)
            with flagged(k, pe) as (t, rank):
                for call in range(2):
                    pe.wait_ge(masked, rank * 2 + (call + 1))
                    turning.multiply(pe, rank, call, mask[:, :], lambda b: hwa[:, b, :], acc[call][:, 0:2 * HEADS])

        @block.scalar
        def _(act):
            t1 = k.t1_dram.rearrange("(p t) c -> p t c", t=TILES)
            act.dma_start(hwa[:, :, :], t1[:, :, C:WIDE]).then_inc(table_in, 16)
            act.wait_ge(zeroed, 2)
            for row, bih, bhh in ((brow[0], "bih_e", "bhh_e"), (brow[1], "bih_n", "bhh_n")):
                r_z, new = d[bhh][:, 0:2 * C], d[bhh][:, 2 * C:3 * C]
                act.dma_start(row[0:3, 0:3 * C], d[bih].broadcast_to([3, 3 * C])).then_inc(rows_in, 16)
                act.dma_start(row[3:6, 0:2 * C], r_z.broadcast_to([3, 2 * C])).then_inc(rows_in, 16)
                act.dma_start(row[3:6, 3 * C:4 * C], new.broadcast_to([3, C])).then_inc(rows_in, 16)
            turning.start(act)
            with flagged(k, act) as (t, rank):
                for call in range(2):
                    turning.copy(act, rank, call)


QUAD_GATHERS = 16 * QUAD * SLOTS


def gather_all(k, pool, to, table, gathered, freed=None):
    for g in range(QUADS):
        if freed is not None:
            freed(g)
        if g >= 2:
            pool.wait_ge(gathered[g % 2], QUAD_GATHERS * (g // 2))
        for t in range(g * QUAD, (g + 1) * QUAD):
            for s in range(SLOTS):
                gather(k.nc, to(t, s), table, k.idx[:, t, s:s + 1]).then_inc(gathered[g % 2], 16)


class Cells:

    LINKS = 4

    def __init__(self, k, stack, name, buffers, bank_s, bank_h, bank_g):
        self.k, self.buffers, self.bank_s, self.bank_h, self.bank_g = k, buffers, bank_s, bank_h, bank_g

        def sb(what, shape):
            return [k.sb(f"{name}_{what}{i}", shape, stack=stack) for i in range(buffers)]

        self.sums_t, self.h_t, self.rz = sb("sums_t", [P, BANK]), sb("h_t", [P, C]), sb("rz", [P, 2, 2 * C])
        self.n_in, self.new = sb("n_in", [P, 2, C]), sb("new", [P, 2, C])
        self.dif, self.both = k.sb(f"{name}_dif", [P, 2, C], stack=stack), k.sb(f"{name}_both", [P, C], stack=stack)
        self.wih_e, self.whh_e, self.whh_n = (
            k.sb(f"{name}_{what}", [P, 3 * C], stack=stack) for what in ("wih_e", "whh_e", "whh_n"))
        self.loaded = k.sem(f"{name}_loaded")
        self.turned, self.copied, self.gated, self.squashed, self.inner_made, self.newed, self.done = (
            k.sem(f"{name}_{what}") for what in ("turned", "copied", "gated", "squashed", "inner_made", "newed", "done"))
        self.inner_link, self.blend_link = k.sem(f"{name}_inner_link"), k.sem(f"{name}_blend_link")

    def load(self, sp, d):
        sp.dma_start(self.wih_e[:, :], d["wih_e"]).then_inc(self.loaded, 16)
        sp.dma_start(self.whh_e[:, :], d["whh_e"]).then_inc(self.loaded, 16)
        sp.dma_start(self.whh_n[:, :], d["whh_n"]).then_inc(self.loaded, 16)

    def turn(self, b, sums, h1):
        nc = self.k.nc
        for j in range(4):
            nc.tensor.transpose(self.bank_s[b][:, j * C:(j + 1) * C], sums[:, j * C:(j + 1) * C], self.k.ident[:, :])
        nc.tensor.transpose(self.bank_h[b][:, 0:C], h1, self.k.ident[:, :]).then_inc(self.turned, 1)

    def copy(self, act, b, t):
        nc = self.k.nc
        act.wait_ge(self.turned, t + 1)
        nc.scalar.activation(self.sums_t[b][:, :], self.bank_s[b][:, :], ACT.Copy)
        nc.scalar.activation(self.h_t[b][:, :], self.bank_h[b][:, 0:C], ACT.Copy).then_inc(self.copied, 1)

    def product(self, pe, b, t):
        k, nc = self.k, self.k.nc
        pe.wait_ge(self.copied, t + 1)
        wait_from(pe, self.inner_made, t - (self.buffers - 1))
        for cell, whh in enumerate((self.whh_e, self.whh_n)):
            out = self.bank_g[b][:, cell, :]
            nc.tensor.matmul(out[:, 0:BANK], k.ones_bf[0:6, :], k.gru_bias[cell][:, :], start=True, stop=False)
            if cell == 0:
                nc.tensor.matmul(out[:, 0:3 * C], self.sums_t[b][:, 0:C], self.wih_e[:, :], start=False, stop=False)
            else:
                for h in range(HEADS):
                    nc.tensor.matmul(out[:, 0:3 * C], self.sums_t[b][:, (1 + h) * C:(2 + h) * C], k.ww[:, h, :],
                                     start=False, stop=False)
            nc.tensor.matmul(out[:, 0:2 * C], self.h_t[b][:, :], whh[:, 0:2 * C], start=False, stop=False)
            mm = nc.tensor.matmul(out[:, 3 * C:4 * C], self.h_t[b][:, :], whh[:, 2 * C:3 * C], start=False, stop=True)
        mm.then_inc(self.gated, 1)

    def squash(self, act, b, t):
        act.wait_ge(self.gated, t + 1)
        wait_from(act, self.done, t - (self.buffers - 1))
        self.k.nc.scalar.activation(self.rz[b][:, :, :], self.bank_g[b][:, :, 0:2 * C],
                                    ACT.Sigmoid).then_inc(self.squashed, 1)

    def inner(self, dve_, b, t):
        nc = self.k.nc
        dve_.wait_ge(self.squashed, t + 1)
        n_in = self.n_in[b][:, :, :]
        Link(dve_, self.inner_link, t)(nc.vector.tensor_tensor(
            n_in, self.rz[b][:, :, 0:C], self.bank_g[b][:, :, 3 * C:4 * C], ALU.mult))
        nc.vector.tensor_tensor(n_in, n_in, self.bank_g[b][:, :, 2 * C:3 * C], ALU.add).then_inc(self.inner_made, 1)

    def tanh(self, act, b, t):
        act.wait_ge(self.inner_made, t + 1)
        self.k.nc.scalar.activation(self.new[b][:, :, :], self.n_in[b][:, :, :], ACT.Tanh).then_inc(self.newed, 1)

    def blend(self, dve_, b, t, h1, x, to, diagonal):
        nc, new, dif = self.k.nc, self.new[b][:, :, :], self.dif[:, :, :]
        link = Link(dve_, self.blend_link, t * self.LINKS)
        dve_.wait_ge(self.newed, t + 1)
        link(nc.vector.tensor_tensor(dif, h1.rearrange("p (o c) -> p o c", o=1).broadcast_to([P, 2, C]), new,
                                     ALU.subtract))
        link(nc.vector.tensor_tensor(dif, dif, self.rz[b][:, :, C:2 * C], ALU.mult))
        link(nc.vector.tensor_tensor(dif, dif, new, ALU.add))
        link(nc.vector.tensor_tensor(self.both[:, :], self.dif[:, 0, :], self.dif[:, 1, :], ALU.add))
        nc.vector.scalar_tensor_tensor(to, self.both[:, :], diagonal, x, ALU.mult, ALU.add).then_inc(self.done, 1)


def attend(k, d):
    nc = k.nc
    st = ExitStack()
    with st:
        e_pack = k.sb("e_pack", [P, TILES, HEADS], stack=st)
        far = k.sb("far", [P, TILES, SLOTS], stack=st)
        e_col = k.sb("e_col", [P, 2 * HEADS, TILES], stack=st)
        eg = k.sb("eg", [P, TILES, SLOTS, HEADS], stack=st)
        logit = [k.sb(f"logit{i}", [P, QUAD, HEADS, SLOTS], stack=st) for i in range(2)]
        prob = [k.sb(f"prob{i}", [P, QUAD, HEADS, SLOTS], stack=st) for i in range(2)]
        top = k.sb("row_max", [P, QUAD, HEADS], stack=st)
        den = k.sb("row_sum", [P, QUAD, HEADS], stack=st)
        rden = k.sb("row_rsum", [P, QUAD, HEADS], stack=st)
        weight = k.sb("weight", [P, QUAD, HEADS, SLOTS], stack=st)
        acc = [k.sb(f"sums{i}", [P, BANK], stack=st) for i in range(QUAD)]
        own = [k.sb(f"own_h{i}", [P, 2, C], stack=st) for i in range(2)]
        own_x = [k.sb(f"own_x{i}", [P, 2, C], stack=st) for i in range(2)]
        cells = Cells(k, st, "gru", 2, [k.ps(f"gru_bank_s{i}", [P, BANK], st) for i in range(2)],
                      [k.ps(f"gru_bank_h{i}", [P, 512], st) for i in range(2)],
                      [k.ps(f"gru_bank_g{i}", [P, 2, BANK], st) for i in range(2)])
        packed, stored, eg0, picked = k.sem("e_packed"), k.sem("e_stored"), k.sem("eg_zeroed"), k.sem("plain_picked")
        dve, shifted, exped, rounds = k.sem("p2_dve"), k.sem("p2_shifted"), k.sem("p2_exped"), k.sem("p2_rounds")
        own_in = [k.sem(f"own_h_in{i}") for i in range(2)]
        gathered = [k.sem(f"e_gathered{i}") for i in range(2)]
        PAIRS = TILES // 2
        ROUNDS = 2 * SLOTS
        OWN = PAIRS // 2
        block = st.enter_context(nc.Block())

        @block.sync
        def _(sp):
            sp.wait_ge(packed, 2)
            sp.dma_start(k.e_dram.rearrange("(p t) c -> p t c", t=TILES), e_pack[:, :, :]).then_inc(stored, 16)
            sp.dma_start(k.ecol_dram.rearrange("c (p t) -> p c t", t=TILES), e_col[:, :, :]).then_inc(stored, 16)
            cells.load(sp, d)
            t1 = k.t1_dram.rearrange("(p t) c -> p t c", t=TILES)
            x_rows = d["x"].rearrange("(p t) c -> p t c", t=TILES)
            for m in range(PAIRS):
                wait_from(sp, cells.done, 2 * (m - 1))
                sp.dma_start(own[m % 2][:, :, :], t1[:, 2 * m:2 * m + 2, 0:C]).then_inc(own_in[m % 2], 16)
                sp.dma_start(own_x[m % 2][:, :, :], x_rows[:, 2 * m:2 * m + 2, :]).then_inc(own_in[m % 2], 16)
            sp.wait_ge(stored, 32)

        @block.gpsimd
        def _(pool):
            nc.gpsimd.memset(eg[:, :, :, :], 0.0).then_inc(eg0, 1)
            pool.wait_ge(eg0, 1)
            pool.wait_ge(stored, 32)
            gather_all(k, pool, lambda t, s: eg[:, t, s, :], k.e_dram, gathered)

        @block.scalar
        def _(act):
            def pick(m, parity):
                wait_from(act, cells.turned, m * 2 - 2)
                for jj in range(2):
                    nc.scalar.activation(acc[2 * parity + jj][:, 0:C],
                                         k.x[:, one(m * 2 + jj), :].rearrange("p a c -> p (a c)"),
                                         ACT.Copy).then_inc(picked, 1)

            def copies(m):
                for jj in range(2):
                    cells.copy(act, jj, m * 2 + jj)

            def gates(m):
                for jj in range(2):
                    cells.squash(act, jj, m * 2 + jj)
                for jj in range(2):
                    cells.tanh(act, jj, m * 2 + jj)

            def step(g, b):
                m = g * 2
                if not isinstance(g, int) or g > 0:
                    copies(m - 1)
                act.wait_ge(shifted, g + 1)
                nc.scalar.activation(prob[b][:, :, :, :], logit[b][:, :, :, :], ACT.Exp).then_inc(exped, 1)
                pick(m, 0)
                if not isinstance(g, int) or g > 0:
                    gates(m - 1)
                pick(m + 1, 1)
                copies(m)
                gates(m)

            act.wait_ge(k.plain, QUAD * SLOTS * QUADS)
            by_quads(act, step)
            copies(PAIRS - 1)
            gates(PAIRS - 1)

        @block.vector
        def _(dve_):
            nc.vector.tensor_copy(e_pack[:, :, :], k.e6[:, :, 0:HEADS]).then_inc(packed, 1)
            nc.vector.tensor_copy(e_col[:, :, :], k.e6[:, :, :].rearrange("p t c -> p c t")).then_inc(packed, 1)
            nc.vector.tensor_scalar(far[:, :, :], k.val[:, :, :], 0.0, FAR, ALU.is_le, ALU.mult).then_inc(packed, 1)
            plain_sums(k, dve_, QUADS // 2, QUADS)
            dve_.wait_ge(packed, 3)
            dve_.wait_ge(k.plain, QUAD * SLOTS * QUADS)

            def wide(x):
                return x.rearrange("p t (c o) -> p t c o", o=1).broadcast_to([P, QUAD, HEADS, SLOTS])

            def over_heads(x, g):
                return x[:, bass.ts(g, QUAD), :].rearrange("p t (o s) -> p t o s", o=1).broadcast_to(
                    [P, QUAD, HEADS, SLOTS])

            def softmax(g, b):
                link = Link(dve_, dve, g * 6)
                dve_.wait_ge(gathered[b], (g - b) * (QUAD_GATHERS // 2) + QUAD_GATHERS)
                lg, pr = logit[b][:, :, :, :], prob[b][:, :, :, :]
                link(nc.vector.tensor_tensor(lg, eg[:, bass.ts(g, QUAD), :, :].rearrange("p t s c -> p t c s"),
                                             over_heads(far, g), ALU.add))
                link(nc.vector.tensor_reduce(top[:, :, :], lg, AX_X, ALU.max))
                nc.vector.tensor_tensor(lg, lg, wide(top[:, :, :]), ALU.subtract).then_inc(shifted, 1)
                dve_.wait_ge(exped, g + 1)
                link(nc.vector.tensor_reduce(den[:, :, :], pr, AX_X, ALU.add))
                link(nc.vector.reciprocal(rden[:, :, :], den[:, :, :]))
                link(nc.vector.tensor_tensor(weight[:, :, :, :], pr, wide(rden[:, :, :]), ALU.mult))
                link(nc.vector.tensor_tensor(weight[:, :, :, :], weight[:, :, :, :], over_heads(k.val, g), ALU.mult))

            def sums(g, pair):
                m = g * 2 + pair
                wait_from(dve_, cells.turned, m * 2 - 2)
                for s in range(SLOTS):
                    for jj in range(2):
                        j = 2 * pair + jj
                        t = g * QUAD + j
                        if s > 0:
                            dve_.wait_ge(rounds, m * ROUNDS + (2 * s + jj - 1))
                        row = k.g[:, one(t), s, 0:C].rearrange("p a c -> p (a c)")
                        for h in range(1, 1 + HEADS):
                            w = weight[:, j, h - 1, s:s + 1]
                            to = acc[j][:, h * C:(h + 1) * C]
                            if s == 0:
                                ins = nc.vector.tensor_scalar(to, row, w, None, ALU.mult)
                            else:
                                ins = nc.vector.scalar_tensor_tensor(to, row, w, to, ALU.mult, ALU.add)
                        ins.then_inc(rounds, 1)

            def gates(m, parity):
                for jj in range(2):
                    cells.inner(dve_, jj, m * 2 + jj)
                for jj in range(2):
                    t = m * 2 + jj
                    xt = k.x[:, one(t), :].rearrange("p a c -> p (a c)")
                    cells.blend(dve_, jj, t, own[parity][:, jj, :], own_x[parity][:, jj, :], xt, k.dcol[:, one(t)])

            def step(g, b):
                softmax(g, b)
                sums(g, 0)
                if not isinstance(g, int) or g > 0:
                    gates(g * 2 - 1, 1)
                sums(g, 1)
                gates(g * 2, 0)

            by_quads(dve_, step)
            gates(PAIRS - 1, 1)

        @block.tensor
        def _(pe):
            pe.wait_ge(cells.loaded, 16 * 3)

            def pair_step(m, parity):
                pe.wait_ge(rounds, m * ROUNDS + ROUNDS)
                pe.wait_ge(own_in[parity], (m - parity) * 16 + 32)
                pe.wait_ge(picked, m * 2 + 2)
                for jj in range(2):
                    cells.turn(jj, acc[2 * parity + jj], own[parity][:, jj, :])
                for jj in range(2):
                    cells.product(pe, jj, m * 2 + jj)

            def step(g, b):
                for pair in range(2):
                    pair_step(g * 2 + pair, pair)

            by_quads(pe, step)


def dense_attend(k, d):
    nc = k.nc
    st = ExitStack()
    with st:
        rows_sb = k.sb("d2_rows", [P, NODES], stack=st)
        e_wide = [[k.sb(f"d2_e{n}_{half}", [P, NODES], stack=st) for half in range(2)] for n in range(2)]
        att = [k.sb(f"d2_att{i}", [P, NODES], stack=st) for i in range(2)]
        positive = k.sb("d2_pos", [P, NODES], U8, stack=st)
        negative = k.sb("d2_neg", [P, NODES], U8, stack=st)
        h = k.sb("d2_h", [P, TILES, C], stack=st)
        top = k.sb("d2_top", [P, HEADS], stack=st)
        minus_top = k.sb("d2_minus_top", [P, HEADS], stack=st)
        carrier = k.sb("d2_carrier", [P, 2], stack=st)
        den = k.sb("d2_den", [P, HEADS], stack=st)
        rden = k.sb("d2_rden", [P, HEADS], stack=st)
        sums = k.sb("d2_sums", [P, BANK], stack=st)
        acc = k.ps("d2_acc", [P, BANK], st)
        own, x1 = k.sb("d2_own_h", [P, C], stack=st), k.sb("d2_x", [P, C], stack=st)
        turning = Turning(k, st, "d2", calls=1 + HEADS)
        cells = Cells(k, st, "d2_gru", 1, [k.ps("d2_bank_s", [P, BANK], st)], [k.ps("d2_bank_h", [P, 512], st)],
                      [k.ps("d2_bank_g", [P, 2, BANK], st)])
        x_in = k.sem("d2_x_in")
        table_in, loaded, finished = k.sem("d2_table_in"), k.sem("d2_loaded"), k.sem("d2_finished")
        e_in = [k.sem(f"d2_e_in{n}") for n in range(2)]
        e_used = k.sem("d2_e_used")
        undiag, ready, dve = k.sem("d2_undiag"), k.sem("d2_ready"), k.sem("d2_dve")
        topped, exped, summed = k.sem("d2_topped"), k.sem("d2_exped"), k.sem("d2_summed")
        rows = d["adj"].rearrange("(p t) j -> t p j", t=TILES)
        block = st.enter_context(nc.Block())

        @block.sync
        def _(sp):
            x_rows = d["x"].rearrange("(p t) c -> p t c", t=TILES)
            with flagged(k, sp) as (t, rank):
                sp.wait_ge(finished, rank + 1)
                sp.sem_inc(k.sp_ticks, 1)
                for n in range(HEADS):
                    if n == 1:
                        sp.dma_start(rows_sb[:, :], rows[one(t)].rearrange("a p j -> p (a j)")).then_inc(loaded, 16)
                    if n == 2:
                        sp.wait_ge(e_used, rank * HEADS + 1)
                        sp.sem_inc(k.sp_ticks, 1)
                    for half in range(2):
                        c = n + HEADS * half
                        sp.dma_start(e_wide[n % 2][half][:, :],
                                     k.ecol_dram[c:c + 1, :].broadcast_to([P, NODES])).then_inc(e_in[n % 2], 16)
                sp.dma_start(x1[:, :], x_rows[:, one(t), :].rearrange("p a c -> p (a c)")).then_inc(x_in, 16)

        @block.vector
        def _(dve_):
            dve_.sem_inc(finished, 1)
            dve_.wait_ge(table_in, 16)
            with flagged(k, dve_) as (t, rank):
                dve_.wait_ge(loaded, rank * 16 + 16)
                diag = rows_sb[:, :].rearrange("p (q t) -> p q t", t=TILES)[:, :, one(t)]
                nc.vector.tensor_tensor(diag, diag, k.not_ident[:, :].rearrange("p (q o) -> p q o", o=1),
                                        ALU.mult).then_inc(undiag, 1)
                dve_.wait_ge(undiag, rank + 1)
                link = Link(dve_, dve, rank * (2 + 5 * HEADS))
                link(nc.vector.tensor_scalar(positive[:, :], rows_sb[:, :], 0.0, None, ALU.is_gt))
                link(nc.vector.tensor_scalar(negative[:, :], rows_sb[:, :], 0.0, None, ALU.is_lt))
                for n in range(HEADS):
                    a = att[n % 2][:, :]
                    if n >= 2:
                        dve_.wait_ge(turning.used, turning.done(rank, n - 1))
                    link(nc.vector.memset(a, NEG_INF))
                    dve_.wait_ge(e_in[n % 2], rank * (64 if n != 1 else 32) + (32 if n < 2 else 64))
                    for half, mask in enumerate((positive, negative)):
                        nc.vector.memset(carrier[:, half:half + 1], 0.0)
                        link(nc.vector.copy_predicated(a, mask[:, :], e_wide[n % 2][half][:, :]))
                    dve_.sem_inc(e_used, 1)
                    link(nc.vector.tensor_reduce(top[:, n:n + 1], a, AX_X, ALU.max))
                    nc.vector.tensor_scalar(minus_top[:, n:n + 1], top[:, n:n + 1], -1.0, None,
                                            ALU.mult).then_inc(topped, 1)
                    dve_.wait_ge(exped, rank * HEADS + (n + 1))
                    nc.vector.tensor_tensor(a, a, rows_sb[:, :], ALU.mult).then_inc(ready, 1)
                    link(nc.vector.reciprocal(rden[:, n:n + 1], den[:, n:n + 1]))
                dve_.wait_ge(turning.used, turning.done(rank, HEADS))
                nc.vector.tensor_copy(sums[:, 0:C], acc[:, 0:C])
                for n in range(HEADS):
                    nc.vector.tensor_scalar(sums[:, (n + 1) * C:(n + 2) * C], acc[:, (n + 1) * C:(n + 2) * C],
                                            rden[:, n:n + 1], None, ALU.mult)
                nc.vector.tensor_copy(own[:, :], h[:, one(t), :].rearrange("p a c -> p (a c)")).then_inc(summed, 1)
                cells.inner(dve_, 0, rank)
                dve_.wait_ge(x_in, rank * 16 + 16)
                cells.blend(dve_, 0, rank, own[:, :], x1[:, :], k.x[:, one(t), :].rearrange("p a c -> p (a c)"),
                            k.dcol[:, one(t)])
                dve_.wait_ge(cells.done, rank + 1)
                dve_.sem_inc(finished, 1)

        @block.scalar
        def _(act):
            t1 = k.t1_dram.rearrange("(p t) c -> p t c", t=TILES)
            act.dma_start(h[:, :, :], t1[:, :, 0:C]).then_inc(table_in, 16)
            cells.load(act, d)
            turning.start(act)
            with flagged(k, act) as (t, rank):
                turning.copy(act, rank, 0)
                for n in range(HEADS):
                    act.wait_ge(topped, rank * HEADS + (n + 1))
                    nc.scalar.activation(att[n % 2][:, :], att[n % 2][:, :], ACT.Exp, bias=minus_top[:, n:n + 1],
                                         accum_out=den[:, n:n + 1]).then_inc(exped, 1)
                    turning.copy(act, rank, n + 1)
                cells.copy(act, 0, rank)
                cells.squash(act, 0, rank)
                cells.tanh(act, 0, rank)

        @block.tensor
        def _(pe):
            pe.wait_ge(table_in, 16)
            pe.wait_ge(cells.loaded, 16 * 3)
            with flagged(k, pe) as (t, rank):
                pe.wait_ge(undiag, rank + 1)
                turning.multiply(pe, rank, 0, rows_sb[:, :], lambda b: h[:, b, :], acc[:, 0:C])
                for n in range(HEADS):
                    pe.wait_ge(ready, rank * HEADS + (n + 1))
                    turning.multiply(pe, rank, n + 1, att[n % 2][:, :], lambda b: h[:, b, :],
                                     acc[:, (n + 1) * C:(n + 2) * C])
                pe.wait_ge(summed, rank + 1)
                cells.turn(0, sums, own[:, :])
                cells.product(pe, 0, rank)


def ffn_weights(k, d):
    nc = k.nc
    st = ExitStack()
    with st:
        wt = k.sb("ffn_wt_in", [P, C], stack=st)
        w_scaled = k.sb("ffn_w_scaled", [P, C], stack=st)
        ln_w, ln_b = k.sb("ffn_ln_w", [P, 1], stack=st), k.sb("ffn_ln_b", [P, 1], stack=st)
        b_row = k.sb("ffn_b_in", [1, C], stack=st)
        ln_b3 = k.sb("ffn_ln_b3", [P, 3], stack=st)
        bias3 = k.sb("ffn_bias3", [3, C], stack=st)
        mean_row = k.sb("ffn_ones_mean", [P, P], stack=st)
        bank = k.ps("ffn_w_bank", [P, 512], st)
        bank_b = k.ps("ffn_b_bank", [3, 512], st)
        w_in, scaled, averaged, put = k.sem("ffn_w_in"), k.sem("ffn_w_scaled_s"), k.sem("ffn_averaged"), k.sem("ffn_put")
        rsd, ready, dve = k.sem("ln1_rstd"), k.sem("ln1_var"), k.sem("ln1_dve")
        block = st.enter_context(nc.Block())

        @block.sync
        def _(sp):
            for to, of in ((wt, "ffn_wt"), (ln_w, "ln_w"), (ln_b, "ln_b"), (b_row, "ffn_b")):
                sp.dma_start(to[:, :], d[of]).then_inc(w_in, 16)

        @block.tensor
        def _(pe):
            pe.wait_ge(w_in, 64)
            pe.wait_ge(scaled, 3)
            nc.tensor.matmul(bank[:, 0:C], mean_row[:, :], w_scaled[:, :], start=True, stop=True).then_inc(averaged, 1)
            nc.tensor.matmul(bank_b[:, 0:C], ln_b3[:, :], wt[:, :], start=True, stop=False)
            nc.tensor.matmul(bank_b[:, 0:C], k.ones[0:1, 0:3], b_row[:, :], start=False, stop=True).then_inc(averaged, 1)

        @block.gpsimd
        def _(pool):
            pool.wait_ge(ready, 1)
            nc.gpsimd.tensor_tensor(k.rstd[:, :], k.var[:, :], k.minus_half[:, :], ALU.pow).then_inc(rsd, 1)

        @block.vector
        def _(dve_):
            dve_.wait_ge(w_in, 64)
            nc.vector.tensor_scalar(w_scaled[:, :], wt[:, :], ln_w[:, 0:1], None, ALU.mult).then_inc(scaled, 1)
            nc.vector.memset(mean_row[:, :], 1.0 / C).then_inc(scaled, 1)
            nc.vector.tensor_scalar(ln_b3[:, :], k.ones[:, 0:3], ln_b[:, 0:1], None, ALU.mult).then_inc(scaled, 1)
            link = Link(dve_, dve)
            layer_stats(k, dve_, link, k.x, ready)
            dve_.wait_ge(averaged, 2)
            nc.vector.tensor_tensor(k.ffn_wc[:, :], w_scaled[:, :], bank[:, 0:C], ALU.subtract)
            link(nc.vector.tensor_copy(bias3[:, :], bank_b[:, 0:C]))
            three_parts(k, link, "ffn_bias", bias3[:, :], k.ffn_bias[:, :], st)
            dve_.wait_ge(rsd, 1)
            normalise(k, dve_, k.x, k.f0, put, 0)


def normalise(k, eng, x, to, done, base):
    with eng.Fori(0, QUADS) as g:
        for j in range(QUAD):
            t = g * QUAD + j
            ins = k.nc.vector.tensor_scalar(to[:, one(t), :], x[:, one(t), :], k.mean[:, one(t)], k.rstd[:, one(t)],
                                            ALU.subtract, ALU.mult)
        ins.then_inc(done, 1)


def feed_forward(k):
    nc = k.nc
    st = ExitStack()
    with st:
        act_out = [k.sb(f"ffn_silu{i}", [P, QUAD, C], stack=st) for i in range(QUADS)]
        diag = [k.sb(f"ffn_diag{i}", [P, QUAD, C], stack=st) for i in range(QUADS)]
        tanh = [k.sb(f"ffn_tanh{i}", [P, QUAD, C], stack=st) for i in range(2)]
        blend = [k.sb(f"ffn_blend{i}", [P, QUAD, C], stack=st) for i in range(2)]
        turned_sb = [k.sb(f"ffn_turned{i}", [P, BANK], stack=st) for i in range(2)]
        stats = [k.sb(f"ffn_stats{i}", [P, QUAD, 6], stack=st) for i in range(2)]
        dif = k.sb("ffn_dif", [P, QUAD], stack=st)
        sq = k.sb("ffn_sq", [P, QUAD], stack=st)
        both = k.sb("ffn_both", [P, QUAD], stack=st)
        var = [k.sb(f"ffn_var{i}", [P, QUAD], stack=st) for i in range(4)]
        rstd = [k.sb(f"ffn_rstd{i}", [P, QUAD], stack=st) for i in range(2)]
        bank_t = [k.ps(f"ffn_bank_t{i}", [P, BANK], st) for i in range(4)]
        bank_z = [k.ps(f"ffn_bank_z{i}", [P, BANK], st) for i in range(4)]
        s_tanh, s_blend, s_silu, s_var, s_rstd, s_diag, s_turn, s_copy, s_z, dve = (
            k.sem("ffn_s_tanh"), k.sem("ffn_s_blend"), k.sem("ffn_s_silu"), k.sem("ffn_s_var"), k.sem("ffn_s_rstd"),
            k.sem("ffn_s_diag"), k.sem("ffn_s_turn"), k.sem("ffn_s_copy"), k.sem("ffn_s_z"), k.sem("ffn_dve"))
        ITEMS = ITERS * QUADS
        LINKS = 3
        block = st.enter_context(nc.Block())

        def schedule(eng, stages, first):
            def step(s, base):
                for stage, lag in stages:
                    j = s - lag
                    if base is not None or 0 <= j < ITEMS:
                        stage(j, base)
            last = ITEMS + max(lag for _, lag in stages)
            head = 2 * QUADS
            tail = ITEMS - QUADS
            for s in range(0, head):
                step(s, None)
            with eng.Fori(head // QUADS, tail // QUADS) as it:
                base = it * QUADS
                for g in range(QUADS):
                    step(g, base)
            for s in range(tail, last + 1):
                step(s, None)

        def at(j, base, n):
            return (j + n) if base is None else base + (j + n)

        def wait(eng, sem, j, base, n):
            if base is not None or j + n >= 1:
                eng.wait_ge(sem, at(j, base, n))

        def source(j, base):
            if base is None and j < QUADS:
                return k.f0[:, j * QUAD:(j + 1) * QUAD, :]
            return bank_z[j % 4][:, :].rearrange("p (q c) -> p q c", q=QUAD)

        T_TANH, T_SILU, T_BLEND, T_STATS, T_RSTD, T_DIAG = 0, 1, 0, 2, 2, 3
        T_TURN, T_COPY, T_PRODUCT = 5, 6, 6

        @block.scalar
        def _(act):
            def do_tanh(j, base):
                if base is not None or j >= QUADS:
                    wait(act, s_z, j, base, 1 - QUADS)
                wait(act, s_blend, j, base, -1)
                nc.scalar.activation(tanh[j % 2][:, :, :], source(j, base), ACT.Tanh).then_inc(s_tanh, 1)

            def do_silu(j, base):
                wait(act, s_blend, j, base, 1)
                wait(act, s_turn, j, base, 1 - QUADS)
                nc.scalar.activation(act_out[j % QUADS][:, :, :], blend[j % 2][:, :, :], ACT.Silu).then_inc(s_silu, 1)

            def do_copy(j, base):
                wait(act, s_turn, j, base, 1)
                wait(act, s_z, j, base, -1)
                nc.scalar.activation(turned_sb[j % 2][:, :], bank_t[j % 4][:, :], ACT.Copy).then_inc(s_copy, 1)

            schedule(act, [(do_copy, T_COPY), (do_tanh, T_TANH), (do_silu, T_SILU)], 0)

        @block.vector
        def _(dve_):
            def do_blend(j, base):
                wait(dve_, s_tanh, j, base, 1)
                wait(dve_, s_silu, j, base, -1)
                nc.vector.scalar_tensor_tensor(blend[j % 2][:, :, :], tanh[j % 2][:, :, :], 0.01, source(j, base),
                                               ALU.mult, ALU.add).then_inc(s_blend, 1)

            def do_moments(j, base):
                wait(dve_, s_silu, j, base, 1)
                stats_ = stats[j % 2]
                for q in range(QUAD):
                    ins = nc.vector.bn_stats(stats_[:, q, :], act_out[j % QUADS][:, q, :])
                ins.then_inc(dve, 1)

            def do_var(j, base):
                stats_ = stats[j % 2]
                n = at(j, base, 0) * LINKS
                dve_.wait_ge(dve, n + 1)
                nc.vector.tensor_tensor(dif[:, :], stats_[:, :, 1], stats_[:, :, 4], ALU.subtract).then_inc(dve, 1)
                nc.vector.scalar_tensor_tensor(both[:, :], stats_[:, :, 2], C * EPS, stats_[:, :, 5],
                                               ALU.add, ALU.add)
                dve_.wait_ge(dve, n + 2)
                nc.vector.scalar_tensor_tensor(sq[:, :], dif[:, :], 0.25, dif[:, :], ALU.mult, ALU.mult).then_inc(dve, 1)
                dve_.wait_ge(dve, n + 3)
                wait(dve_, s_rstd, j, base, -3)
                nc.vector.scalar_tensor_tensor(var[j % 4][:, :], both[:, :], 1.0 / C, sq[:, :],
                                               ALU.mult, ALU.add).then_inc(s_var, 1)

            schedule(dve_, [(do_moments, T_STATS), (do_blend, T_BLEND), (do_var, T_STATS)], 0)
            for g in range(QUADS):
                dve_.wait_ge(s_z, ITEMS - QUADS + g + 1)
                xg = k.x[:, g * QUAD:(g + 1) * QUAD, :]
                nc.vector.tensor_tensor(xg, xg, bank_z[g % 4][:, :].rearrange("p (q c) -> p q c", q=QUAD),
                                        ALU.add).then_inc(s_blend, 1)

        @block.gpsimd
        def _(pool):
            ident = k.ident[:, :].rearrange("p (o c) -> p o c", o=1).broadcast_to([P, QUAD, C])

            def do_rstd(j, base):
                wait(pool, s_var, j, base, 1)
                wait(pool, s_diag, j, base, -1)
                nc.gpsimd.tensor_tensor(rstd[j % 2][:, :], var[j % 4][:, :], k.minus_half[:, 0:QUAD], ALU.pow).then_inc(s_rstd, 1)

            def do_diag(j, base):
                wait(pool, s_rstd, j, base, 1)
                wait(pool, s_turn, j, base, 1 - QUADS)
                nc.gpsimd.tensor_tensor(diag[j % QUADS][:, :, :], ident,
                                        rstd[j % 2][:, :].rearrange("p (q o) -> p q o", o=1).broadcast_to([P, QUAD, C]),
                                        ALU.mult).then_inc(s_diag, 1)

            schedule(pool, [(do_rstd, T_RSTD), (do_diag, T_DIAG)], 0)

        @block.tensor
        def _(pe):
            def do_turn(j, base):
                wait(pe, s_diag, j, base, 1)
                wait(pe, s_copy, j, base, -3)
                for q in range(QUAD):
                    mm = nc.tensor.matmul(bank_t[j % 4][:, q * C:(q + 1) * C], act_out[j % QUADS][:, q, :],
                                          diag[j % QUADS][:, q, :], start=True, stop=True)
                mm.then_inc(s_turn, 1)

            def do_product(j, base):
                wait(pe, s_copy, j, base, 1)
                wait(pe, s_blend, j, base, QUADS - 3)
                for q in range(QUAD):
                    out = bank_z[j % 4][:, q * C:(q + 1) * C]
                    nc.tensor.matmul(out, k.ones_bf[0:3, :], k.ffn_bias[:, :], start=True, stop=False)
                    mm = nc.tensor.matmul(out, turned_sb[j % 2][:, q * C:(q + 1) * C], k.ffn_wc[:, :],
                                          start=False, stop=True)
                mm.then_inc(s_z, 1)

            schedule(pe, [(do_turn, T_TURN), (do_product, T_PRODUCT)], 0)


def poly_weights(k, d):
    nc = k.nc
    st = ExitStack()
    with st:
        w1t, bk = k.sb("poly_w1t", [KPOLY, C], stack=st), k.sb("poly_bk", [KPOLY, C], stack=st)
        bank = k.ps("poly_w_bank", [P, 512], st)
        w_in, made, ready, rsd, dve = (
            k.sem("poly_w_in"), k.sem("poly_w_made"), k.sem("ln2_var"), k.sem("ln2_rstd"), k.sem("ln2_dve"))
        block = st.enter_context(nc.Block())

        @block.sync
        def _(sp):
            sp.dma_start(k.poly_w1[:, 0:KPOLY], d["w1"]).then_inc(w_in, 16)
            sp.dma_start(w1t[:, :], d["w1t"]).then_inc(w_in, 16)
            sp.dma_start(bk[:, :], d["bk"]).then_inc(w_in, 16)
            sp.dma_start(k.poly_w2[:, :, :], d["w2"]).then_inc(w_in, 16)

        @block.tensor
        def _(pe):
            pe.wait_ge(w_in, 64)
            nc.tensor.matmul(bank[:, 0:C], w1t[:, :], bk[:, :], start=True, stop=True).then_inc(made, 1)

        @block.gpsimd
        def _(pool):
            pool.wait_ge(ready, 1)
            nc.gpsimd.tensor_tensor(k.rstd[:, :], k.var[:, :], k.minus_half[:, :], ALU.pow).then_inc(rsd, 1)

        @block.vector
        def _(dve_):
            layer_stats(k, dve_, Link(dve_, dve), k.x, ready)
            dve_.wait_ge(made, 1)
            nc.vector.tensor_copy(k.poly_w1[:, KPOLY:], bank[:, 0:C])
            dve_.wait_ge(rsd, 1)


def poly(k):
    nc = k.nc
    st = ExitStack()
    with st:
        h4 = [k.sb(f"poly_h{i}", [P, QUAD, C], stack=st) for i in range(2)]
        h4t = [k.sb(f"poly_ht{i}", [P, BANK], stack=st) for i in range(2)]
        node = [k.sb(f"poly_node{i}", [P, KPOLY], stack=st) for i in range(2)]
        sums = [[k.sb(f"poly_sum{i}_{j}", [P, C], stack=st) for j in range(4)] for i in range(2)]
        bank_t = [k.ps(f"poly_bank_t{i}", [P, BANK], st) for i in range(2)]
        bank_n = [k.ps(f"poly_bank_n{i}", [P, 512], st) for i in range(2)]
        bank_w = [k.ps(f"poly_bank_w{i}", [P, BANK], st) for i in range(4)]
        normed, turned, copied, noded, put, wide, summed, done, stored, zeroed = (
            k.sem("poly_normed"), k.sem("poly_turned"), k.sem("poly_copied"), k.sem("poly_noded"), k.sem("poly_put"),
            k.sem("poly_wide"), k.sem("poly_summed"), k.sem("poly_done"), k.sem("poly_stored"), k.sem("poly_zeroed"))
        block = st.enter_context(nc.Block())

        @block.sync
        def _(sp):
            sp.wait_ge(done, TILES + 2)
            sp.dma_start(k.y_dram.rearrange("(p t) c -> p t c", t=TILES), k.y[:, :, :]).then_inc(stored, 16)
            sp.wait_ge(stored, 16)

        @block.gpsimd
        def _(pool):
            nc.gpsimd.memset(k.yg[:, :, :, :, :], 0.0).then_inc(zeroed, 1)

        QUAD_WIDE = QUAD * 4
        STEPS = KPOLY + 2

        @block.scalar
        def _(act):
            act.sem_inc(wide, 2 * QUAD_WIDE)
            with act.Fori(0, QUADS // 2) as i:
                for b in range(2):
                    act.wait_ge(turned, i * 2 + (b + 3))
                    act.wait_ge(wide, i * (2 * QUAD_WIDE) + (b + 1) * QUAD_WIDE)
                    nc.scalar.activation(h4t[b][:, :], bank_t[b][:, :], ACT.Copy).then_inc(copied, 1)
                for jj in range(2 * QUAD):
                    t = i * (2 * QUAD) + jj
                    act.wait_ge(noded, t + 1)
                    nc.scalar.activation(k.z[:, one(t), :].rearrange("p a c -> p (a c)"),
                                         bank_n[jj % 2][:, KPOLY:KPOLY + C], ACT.Copy)
                    act.wait_ge(done, t + 1)
                    nc.scalar.activation(node[jj % 2][:, :], bank_n[jj % 2][:, 0:KPOLY], ACT.Copy).then_inc(put, 1)

        @block.vector
        def _(dve_):
            dve_.sem_inc(turned, 2)
            dve_.sem_inc(done, 2)
            dve_.sem_inc(summed, STEPS)
            with dve_.Fori(0, QUADS // 2) as i:
                for b in range(2):
                    dve_.wait_ge(turned, i * 2 + (b + 1))
                    for j in range(QUAD):
                        t = i * (2 * QUAD) + (b * QUAD + j)
                        ins = nc.vector.tensor_scalar(h4[b][:, j, :], k.x[:, one(t), :], k.mean[:, one(t)],
                                                      k.rstd[:, one(t)], ALU.subtract, ALU.mult)
                    ins.then_inc(normed, 1)
                for jj in range(2 * QUAD):
                    t = i * (2 * QUAD) + jj
                    values, part = node[jj % 2], sums[jj % 2]
                    dve_.wait_ge(done, t + 1)
                    dve_.wait_ge(put, t + 3)
                    for m in range(KPOLY):
                        n, c = m // 4, m % 4
                        if c == 0:
                            dve_.wait_ge(wide, t * 4 + (n + 1 + 2 * QUAD_WIDE))
                        product, w, to = bank_w[n][:, c * C:(c + 1) * C], values[:, m:m + 1], part[c][:, :]
                        if n == 0:
                            ins = nc.vector.tensor_scalar(to, product, w, None, ALU.mult)
                        else:
                            dve_.wait_ge(summed, t * STEPS + (STEPS + m - 3))
                            ins = nc.vector.scalar_tensor_tensor(to, product, w, to, ALU.mult, ALU.add)
                        ins.then_inc(summed, 1)
                    dve_.wait_ge(summed, t * STEPS + (STEPS + KPOLY - 2))
                    nc.vector.tensor_tensor(part[0][:, :], part[0][:, :], part[1][:, :], ALU.add).then_inc(summed, 1)
                    dve_.wait_ge(summed, t * STEPS + (STEPS + KPOLY))
                    nc.vector.tensor_tensor(part[2][:, :], part[2][:, :], part[3][:, :], ALU.add).then_inc(summed, 1)
                    dve_.wait_ge(summed, t * STEPS + (STEPS + KPOLY + 2))
                    nc.vector.tensor_tensor(k.y[:, one(t), :].rearrange("p a c -> p (a c)"), part[0][:, :],
                                            part[2][:, :], ALU.add).then_inc(done, 1)

        @block.tensor
        def _(pe):
            pe.sem_inc(copied, 2)
            pe.sem_inc(put, 2)
            with pe.Fori(0, QUADS // 2) as i:
                for b in range(2):
                    pe.wait_ge(normed, i * 2 + (b + 1))
                    pe.wait_ge(copied, i * 2 + (b + 1))
                    for j in range(QUAD):
                        mm = nc.tensor.transpose(bank_t[b][:, j * C:(j + 1) * C], h4[b][:, j, :], k.ident[:, :])
                    mm.then_inc(turned, 1)
                for jj in range(2 * QUAD):
                    b, j = jj // QUAD, jj % QUAD
                    t = i * (2 * QUAD) + jj
                    if j == 0:
                        pe.wait_ge(copied, i * 2 + (b + 3))
                    lhs = h4t[b][:, j * C:(j + 1) * C]
                    pe.wait_ge(put, t + 1)
                    nc.tensor.matmul(bank_n[jj % 2][:, 0:KPOLY + C], lhs, k.poly_w1[:, :], start=True,
                                     stop=True).then_inc(noded, 1)
                    for n in range(4):
                        pe.wait_ge(summed, t * STEPS + 4 * (n + 1))
                        nc.tensor.matmul(bank_w[n][:, :], lhs, k.poly_w2[:, 4 * n:4 * n + 4, :], start=True,
                                         stop=True).then_inc(wide, 1)



def spread_and_mix(k, d, out):
    nc = k.nc
    st = ExitStack()
    with st:
        router = k.sb("router", [P, EXPERTS], stack=st)
        w1, w2 = k.sb("moe_w1", [P, EXPERTS, C], stack=st), k.sb("moe_w2", [P, EXPERTS, C], stack=st)
        b1, b2 = k.sb("moe_b1", [P, EXPERTS], stack=st), k.sb("moe_b2", [3, EXPERTS * C], BF16, stack=st)
        b2_rows = k.sb("moe_b2_rows", [3, EXPERTS * C], stack=st)
        number_i, number_f = k.sb("moe_number_i", [P, EXPERTS], I32, stack=st), k.sb("moe_number", [P, EXPERTS], stack=st)
        rows_sb = k.sb("d3_rows", [P, NODES], stack=st)
        stats = k.sb("moe_stats", [P, QUAD, 6], stack=st)
        dif, sq, both = (k.sb(f"moe_{n}", [P, QUAD], stack=st) for n in ("dif", "sq", "both"))
        mean, var, rstd = ([k.sb(f"moe_{n}{i}", [P, QUAD], stack=st) for i in range(2)] for n in ("mean", "var", "rstd"))
        h4 = [k.sb(f"moe_h{i}", [P, QUAD, C], stack=st) for i in range(2)]
        h4t = [k.sb(f"moe_ht{i}", [P, BANK], stack=st) for i in range(2)]
        wide = [P, QUAD, EXPERTS]
        logit, prob, sorted_p, mask = (k.sb(f"moe_{n}", wide, stack=st) for n in ("logit", "prob", "sorted", "mask"))
        share = [k.sb(f"moe_share{i}", wide, stack=st) for i in range(2)]
        index = k.sb("moe_index", wide, U32, stack=st)
        index_f = k.sb("moe_index_f", [P, QUAD, 2], stack=st)
        top, den, rden = (k.sb(f"moe_{n}", [P, QUAD], stack=st) for n in ("top", "den", "rden"))
        hidden = [k.sb(f"moe_hidden{i}", [P, BANK], stack=st) for i in range(2)]
        bank_1 = [k.ps(f"moe_bank_1{i}", [P, BANK], st) for i in range(2)]
        bank_2 = [k.ps(f"moe_bank_2{i}", [P, BANK], st) for i in range(4)]
        bank_t = k.ps("moe_bank_t", [P, BANK], st)
        bank_s = k.ps("moe_bank_small", [P, BANK], st)
        acc = bank_s[:, 0:C]
        bank_l = bank_s[:, 2 * C:2 * C + QUAD * EXPERTS].rearrange("p (q e) -> p q e", q=QUAD)

        turning = Turning(k, st, "d3", calls=1, banks=bank_1)
        loaded, free, undiag = k.sem("d3_loaded"), k.sem("d3_free"), k.sem("d3_undiag")
        gathered = [k.sem(f"y_gathered{i}") for i in range(2)]
        rounds, w_in, numbered = k.sem("z_rounds"), k.sem("moe_w_in"), k.sem("moe_numbered")
        var_made, rstd_made, split, settled = (
            k.sem("moe_var_made"), k.sem("moe_rstd_made"), k.sem("moe_b2_split"), k.sem("moe_settled"))
        normed, turned, copied, routed, shifted, exped, chosen = (
            k.sem("moe_normed"), k.sem("moe_turned"), k.sem("moe_copied"), k.sem("moe_routed"),
            k.sem("moe_shifted"), k.sem("moe_exped"), k.sem("moe_chosen"))
        first, gelued, second, mixed = k.sem("moe_first"), k.sem("moe_gelued"), k.sem("moe_second"), k.sem("moe_mixed")
        stored = k.sem("out_stored")
        paced = k.sem("moe_paced")
        rows = d["adj"].rearrange("(p t) j -> t p j", t=TILES)
        out_rows = out.rearrange("(p t) c -> p t c", t=TILES)
        ROUNDS = QUAD * (SLOTS + 1)
        MIXES = QUAD * EXPERTS
        WEIGHTS = 5
        block = st.enter_context(nc.Block())

        @block.sync
        def _(sp):
            loads = [(router[:, :], d["router_t"]), (w1[:, :, :], d["e_w1"]), (w2[:, :, :], d["e_w2"]),
                     (b1[:, :], d["e_b1"]), (b2_rows[:, :], d["e_b2"].broadcast_to([3, EXPERTS * C]))]
            assert len(loads) == WEIGHTS
            for to, of in loads:
                sp.dma_start(to, of).then_inc(w_in, 16)
            with flagged(k, sp) as (t, rank):
                sp.wait_ge(free, rank + 1)
                sp.sem_inc(k.sp_ticks, 1)
                sp.dma_start(rows_sb[:, :], rows[one(t)].rearrange("a p j -> p (a j)")).then_inc(loaded, 16)
            for g in range(QUADS):
                sp.wait_ge(mixed, MIXES * (g + 1))
                ts = slice(g * QUAD, (g + 1) * QUAD)
                sp.dma_start(out_rows[:, ts, :], k.x[:, ts, :]).then_inc(stored, 16)
            sp.wait_ge(stored, 16 * QUADS)

        @block.gpsimd
        def _(pool):
            nc.gpsimd.iota(number_i[:, :], pattern=[[1, EXPERTS]], base=0, channel_multiplier=0).then_inc(numbered, 1)
            pool.wait_ge(numbered, 1)
            nc.gpsimd.tensor_copy(number_f[:, :], number_i[:, :]).then_inc(numbered, 1)

            def power(g):
                pool.wait_ge(var_made, g + 1)
                nc.gpsimd.tensor_tensor(rstd[g % 2][:, :], var[g % 2][:, :], k.minus_half[:, 0:QUAD],
                                        ALU.pow).then_inc(rstd_made, 1)

            for g in range(QUADS):
                if g >= 2:
                    pool.wait_ge(gathered[g % 2], QUAD_GATHERS * (g // 2))
                    pool.wait_ge(rounds, ROUNDS * (g - 1))
                for j in range(QUAD):
                    for s in range(SLOTS):
                        gather(nc, k.yg[:, g % 2, j, s, :], k.y_dram,
                               k.idx[:, g * QUAD + j, s:s + 1]).then_inc(gathered[g % 2], 16)
                    if g >= 1 and j == 1:
                        power(g - 1)
            power(QUADS - 1)

        @block.vector
        def _(dve_):
            dve_.sem_inc(free, 1)
            with flagged(k, dve_) as (t, rank):
                z = k.z[:, one(t), :].rearrange("p a c -> p (a c)")
                dve_.wait_ge(loaded, rank * 16 + 16)
                diag = rows_sb[:, :].rearrange("p (q t) -> p q t", t=TILES)[:, :, one(t)]
                nc.vector.tensor_tensor(diag, diag, k.not_ident[:, :].rearrange("p (q o) -> p q o", o=1),
                                        ALU.mult).then_inc(undiag, 1)
                dve_.wait_ge(turning.used, turning.done(rank, 0))
                nc.vector.tensor_tensor(z, acc, z, ALU.add).then_inc(free, 1)
            nc.vector.drain()
            dve_.wait_ge(w_in, 16 * WEIGHTS)
            three_parts(k, Link(dve_, split), "moe_b2", b2_rows[:, :], b2[:, :], st)
            dve_.sem_inc(split, 1)
            dve_.wait_ge(numbered, 2)
            links_per_quad = 20

            def sums(g, b):
                dve_.wait_ge(gathered[b], (g - b) * (QUAD_GATHERS // 2) + QUAD_GATHERS)
                for s in range(-1, SLOTS):
                    for j in range(QUAD):
                        n = (s + 1) * QUAD + j
                        t = g * QUAD + j
                        to = k.z[:, one(t), :].rearrange("p a c -> p (a c)")
                        if s < 0:
                            row, w = k.y[:, one(t), :].rearrange("p a c -> p (a c)"), k.dcol[:, one(t)]
                        else:
                            row, w = k.yg[:, b, j, s, :], k.val[:, one(t), s]
                            dve_.wait_ge(rounds, g * ROUNDS + (n - 3))
                        nc.vector.scalar_tensor_tensor(to, row, w, to, ALU.mult, ALU.add).then_inc(rounds, 1)
                dve_.wait_ge(rounds, g * ROUNDS + ROUNDS)

            def statistics(g, b, link):
                xg = k.x[:, bass.ts(g, QUAD), :]
                link(nc.vector.scalar_tensor_tensor(xg, k.z[:, bass.ts(g, QUAD), :], 0.0, xg, ALU.max, ALU.add))
                dve_.sem_inc(paced, 1)
                for j in range(QUAD):
                    ins = nc.vector.bn_stats(stats[:, j, :], k.x[:, one(g * QUAD + j), :])
                link(ins)
                nc.vector.tensor_tensor(dif[:, :], stats[:, :, 1], stats[:, :, 4], ALU.subtract)
                nc.vector.tensor_tensor(mean[b][:, :], stats[:, :, 1], stats[:, :, 4], ALU.add)
                link(nc.vector.scalar_tensor_tensor(both[:, :], stats[:, :, 2], C * EPS, stats[:, :, 5],
                                                    ALU.add, ALU.add))
                nc.vector.tensor_scalar(mean[b][:, :], mean[b][:, :], 0.5, None, ALU.mult)
                link(nc.vector.scalar_tensor_tensor(sq[:, :], dif[:, :], 0.25, dif[:, :], ALU.mult, ALU.mult))
                nc.vector.scalar_tensor_tensor(var[b][:, :], both[:, :], 1.0 / C, sq[:, :],
                                               ALU.mult, ALU.add).then_inc(var_made, 1)

            def mix(g, b):
                for e in range(EXPERTS):
                    dve_.wait_ge(second, g * EXPERTS + (e + 1))
                    for j in range(QUAD):
                        n = e * QUAD + j
                        xt = k.x[:, one(g * QUAD + j), :].rearrange("p a c -> p (a c)")
                        if e > 0:
                            dve_.wait_ge(mixed, g * MIXES + (n - 3))
                        nc.vector.scalar_tensor_tensor(xt, bank_2[e % 4][:, j * C:(j + 1) * C],
                                                       share[b][:, j, e:e + 1], xt, ALU.mult, ALU.add).then_inc(mixed, 1)

            def norm(g, b, link):
                dve_.wait_ge(rstd_made, g + 1)
                for j in range(QUAD):
                    ins = nc.vector.tensor_scalar(h4[b][:, j, :], k.x[:, one(g * QUAD + j), :].rearrange("p a c -> p (a c)"),
                                                  mean[b][:, j:j + 1], rstd[b][:, j:j + 1], ALU.subtract, ALU.mult)
                ins.then_inc(normed, 1)
                dve_.wait_ge(normed, g + 1)
                xg = k.x[:, bass.ts(g, QUAD), :]
                link(nc.vector.tensor_tensor(xg, xg, h4[b][:, :, :], ALU.add))

            def route(g, b, link):
                def wide_of(x):
                    return x.rearrange("p (t o) -> p t o", o=1).broadcast_to(wide)

                dve_.wait_ge(routed, g + 1)
                link(nc.vector.tensor_copy(logit[:, :, :], bank_l))
                link(nc.vector.tensor_reduce(top[:, :], logit[:, :, :], AX_X, ALU.max))
                nc.vector.tensor_tensor(prob[:, :, :], logit[:, :, :], wide_of(top[:, :]),
                                        ALU.subtract).then_inc(shifted, 1)
                dve_.wait_ge(exped, g + 1)
                link(nc.vector.tensor_reduce(den[:, :], prob[:, :, :], AX_X, ALU.add))
                link(nc.vector.reciprocal(rden[:, :], den[:, :]))
                link(nc.vector.tensor_tensor(prob[:, :, :], prob[:, :, :], wide_of(rden[:, :]), ALU.mult))
                dve_.sem_inc(paced, 1)
                for j in range(QUAD):
                    ins = nc.vector.max(sorted_p[:, j, :], prob[:, j, :])
                link(ins)
                dve_.sem_inc(paced, 1)
                for j in range(QUAD):
                    ins = nc.vector.max_index(index[:, j, :], sorted_p[:, j, :], prob[:, j, :])
                link(nc.vector.tensor_tensor(den[:, :], sorted_p[:, :, 0], sorted_p[:, :, 1], ALU.add))
                nc.vector.tensor_copy(index_f[:, :, :], index[:, :, 0:2])
                link(nc.vector.tensor_scalar(den[:, :], den[:, :], 1e-12, None, ALU.max))
                link(nc.vector.reciprocal(rden[:, :], den[:, :]))
                number = number_f[:, :].rearrange("p (o e) -> p o e", o=1).broadcast_to(wide)
                nc.vector.tensor_tensor(share[b][:, :, :], number, wide_of(index_f[:, :, 0]), ALU.is_equal)
                link(nc.vector.tensor_tensor(mask[:, :, :], number, wide_of(index_f[:, :, 1]), ALU.is_equal))
                link(nc.vector.tensor_tensor(mask[:, :, :], mask[:, :, :], share[b][:, :, :], ALU.add))
                link(nc.vector.tensor_tensor(mask[:, :, :], mask[:, :, :], prob[:, :, :], ALU.mult))
                link(nc.vector.tensor_tensor(share[b][:, :, :], mask[:, :, :], wide_of(rden[:, :]), ALU.mult))

            def step(g, b):
                link = Link(dve_, settled, g * links_per_quad)
                sums(g, b)
                statistics(g, b, link)
                if not isinstance(g, int) or g > 0:
                    mix(g - 1, 1 - b)
                norm(g, b, link)
                route(g, b, link)
                while link.n < links_per_quad:
                    link.n += 1
                    dve_.sem_inc(settled, 1)

            by_quads(dve_, step)
            mix(QUADS - 1, 1)

        @block.tensor
        def _(pe):
            with flagged(k, pe) as (t, rank):
                pe.wait_ge(undiag, rank + 1)
                turning.multiply(pe, rank, 0, rows_sb[:, :], lambda b: k.y[:, b, :], acc)
            pe.wait_ge(w_in, 16 * WEIGHTS)

            def turn(g, b):
                pe.wait_ge(normed, g + 1)
                for j in range(QUAD):
                    mm = nc.tensor.transpose(bank_t[:, j * C:(j + 1) * C], h4[b][:, j, :], k.ident[:, :])
                mm.then_inc(turned, 1)
                pe.wait_ge(copied, g + 1)
                for j in range(QUAD):
                    mm = nc.tensor.matmul(bank_l[:, j, :], h4t[b][:, j * C:(j + 1) * C], router[:, :],
                                          start=True, stop=True)
                mm.then_inc(routed, 1)

            def experts(g, b):
                for e in range(EXPERTS + 1):
                    if e < EXPERTS:
                        wait_from(pe, gelued, g * EXPERTS + (e - 1))
                        nc.tensor.matmul(bank_1[e % 2][:, :], w1[:, e, :], h4t[b][:, :],
                                         start=True, stop=True).then_inc(first, 1)
                    if e >= 1:
                        m = e - 1
                        pe.wait_ge(gelued, g * EXPERTS + (m + 1))
                        wait_from(pe, mixed, g * MIXES + QUAD * (m - 3))
                        for j in range(QUAD):
                            to = bank_2[m % 4][:, j * C:(j + 1) * C]
                            nc.tensor.matmul(to, k.ones_bf[0:3, :], b2[:, m * C:(m + 1) * C], start=True, stop=False)
                            mm = nc.tensor.matmul(to, hidden[m % 2][:, j * C:(j + 1) * C], w2[:, m, :],
                                                  start=False, stop=True)
                        mm.then_inc(second, 1)

            def step(g, b):
                if not isinstance(g, int) or g > 0:
                    experts(g - 1, 1 - b)
                turn(g, b)

            pe.wait_ge(split, 8)
            by_quads(pe, step)
            experts(QUADS - 1, 1)

        @block.scalar
        def _(act):
            turning.start(act)
            with flagged(k, act) as (t, rank):
                turning.copy(act, rank, 0)
            act.wait_ge(w_in, 16 * WEIGHTS)

            def gelus(g):
                for e in range(EXPERTS):
                    act.wait_ge(first, g * EXPERTS + (e + 1))
                    wait_from(act, second, g * EXPERTS + (e - 1))
                    nc.scalar.activation(hidden[e % 2][:, :], bank_1[e % 2][:, :], ACT.Gelu,
                                         bias=b1[:, e:e + 1]).then_inc(gelued, 1)

            def step(g, b):
                if not isinstance(g, int) or g > 0:
                    gelus(g - 1)
                act.wait_ge(turned, g + 1)
                nc.scalar.activation(h4t[b][:, :], bank_t[:, :], ACT.Copy).then_inc(copied, 1)
                act.wait_ge(shifted, g + 1)
                nc.scalar.activation(prob[:, :, :], prob[:, :, :], ACT.Exp).then_inc(exped, 1)

            by_quads(act, step)
            gelus(QUADS - 1)


def program(nc, d, out):
    stack = ExitStack()
    with stack:
        k = Core(nc, stack)
        k.t1_dram = nc.dram_tensor("t1_rows", (NODES, WIDE), F32).ap()
        k.e_dram = nc.dram_tensor("e_rows", (NODES, HEADS), F32).ap()
        k.ecol_dram = nc.dram_tensor("e_columns", (2 * HEADS, NODES), F32).ap()
        k.y_dram = nc.dram_tensor("y_rows", (NODES, C), F32).ap()
        k.ident = k.sb("ident", [P, P])
        k.not_ident = k.sb("not_ident", [P, P])
        k.ones = k.sb("ones", [P, P])
        k.ones_bf = k.sb("ones_bf", [P, P], BF16)
        k.of_three = k.sb("of_three", [P, 3])
        k.tiny = k.sb("tiny", [P, 1])
        k.minus_half = k.sb("minus_half", [P, TILES])
        k.mean, k.var, k.rstd = k.sb("mean", [P, TILES]), k.sb("var", [P, TILES]), k.sb("rstd", [P, TILES])
        k.dif, k.sq = k.sb("dif", [P, TILES]), k.sb("sq", [P, TILES])
        k.stats = k.sb("stats", [P, TILES, 6])
        k.stats_s, k.stats_n = k.sem("stats_s"), 0
        k.dcol = k.sb("dcol", [P, TILES])
        k.val = k.sb("val", [P, TILES, SLOTS])
        k.idx = k.sb("idx", [P, TILES, SLOTS], U32)
        k.e6 = k.sb("e6", [P, TILES, 2 * HEADS])
        k.tiles_left = k.sb("tiles_left", [1, TILES])
        k.order = k.sb("order", [1, TILES], I32)
        k.count = k.sb("count", [1, 1], I32)
        k.after_flagged = k.sem("after_flagged")
        k.sp_ticks = k.sem("sp_ticks")
        k.gathered = k.sem("gathered")
        k.plain = k.sem("plain_sums")
        with ExitStack() as gnn:
            k.ww = k.sb("ww", [P, HEADS, 3 * C], stack=gnn)
            k.gru_bias = [k.sb(f"gru_bias{i}", [6, BANK], BF16, stack=gnn) for i in range(2)]
            k.x = k.sb("x", [P, TILES, C], stack=gnn)
            prepare(k, d)
            with ExitStack() as gat:
                k.g = k.sb("g", [P, TILES, SLOTS, WIDE], stack=gat)
                extract(k, d)
                dense_logits(k, d)
                attend(k, d)
            dense_attend(k, d)
            k.ffn_wc = k.sb("ffn_wc", [P, C], stack=gnn)
            k.ffn_bias = k.sb("ffn_bias", [3, C], BF16, stack=gnn)
            with ExitStack() as ffn:
                k.f0 = k.sb("f0", [P, TILES, C], stack=ffn)
                ffn_weights(k, d)
                feed_forward(k)
            with ExitStack() as gnn2:
                k.z = k.sb("z", [P, TILES, C], stack=gnn2)
                k.y = k.sb("y", [P, TILES, C], stack=gnn2)
                k.yg = k.sb("yg", [P, 2, QUAD, SLOTS, C], stack=gnn2)
                with ExitStack() as poly_stack:
                    k.poly_w1 = k.sb("poly_w1", [P, KPOLY + C], stack=poly_stack)
                    k.poly_w2 = k.sb("poly_w2", [P, KPOLY, C], stack=poly_stack)
                    poly_weights(k, d)
                    poly(k)
                spread_and_mix(k, d, out)


def kernel(**inputs):
    import numpy as _np
    import concourse.bacc as _bacc
    from concourse import mybir as _mybir
    from concourse.bass_utils import run_bass_kernel_spmd as _run

    nc = _bacc.Bacc("TRN2", target_bir_lowering=False, num_devices=1)
    arrays = lay_out(inputs)
    d = {}
    for name, a in arrays.items():
        d[name] = nc.dram_tensor(f"in_{name}", a.shape, _mybir.dt.from_np(a.dtype), kind="ExternalInput").ap()
    out = nc.dram_tensor("out_0", (NODES, C), F32, kind="ExternalOutput").ap()
    program(nc, d, out)
    r = _run(nc, [{f"in_{n}": a for n, a in arrays.items()}], core_ids=[0])
    return r.results[0]["out_0"]


def lay_out(inputs):
    import numpy as np

    i = {n: np.asarray(a) for n, a in inputs.items()}
    row = lambda a: a.reshape(1, -1)
    laid = {
        "x": i["x"],
        "adj": i["adj"],
        "gat_wt": i["L0_gnn_gat_W"].transpose(2, 0, 1),
        "gat_at": i["L0_gnn_gat_a"].reshape(HEADS, 2, C).transpose(2, 1, 0).reshape(C, 2 * HEADS),
        "wih_e": i["L0_gnn_edge_Wih"].T,
        "whh_e": i["L0_gnn_edge_Whh"].T,
        "wih_n": i["L0_gnn_node_Wih"].T,
        "whh_n": i["L0_gnn_node_Whh"].T,
        "bih_e": row(i["L0_gnn_edge_bih"]),
        "bhh_e": row(i["L0_gnn_edge_bhh"]),
        "bih_n": row(i["L0_gnn_node_bih"]),
        "bhh_n": row(i["L0_gnn_node_bhh"]),
        "ln_w": i["L0_ffn_ln_w"].reshape(C, 1),
        "ln_b": i["L0_ffn_ln_b"].reshape(C, 1),
        "ffn_wt": i["L0_ffn_W"].T,
        "ffn_b": row(i["L0_ffn_b"]),
        "w1": i["L1_gnn_W1"],
        "w1t": i["L1_gnn_W1"].T,
        "w2": i["L1_gnn_W2"].transpose(1, 0, 2),
        "bk": i["L1_gnn_b"],
        "router_t": i["L1_ffn_router_w"].T,
        "e_w1": i["L1_ffn_w1"].transpose(1, 0, 2),
        "e_b1": i["L1_ffn_b1"].T,
        "e_w2": i["L1_ffn_w2"].transpose(1, 0, 2),
        "e_b2": row(i["L1_ffn_b2"]),
    }
    return {n: np.ascontiguousarray(a) for n, a in laid.items()}
```

```python
from contextlib import ExitStack, contextmanager

import concourse.bass as bass
from concourse import mybir

ALU = mybir.AluOpType
ACT = mybir.ActivationFunctionType
AX_X = mybir.AxisListType.X
F32 = mybir.dt.float32
BF16 = mybir.dt.bfloat16
U32 = mybir.dt.uint32
I32 = mybir.dt.int32
U8 = mybir.dt.uint8

P = 128
NODES = 4096
C = 128
TILES = NODES // P
QUAD = 4
QUADS = TILES // QUAD
BANK = QUAD * C
HEADS = 3
SLOTS = 8
WIDE = C + 2 * HEADS
EPS = 1e-5
ALPHA = 0.2
NEG_INF = -9000000000000000.0
FAR = -1.0e30
KPOLY = 16
EXPERTS = 8
ITERS = 30


class Core:

    def __init__(self, nc, stack):
        self.nc, self.stack = nc, stack

    def sb(self, name, shape, dtype=F32, stack=None):
        return (stack or self.stack).enter_context(self.nc.sbuf_tensor(name, shape, dtype))

    def ps(self, name, shape, stack, dtype=F32):
        return stack.enter_context(self.nc.psum_tensor(name, shape, dtype))

    def sem(self, name):
        return self.stack.enter_context(self.nc.semaphore(name))


class Link:

    def __init__(self, engine, sem, base=0):
        self.engine, self.sem, self.base, self.n = engine, sem, base, 0

    def __call__(self, ins):
        self.n += 1
        ins.then_inc(self.sem, 1)
        self.engine.wait_ge(self.sem, self.base + self.n)


def one(t):
    return bass.ds(t, 1)


def wait_from(eng, sem, value):
    if not isinstance(value, int) or value > 0:
        eng.wait_ge(sem, value)


def by_quads(eng, step):
    step(0, 0)
    step(1, 1)
    with eng.Fori(1, QUADS // 2) as i:
        for b in range(2):
            step(i * 2 + b, b)


def three_parts(k, link, name, source, out, stack):
    nc = k.nc
    rows, n = source.shape[0], source.shape[1]
    hi, mid = (k.sb(f"{name}_{part}", [rows, n], BF16, stack=stack) for part in ("hi", "mid"))
    rest = source
    of_three = [k.of_three[0:rows, j:j + 1] for j in range(3)]
    link(nc.vector.tensor_copy(hi[:, :], source))
    link(nc.vector.tensor_tensor(rest, source, hi[:, :], ALU.subtract))
    link(nc.vector.tensor_copy(mid[:, :], rest))
    link(nc.vector.tensor_tensor(rest, rest, mid[:, :], ALU.subtract))
    link(nc.vector.tensor_scalar(hi[:, :], hi[:, :], of_three[0], None, ALU.mult))
    link(nc.vector.scalar_tensor_tensor(mid[:, :], mid[:, :], of_three[1], hi[:, :], ALU.mult, ALU.add))
    link(nc.vector.scalar_tensor_tensor(out, rest, of_three[2], mid[:, :], ALU.mult, ALU.add))


def layer_stats(k, eng, link, x, ready):
    nc = k.nc
    stats, dif, sq = k.stats, k.dif, k.sq
    for t in range(TILES):
        ins = nc.vector.bn_stats(stats[:, t, :], x[:, t, :])
    ins.then_inc(k.stats_s, 1)
    k.stats_n += 1
    eng.wait_ge(k.stats_s, k.stats_n)
    even_m, even_v, odd_m, odd_v = stats[:, :, 1], stats[:, :, 2], stats[:, :, 4], stats[:, :, 5]
    nc.vector.tensor_tensor(dif[:, :], even_m, odd_m, ALU.subtract)
    nc.vector.tensor_tensor(k.mean[:, :], even_m, odd_m, ALU.add)
    link(nc.vector.scalar_tensor_tensor(k.var[:, :], even_v, C * EPS, odd_v, ALU.add, ALU.add))
    nc.vector.tensor_scalar(k.mean[:, :], k.mean[:, :], 0.5, None, ALU.mult)
    link(nc.vector.scalar_tensor_tensor(sq[:, :], dif[:, :], 0.25, dif[:, :], ALU.mult, ALU.mult))
    nc.vector.scalar_tensor_tensor(k.var[:, :], k.var[:, :], 1.0 / C, sq[:, :],
                                   ALU.mult, ALU.add).then_inc(ready, 1)


def extract(k, d):
    nc = k.nc
    st = ExitStack()
    with st:
        x = k.x
        table = [k.sb(f"table_part{i}", [P, QUAD, WIDE], stack=st) for i in range(2)]
        spare = k.g[:, TILES - 1, :, :].rearrange("p s c -> p (s c)")
        gat_wt = spare[:, 0:HEADS * C].rearrange("p (h c) -> p h c", h=HEADS)
        wih_n = spare[:, HEADS * C:2 * HEADS * C]
        gat_at = spare[:, 2 * HEADS * C:2 * HEADS * C + 2 * HEADS]
        tile_no = k.sb("tile_no", [1, TILES], I32, stack=st)
        wa = k.sb("wa", [P, 2 * HEADS], stack=st)
        h4t = k.sb("h4t", [P, BANK], stack=st)
        bank_w = [k.ps(f"bank_w{i}", [P, 512], st) for i in range(HEADS)]
        bank_a = k.ps("bank_a", [P, 512], st)
        bank_t = k.ps("bank_t", [P, 512], st)
        bank_p = [k.ps(f"bank_p{i}", [P, QUAD, 8], st) for i in range(2)]
        x_in, w_in, d_in = k.sem("x_in_s"), k.sem("w_in"), k.sem("d_in")
        pool0, made, rsd, stats_in, dve0 = (
            k.sem("p0_pool"), k.sem("consts_made"), k.sem("p0_rstd"), k.sem("p0_var"), k.sem("p0_dve"))
        folded, wa_put = k.sem("folded"), k.sem("wa_put")
        normed, turned, put_t, prod, put_p = (
            k.sem("p0_normed"), k.sem("p0_turned"), k.sem("p0_put_t"),
            k.sem("p0_prod"), k.sem("p0_put_p"))
        stored = [k.sem(f"table_stored{i}") for i in range(2)]
        EARLY = QUADS // 2
        HALF = NODES // 2

        a = [k.sb(f"adj_rows{i}", [P, NODES], stack=st) for i in range(2)]
        signs = k.sb("signs", [P, HALF], BF16, stack=st)
        top = [k.sb(f"top{i}", [P, SLOTS], stack=st) for i in range(2)]
        raw = [k.sb(f"raw_index{i}", [P, SLOTS], U32, stack=st) for i in range(2)]
        off = [k.sb(f"off{i}", [P, SLOTS], stack=st) for i in range(2)]
        cnt = k.sb("cnt", [P, 2, 2, TILES], stack=st)
        found = h4t[:, 0:TILES * SLOTS].rearrange("p (t s) -> p t s", t=TILES)
        sixes = h4t[:, TILES * SLOTS:TILES * (SLOTS + 2 * HEADS)].rearrange("p (t c) -> p t c", t=TILES)
        nfound = k.sb("nfound", [P, TILES], stack=st)
        twice = k.sb("twice", [P, TILES], stack=st)
        bad = k.sb("bad", [P, 2, TILES], stack=st)
        good = k.sb("good", [P, TILES], stack=st)
        keys = [k.sb(f"flag_keys{i}", [1, TILES], stack=st) for i in range(2)]
        order = k.sb("flag_order", [1, TILES], stack=st)
        countf = k.sb("flag_count", [1, 1], stack=st)
        bank = k.ps("bank_flags", [P, 512], st)

        loaded = [k.sem(f"adj_loaded{i}") for i in range(2)]
        undiag, maxed, indexed, off_s, idx_ready = (
            k.sem("undiag"), k.sem("maxed"), k.sem("indexed"), k.sem("off_s"), k.sem("idx_ready"))
        counted, zeroed, dve, summed = k.sem("counted"), k.sem("g_zeroed"), k.sem("p1_dve"), k.sem("bad_summed")
        half_counted, bad_made = k.sem("half_counted"), k.sem("bad_made")
        rows = d["adj"].rearrange("(p t) j -> t p j", t=TILES)
        block = st.enter_context(nc.Block())

        @block.sync
        def _(sp):
            sp.dma_start(x[:, :, :], d["x"].rearrange("(p t) c -> p t c", t=TILES)).then_inc(x_in, 16)
            sp.dma_start(a[0][:, :], rows[0]).then_inc(loaded[0], 16)
            for to, of in ((gat_wt, "gat_wt"), (gat_at, "gat_at"), (wih_n, "wih_n")):
                sp.dma_start(to, d[of]).then_inc(w_in, 16)
            sp.dma_start(a[1][:, :], rows[1]).then_inc(loaded[1], 16)
            with nc.allow_non_contiguous_dma("the diagonal"):
                diagonal = bass.AP(d["adj"].tensor, 0, [[TILES * (NODES + 1), P], [NODES + 1, TILES]])
                sp.dma_start(k.dcol[:, :], diagonal).then_inc(d_in, 16)

            def load(t):
                sp.wait_ge(indexed, t - 1)
                sp.wait_ge(counted, t)
                sp.dma_start(a[t % 2][:, :], rows[t]).then_inc(loaded[t % 2], 16)

            table_rows = k.t1_dram.rearrange("(p t) c -> p t c", t=TILES)
            for i in range(EARLY):
                if i >= 1:
                    load(i + 1)
                for b in range(2):
                    g = 2 * i + b
                    sp.wait_ge(put_p, g + 1)
                    sp.dma_start(table_rows[:, g * QUAD:(g + 1) * QUAD, :], table[b][:, :, :]).then_inc(stored[b], 16)
            for t in range(EARLY + 1, TILES):
                load(t)
            sp.wait_ge(d_in, 16)

        @block.scalar
        def _(act):
            def count(t, b):
                act.wait_ge(undiag, t + 1)
                act.wait_ge(counted, t + 1)
                for n in range(4):
                    if n > 0:
                        act.wait_ge(half_counted, t * 3 + n)
                    part = a[b][:, (n // 2) * HALF:(n // 2 + 1) * HALF]
                    to = cnt[:, n % 2, n // 2, one(t)]
                    if n % 2 == 0:
                        ins = nc.scalar.activation(signs[:, :], part, ACT.Sign, accum_out=to)
                    else:
                        ins = nc.scalar.activation(signs[:, :], part, ACT.Sign, bias=k.tiny[:, 0:1], accum_out=to)
                    ins.then_inc(half_counted if n < 3 else counted, 1)

            act.sem_inc(counted, 1)
            for i in range(EARLY):
                for b in range(2):
                    g = 2 * i + b
                    act.wait_ge(turned, g + 1)
                    if g >= 1:
                        act.wait_ge(prod, g)
                    nc.scalar.activation(h4t[:, :], bank_t[:, :], ACT.Copy).then_inc(put_t, 1)
                if i == 0:
                    act.wait_ge(folded, 2)
                    for h in range(HEADS):
                        nc.scalar.activation(k.ww[:, h, :], bank_w[h][:, 0:3 * C], ACT.Copy,
                                             scale=1.0 / HEADS)
                count(i, i % 2)
            with act.Fori(EARLY // 2, TILES // 2) as i:
                for b in range(2):
                    count(i * 2 + b, b)

        @block.vector
        def _(dve_):
            def zero_diagonal(i, b):
                dve_.wait_ge(loaded[b], i * 16 + 16)
                diag = a[b][:, :].rearrange("p (q t) -> p q t", t=TILES)[:, :, one(i * 2 + b)]
                nc.vector.tensor_tensor(diag, diag, k.not_ident[:, :].rearrange("p (q o) -> p q o", o=1),
                                        ALU.mult).then_inc(undiag, 1)

            def put_index(t, b):
                dve_.wait_ge(indexed, t + 1)
                dve_.wait_ge(off_s, t + 1)
                nc.vector.tensor_tensor(k.idx[:, one(t), :].rearrange("p a s -> p (a s)"), raw[b][:, :],
                                        off[b][:, :], ALU.add).then_inc(idx_ready, 1)

            def search(t, b):
                nc.vector.max(top[b][:, :], a[b][:, :]).then_inc(maxed, 1)
                dve_.wait_ge(maxed, t + 1)
                nc.vector.tensor_copy(k.val[:, one(t), :].rearrange("p a s -> p (a s)"), top[b][:, :])
                nc.vector.max_index(raw[b][:, :], top[b][:, :], a[b][:, :]).then_inc(indexed, 1)
                nc.vector.tensor_scalar(off[b][:, :], top[b][:, :], 0.0, 2.0 * NODES,
                                        ALU.is_le, ALU.mult).then_inc(off_s, 1)

            nc.vector.memset(k.ones[:, :], 1.0)
            nc.vector.memset(k.ones_bf[:, :], 1.0)
            nc.vector.memset(k.tiny[:, :], -1e-30)
            dve_.wait_ge(made, 1)
            link = Link(dve_, dve0)
            link(nc.vector.tensor_scalar(k.not_ident[:, :], k.ident[:, :], -1.0, 1.0, ALU.mult, ALU.add))
            nc.vector.tensor_tensor(k.of_three[:, :], k.ident[:, 0:3], k.ident[:, 3:6], ALU.add)
            dve_.wait_ge(x_in, 16)
            layer_stats(k, dve_, link, x, stats_in)
            zero_diagonal(0, 0)
            dve_.wait_ge(undiag, 1)
            search(0, 0)
            dve_.wait_ge(rsd, 1)
            dve_.wait_ge(folded, 1)
            nc.vector.tensor_copy(wa[:, :], bank_a[:, 0:2 * HEADS]).then_inc(wa_put, 1)
            for i in range(EARLY):
                for b in range(2):
                    g = 2 * i + b
                    if i >= 1:
                        dve_.wait_ge(turned, g - 1)
                        dve_.wait_ge(stored[b], 16 * i)
                    for j in range(QUAD):
                        t = g * QUAD + j
                        ins = nc.vector.tensor_scalar(table[b][:, j, 0:C], x[:, t, :], k.mean[:, t:t + 1],
                                                      k.rstd[:, t:t + 1], ALU.subtract, ALU.mult)
                    ins.then_inc(normed, 1)
                if i >= 1:
                    zero_diagonal(i // 2, i % 2)
                    dve_.wait_ge(undiag, i + 1)
                    put_index(i - 1, 1 - i % 2)
                    search(i, i % 2)
                for b in range(2):
                    g = 2 * i + b
                    dve_.wait_ge(prod, g + 1)
                    nc.vector.tensor_copy(table[b][:, :, C:WIDE], bank_p[b][:, :, 0:2 * HEADS]).then_inc(put_p, 1)
            with dve_.Fori(EARLY // 2, TILES // 2) as i:
                for b in range(2):
                    zero_diagonal(i, b)
                    dve_.wait_ge(undiag, i * 2 + (b + 1))
                    put_index(i * 2 + (b - 1), 1 - b)
                    search(i * 2 + b, b)
            put_index(TILES - 1, 1)
            link = Link(dve_, dve)
            dve_.wait_ge(pool0, 4)
            link(nc.vector.tensor_scalar(found, k.val[:, :, :], 0.0, None, ALU.is_gt))
            link(nc.vector.tensor_reduce(nfound[:, :], found, AX_X, ALU.add))
            link(nc.vector.tensor_scalar(twice[:, :], nfound[:, :], 2.0, -float(NODES), ALU.mult, ALU.add))
            dve_.wait_ge(counted, TILES + 1)
            for n in range(2):
                link(nc.vector.tensor_tensor(cnt[:, n, 0, :], cnt[:, n, 0, :], cnt[:, n, 1, :], ALU.add))
            nc.vector.tensor_tensor(bad[:, 0, :], cnt[:, 0, 0, :], nfound[:, :], ALU.not_equal)
            nc.vector.tensor_tensor(bad[:, 1, :], cnt[:, 1, 0, :], twice[:, :], ALU.not_equal).then_inc(bad_made, 1)
            dve_.wait_ge(summed, 1)
            link(nc.vector.tensor_scalar(good[:, :], bank[:, 0:TILES], 0.5, None, ALU.is_lt))
            nc.vector.tensor_tensor(k.val[:, :, :], k.val[:, :, :],
                                    good[:, :].rearrange("p (t o) -> p t o", o=1).broadcast_to([P, TILES, SLOTS]),
                                    ALU.mult)
            link(nc.vector.tensor_scalar(keys[0][:, :], good[0:1, :], -1.0, 1.0, ALU.mult, ALU.add))
            link(nc.vector.tensor_reduce(countf[:, :], keys[0][:, :], AX_X, ALU.add))
            nc.vector.tensor_copy(k.count[:, :], countf[:, :])
            link(nc.vector.tensor_tensor(keys[0][:, :], keys[0][:, :], k.tiles_left[:, :], ALU.mult))
            for r in range(TILES // 8):
                eight = order[:, 8 * r:8 * r + 8]
                link(nc.vector.max(eight, keys[r % 2][:, :]))
                if r < TILES // 8 - 1:
                    link(nc.vector.match_replace(out=keys[1 - r % 2][:, :], in_to_replace=eight,
                                                 in_values=keys[r % 2][:, :], imm_value=0.0))
            link(nc.vector.tensor_scalar(k.order[:, :], order[:, :], -1.0, float(TILES), ALU.mult, ALU.add))
            dve_.wait_ge(k.gathered, 16 * TILES * SLOTS)
            quarter = TILES // 4
            for q in range(4):
                ts = slice(q * quarter, (q + 1) * quarter)
                link(nc.vector.tensor_reduce(sixes[:, ts, :], k.g[:, ts, :, C:WIDE].rearrange("p t s c -> p t c s"),
                                             AX_X, ALU.add))
            link(nc.vector.scalar_tensor_tensor(k.e6[:, :, :], sixes, ALPHA, sixes,
                                                ALU.mult, ALU.max))

        @block.tensor
        def _(pe):
            pe.wait_ge(w_in, 16 * 3)
            for half in range(2):
                for h in range(HEADS):
                    c = half * HEADS + h
                    mm = nc.tensor.matmul(bank_a[:, c:c + 1], gat_wt[:, h, :], gat_at[:, c:c + 1],
                                          start=True, stop=True)
            mm.then_inc(folded, 1)
            for h in range(HEADS):
                mm = nc.tensor.matmul(bank_w[h][:, 0:3 * C], gat_wt[:, h, :], wih_n,
                                      start=True, stop=True)
            mm.then_inc(folded, 1)
            pe.wait_ge(made, 1)
            pe.wait_ge(wa_put, 1)
            for g in range(QUADS):
                pe.wait_ge(normed, g + 1)
                for j in range(QUAD):
                    mm = nc.tensor.transpose(bank_t[:, j * C:(j + 1) * C], table[g % 2][:, j, 0:C], k.ident[:, :])
                mm.then_inc(turned, 1)
                pe.wait_ge(put_t, g + 1)
                if g >= 2:
                    pe.wait_ge(put_p, g - 1)
                for j in range(QUAD):
                    mm = nc.tensor.matmul(bank_p[g % 2][:, j, 0:2 * HEADS], h4t[:, j * C:(j + 1) * C], wa[:, :],
                                          start=True, stop=True)
                mm.then_inc(prod, 1)
            pe.wait_ge(bad_made, 1)
            for i in range(2):
                mm = nc.tensor.matmul(bank[:, 0:TILES], k.ones[:, :], bad[:, i, :], start=(i == 0), stop=(i == 1))
            mm.then_inc(summed, 1)

        @block.gpsimd
        def _(pool):
            nc.gpsimd.memset(k.ident[:, :], 0.0).then_inc(pool0, 1)
            pool.wait_ge(pool0, 1)
            nc.gpsimd.affine_select(out=k.ident[:, :], in_=k.ident[:, :], compare_op=ALU.not_equal, fill=1.0,
                                    base=0, pattern=[[-1, P]], channel_multiplier=1).then_inc(made, 1)
            nc.gpsimd.memset(k.minus_half[:, :], -0.5).then_inc(pool0, 1)
            nc.gpsimd.iota(tile_no[:, :], pattern=[[1, TILES]], base=0, channel_multiplier=0).then_inc(pool0, 1)
            pool.wait_ge(pool0, 3)
            nc.gpsimd.tensor_scalar(k.tiles_left[:, :], tile_no[:, :], -1.0, float(TILES), ALU.mult,
                                    ALU.add).then_inc(pool0, 1)
            pool.wait_ge(stats_in, 1)
            nc.gpsimd.tensor_tensor(k.rstd[:, :], k.var[:, :], k.minus_half[:, :], ALU.pow).then_inc(rsd, 1)
            pool.wait_ge(folded, 2)
            nc.gpsimd.memset(k.g[:, :, :, :], 0.0).then_inc(zeroed, 1)
            pool.wait_ge(zeroed, 1)
            for b in range(2):
                pool.wait_ge(stored[b], 16 * (QUADS // 2))
            for t in range(TILES):
                pool.wait_ge(idx_ready, t + 1)
                for s in range(SLOTS):
                    gather(nc, k.g[:, t, s, :], k.t1_dram, k.idx[:, t, s:s + 1]).then_inc(k.gathered, 16)


def gather(nc, to, table, index):
    return nc.gpsimd.indirect_dma_start(
        out=to, out_offset=None, in_=table, in_offset=bass.IndirectOffsetOnAxis(ap=index, axis=0),
        bounds_check=NODES - 1, oob_is_err=False)


class Turning:

    GROUPS = TILES // 4
    CREDIT = 2

    def __init__(self, k, stack, name, calls, banks=None, dtype=F32, ident=None):
        self.k, self.calls, self.ident = k, calls, k.ident if ident is None else ident
        self.banks = banks or [k.ps(f"{name}_turn{i}", [P, BANK], stack, dtype) for i in range(2)]
        self.turned_sb = [k.sb(f"{name}_turned{i}", [P, BANK], stack=stack) for i in range(2)]
        self.turned, self.copied, self.used = (
            k.sem(f"{name}_turned_s"), k.sem(f"{name}_copied_s"), k.sem(f"{name}_used_s"))

    def start(self, act):
        act.sem_inc(self.copied, self.CREDIT)
        act.sem_inc(self.used, self.CREDIT)

    def base(self, rank, call):
        return rank * (self.calls * self.GROUPS) + call * self.GROUPS

    def done(self, rank, call):
        return rank * (self.calls * self.GROUPS) + ((call + 1) * self.GROUPS + self.CREDIT)

    def multiply(self, pe, rank, call, rows, table, out):
        nc = self.k.nc
        r = rank * (self.calls * self.GROUPS)
        blocks = rows.rearrange("p (q t) -> p q t", t=TILES)
        for g in range(self.GROUPS + 1):
            n = call * self.GROUPS + g
            if g < self.GROUPS:
                pe.wait_ge(self.copied, r + (n + 1))
                for j in range(4):
                    mm = nc.tensor.transpose(self.banks[g % 2][:, j * P:(j + 1) * P], blocks[:, :, 4 * g + j],
                                             self.ident[:, :])
                mm.then_inc(self.turned, 1)
            if g >= 1:
                pe.wait_ge(self.copied, r + (n - 1 + 1 + self.CREDIT))
                for j in range(4):
                    b = 4 * (g - 1) + j
                    mm = nc.tensor.matmul(out, self.turned_sb[(g - 1) % 2][:, j * P:(j + 1) * P], table(b),
                                          start=(b == 0), stop=(b == TILES - 1))
                mm.then_inc(self.used, 1)

    def copy(self, act, rank, call):
        nc = self.k.nc
        r = rank * (self.calls * self.GROUPS)
        for g in range(self.GROUPS):
            n = call * self.GROUPS + g
            act.wait_ge(self.turned, r + (n + 1))
            act.wait_ge(self.used, r + (n + 1))
            nc.scalar.activation(self.turned_sb[g % 2][:, :], self.banks[g % 2][:, :], ACT.Copy).then_inc(self.copied, 1)


@contextmanager
def flagged(k, eng):
    count = eng.value_load(k.count[0:1, 0:1], min_val=0, max_val=TILES)
    with eng.If(count > 0):
        with eng.Fori(0, count) as rank:
            yield eng.value_load(k.order[0:1, one(rank)], min_val=0, max_val=TILES - 1), rank
        eng.sem_inc(k.after_flagged, 1)


def plain_sums(k, eng, first, last):
    steps = QUAD * SLOTS
    with eng.Fori(first, last) as g:
        for s in range(SLOTS):
            for j in range(QUAD):
                to = k.x[:, one(g * QUAD + j), :].rearrange("p a c -> p (a c)")
                row = k.g[:, one(g * QUAD + j), s, 0:C].rearrange("p a c -> p (a c)")
                w = k.val[:, one(g * QUAD + j), s]
                if s == 0:
                    ins = k.nc.vector.tensor_scalar(to, row, w, None, ALU.mult)
                else:
                    eng.wait_ge(k.plain, g * steps + (s * QUAD + j - 3))
                    ins = k.nc.vector.scalar_tensor_tensor(to, row, w, to, ALU.mult, ALU.add)
                ins.then_inc(k.plain, 1)


def dense_logits(k, d):
    nc = k.nc
    st = ExitStack()
    with st:
        rows_sb = k.sb("d1_rows", [P, NODES], stack=st)
        mask = [k.sb(f"d1_mask{i}", [P, NODES], BF16, stack=st) for i in range(2)]
        ident_bf = k.sb("ident_bf", [P, P], BF16, stack=st)
        hwa = k.sb("d1_hwa", [P, TILES, 2 * HEADS], stack=st)
        pos = k.sb("d1_pos", [P, 2 * HEADS], stack=st)
        six = k.sb("d1_six", [P, 2 * HEADS], stack=st)
        acc = [k.ps(f"d1_acc{i}", [P, 512], st) for i in range(2)]
        turning = Turning(k, st, "d1", calls=2, dtype=BF16, ident=ident_bf)
        brow = [k.sb(f"gru_bias_rows{i}", [6, BANK], stack=st) for i in range(2)]
        zeroed, rows_in, split = k.sem("gru_bias_zeroed"), k.sem("gru_bias_in"), k.sem("gru_bias_split")
        table_in, loaded, free = k.sem("d1_table_in"), k.sem("d1_loaded"), k.sem("d1_free")
        undiag, masked, dve = k.sem("d1_undiag"), k.sem("d1_masked"), k.sem("d1_dve")
        rows = d["adj"].rearrange("(p t) j -> t p j", t=TILES)
        block = st.enter_context(nc.Block())

        @block.sync
        def _(sp):
            with flagged(k, sp) as (t, rank):
                sp.wait_ge(free, rank + 1)
                sp.sem_inc(k.paced, 1)
                sp.dma_start(rows_sb[:, :], rows[one(t)].rearrange("a p j -> p (a j)")).then_inc(loaded, 16)

        @block.vector
        def _(dve_):
            nc.vector.tensor_copy(ident_bf[:, :], k.ident[:, :])
            for cell in range(2):
                nc.vector.memset(brow[cell][:, :], 0.0).then_inc(zeroed, 1)
            dve_.sem_inc(free, 1)
            plain_sums(k, dve_, 0, QUADS // 2)
            dve_.wait_ge(rows_in, 16 * 6)
            link = Link(dve_, split)
            for cell in range(2):
                with ExitStack() as parts:
                    three_parts(k, link, f"gru_bias{cell}", brow[cell][:, :], k.gru_bias[cell][:, :], parts)
            with flagged(k, dve_) as (t, rank):
                dve_.wait_ge(loaded, rank * 16 + 16)
                diag = rows_sb[:, :].rearrange("p (q t) -> p q t", t=TILES)[:, :, one(t)]
                nc.vector.tensor_tensor(diag, diag, k.not_ident[:, :].rearrange("p (q o) -> p q o", o=1),
                                        ALU.mult).then_inc(undiag, 1)
                dve_.wait_ge(undiag, rank + 1)
                nc.vector.tensor_scalar(mask[0][:, :], rows_sb[:, :], 0.0, None, ALU.is_gt).then_inc(masked, 1)
                nc.vector.tensor_scalar(mask[1][:, :], rows_sb[:, :], 0.0, None, ALU.is_lt).then_inc(masked, 1)
                dve_.wait_ge(turning.used, turning.done(rank, 0))
                link = Link(dve_, dve, rank * 3)
                link(nc.vector.tensor_copy(pos[:, :], acc[0][:, 0:2 * HEADS]))
                dve_.wait_ge(turning.used, turning.done(rank, 1))
                nc.vector.tensor_tensor(six[:, 0:HEADS], pos[:, 0:HEADS], acc[1][:, HEADS:2 * HEADS], ALU.add)
                link(nc.vector.tensor_tensor(six[:, HEADS:], pos[:, HEADS:], acc[1][:, 0:HEADS], ALU.add))
                link(nc.vector.scalar_tensor_tensor(k.e6[:, one(t), :].rearrange("p a c -> p (a c)"), six[:, :],
                                                    ALPHA, six[:, :], ALU.mult, ALU.max))
                dve_.sem_inc(free, 1)

        @block.tensor
        def _(pe):
            pe.wait_ge(table_in, 16)
            with flagged(k, pe) as (t, rank):
                for call in range(2):
                    pe.wait_ge(masked, rank * 2 + (call + 1))
                    turning.multiply(pe, rank, call, mask[call][:, :], lambda b: hwa[:, b, :], acc[call][:, 0:2 * HEADS])

        @block.scalar
        def _(act):
            t1 = k.t1_dram.rearrange("(p t) c -> p t c", t=TILES)
            act.dma_start(hwa[:, :, :], t1[:, :, C:WIDE]).then_inc(table_in, 16)
            act.wait_ge(zeroed, 2)
            for row, bih, bhh in ((brow[0], "bih_e", "bhh_e"), (brow[1], "bih_n", "bhh_n")):
                r_z, new = d[bhh][:, 0:2 * C], d[bhh][:, 2 * C:3 * C]
                act.dma_start(row[0:3, 0:3 * C], d[bih].broadcast_to([3, 3 * C])).then_inc(rows_in, 16)
                act.dma_start(row[3:6, 0:2 * C], r_z.broadcast_to([3, 2 * C])).then_inc(rows_in, 16)
                act.dma_start(row[3:6, 3 * C:4 * C], new.broadcast_to([3, C])).then_inc(rows_in, 16)
            turning.start(act)
            with flagged(k, act) as (t, rank):
                for call in range(2):
                    turning.copy(act, rank, call)


QUAD_GATHERS = 16 * QUAD * SLOTS


def gather_all(k, pool, to, table, gathered):
    for g in range(QUADS):
        if g >= 2:
            pool.wait_ge(gathered[g % 2], QUAD_GATHERS * (g // 2))
        for t in range(g * QUAD, (g + 1) * QUAD):
            for s in range(SLOTS):
                gather(k.nc, to(t, s), table, k.idx[:, t, s:s + 1]).then_inc(gathered[g % 2], 16)


class Cells:

    LINKS = 4

    def __init__(self, k, stack, name, buffers, bank_s, bank_h, bank_g):
        self.k, self.buffers, self.bank_s, self.bank_h, self.bank_g = k, buffers, bank_s, bank_h, bank_g

        def sb(what, shape):
            return [k.sb(f"{name}_{what}{i}", shape, stack=stack) for i in range(buffers)]

        self.sums_t, self.h_t, self.rz = sb("sums_t", [P, BANK]), sb("h_t", [P, C]), sb("rz", [P, 2, 2 * C])
        self.n_in, self.new = sb("n_in", [P, 2, C]), sb("new", [P, 2, C])
        self.dif, self.both = sb("dif", [P, 2, C]), sb("both", [P, C])
        self.wih_e, self.whh_e, self.whh_n = (
            k.sb(f"{name}_{what}", [P, 3 * C], stack=stack) for what in ("wih_e", "whh_e", "whh_n"))
        self.loaded = k.sem(f"{name}_loaded")
        self.turned, self.copied, self.gated, self.squashed, self.inner_made, self.newed, self.done = (
            k.sem(f"{name}_{what}") for what in ("turned", "copied", "gated", "squashed", "inner_made", "newed", "done"))
        self.inner_link, self.blend_link = k.sem(f"{name}_inner_link"), k.sem(f"{name}_blend_link")

    def load(self, sp, d):
        sp.dma_start(self.wih_e[:, :], d["wih_e"]).then_inc(self.loaded, 16)
        sp.dma_start(self.whh_e[:, :], d["whh_e"]).then_inc(self.loaded, 16)
        sp.dma_start(self.whh_n[:, :], d["whh_n"]).then_inc(self.loaded, 16)

    def turn(self, b, sums, h1):
        nc = self.k.nc
        for j in range(4):
            nc.tensor.transpose(self.bank_s[b][:, j * C:(j + 1) * C], sums[:, j * C:(j + 1) * C], self.k.ident[:, :])
        nc.tensor.transpose(self.bank_h[b][:, 0:C], h1, self.k.ident[:, :]).then_inc(self.turned, 1)

    def copy(self, act, b, t):
        nc = self.k.nc
        act.wait_ge(self.turned, t + 1)
        nc.scalar.activation(self.sums_t[b][:, :], self.bank_s[b][:, :], ACT.Copy)
        nc.scalar.activation(self.h_t[b][:, :], self.bank_h[b][:, 0:C], ACT.Copy).then_inc(self.copied, 1)

    def product(self, pe, b, t):
        k, nc = self.k, self.k.nc
        pe.wait_ge(self.copied, t + 1)
        wait_from(pe, self.inner_made, t - (self.buffers - 1))
        for cell, whh in enumerate((self.whh_e, self.whh_n)):
            out = self.bank_g[b][:, cell, :]
            nc.tensor.matmul(out[:, 0:BANK], k.ones_bf[0:6, :], k.gru_bias[cell][:, :], start=True, stop=False)
            if cell == 0:
                nc.tensor.matmul(out[:, 0:3 * C], self.sums_t[b][:, 0:C], self.wih_e[:, :], start=False, stop=False)
            else:
                for h in range(HEADS):
                    nc.tensor.matmul(out[:, 0:3 * C], self.sums_t[b][:, (1 + h) * C:(2 + h) * C], k.ww[:, h, :],
                                     start=False, stop=False)
            nc.tensor.matmul(out[:, 0:2 * C], self.h_t[b][:, :], whh[:, 0:2 * C], start=False, stop=False)
            mm = nc.tensor.matmul(out[:, 3 * C:4 * C], self.h_t[b][:, :], whh[:, 2 * C:3 * C], start=False, stop=True)
        mm.then_inc(self.gated, 1)

    def squash(self, act, b, t):
        act.wait_ge(self.gated, t + 1)
        wait_from(act, self.done, t - (self.buffers - 1))
        self.k.nc.scalar.activation(self.rz[b][:, :, :], self.bank_g[b][:, :, 0:2 * C],
                                    ACT.Sigmoid).then_inc(self.squashed, 1)

    def inner(self, dve_, t, tiles=1):
        nc = self.k.nc
        for b in range(tiles):
            dve_.wait_ge(self.squashed, t + (b + 1))
            nc.vector.tensor_tensor(self.n_in[b][:, :, :], self.rz[b][:, :, 0:C], self.bank_g[b][:, :, 3 * C:4 * C],
                                    ALU.mult).then_inc(self.inner_link, 1)
        for b in range(tiles):
            dve_.wait_ge(self.inner_link, t + (b + 1))
            nc.vector.tensor_tensor(self.n_in[b][:, :, :], self.n_in[b][:, :, :], self.bank_g[b][:, :, 2 * C:3 * C],
                                    ALU.add).then_inc(self.inner_made, 1)

    def tanh(self, act, b, t):
        act.wait_ge(self.inner_made, t + 1)
        self.k.nc.scalar.activation(self.new[b][:, :, :], self.n_in[b][:, :, :], ACT.Tanh).then_inc(self.newed, 1)

    def blend(self, dve_, t, tiles):
        nc, n = self.k.nc, len(tiles)

        for number in range(self.LINKS + 1):
            for b, (h1, x, to, diagonal) in enumerate(tiles):
                new, dif, both = self.new[b][:, :, :], self.dif[b][:, :, :], self.both[b][:, :]
                if number == 0:
                    dve_.wait_ge(self.newed, t + (b + 1))
                    h2 = h1.rearrange("p (o c) -> p o c", o=1).broadcast_to([P, 2, C])
                    ins = nc.vector.tensor_tensor(dif, h2, new, ALU.subtract)
                else:
                    dve_.wait_ge(self.blend_link, t * self.LINKS + ((number - 1) * n + b + 1))
                if number == 1:
                    ins = nc.vector.tensor_tensor(dif, dif, self.rz[b][:, :, C:2 * C], ALU.mult)
                elif number == 2:
                    ins = nc.vector.tensor_tensor(dif, dif, new, ALU.add)
                elif number == 3:
                    ins = nc.vector.tensor_tensor(both, dif[:, 0, :], dif[:, 1, :], ALU.add)
                elif number == 4:
                    ins = nc.vector.scalar_tensor_tensor(to, both, diagonal, x, ALU.mult, ALU.add)
                ins.then_inc(self.blend_link if number < self.LINKS else self.done, 1)


def attend(k, d):
    nc = k.nc
    st = ExitStack()
    with st:
        e_pack = k.sb("e_pack", [P, TILES, HEADS], stack=st)
        far = k.sb("far", [P, TILES, SLOTS], stack=st)
        e_col = k.sb("e_col", [P, 2 * HEADS, TILES], stack=st)
        eg = k.sb("eg", [P, TILES, SLOTS, HEADS], stack=st)
        logit = [k.sb(f"logit{i}", [P, QUAD, HEADS, SLOTS], stack=st) for i in range(2)]
        prob = [k.sb(f"prob{i}", [P, QUAD, HEADS, SLOTS], stack=st) for i in range(2)]
        top = k.sb("row_max", [P, QUAD, HEADS], stack=st)
        den = k.sb("row_sum", [P, QUAD, HEADS], stack=st)
        rden = k.sb("row_rsum", [P, QUAD, HEADS], stack=st)
        weight = k.sb("weight", [P, QUAD, HEADS, SLOTS], stack=st)
        acc = [k.sb(f"sums{i}", [P, BANK], stack=st) for i in range(QUAD)]
        own = [k.sb(f"own_h{i}", [P, 2, C], stack=st) for i in range(2)]
        own_x = [k.sb(f"own_x{i}", [P, 2, C], stack=st) for i in range(2)]
        cells = Cells(k, st, "gru", 2, [k.ps(f"gru_bank_s{i}", [P, BANK], st) for i in range(2)],
                      [k.ps(f"gru_bank_h{i}", [P, 512], st) for i in range(2)],
                      [k.ps(f"gru_bank_g{i}", [P, 2, BANK], st) for i in range(2)])
        packed, stored, eg0, picked = k.sem("e_packed"), k.sem("e_stored"), k.sem("eg_zeroed"), k.sem("plain_picked")
        dve, shifted, exped, rounds = k.sem("p2_dve"), k.sem("p2_shifted"), k.sem("p2_exped"), k.sem("p2_rounds")
        own_in = [k.sem(f"own_h_in{i}") for i in range(2)]
        gathered = [k.sem(f"e_gathered{i}") for i in range(2)]
        PAIRS = TILES // 2
        ROUNDS = 2 * SLOTS
        OWN = PAIRS // 2
        block = st.enter_context(nc.Block())

        @block.sync
        def _(sp):
            sp.wait_ge(packed, 2)
            sp.dma_start(k.e_dram.rearrange("(p t) c -> p t c", t=TILES), e_pack[:, :, :]).then_inc(stored, 16)
            sp.dma_start(k.ecol_dram.rearrange("c (p t) -> p c t", t=TILES), e_col[:, :, :]).then_inc(stored, 16)
            cells.load(sp, d)
            t1 = k.t1_dram.rearrange("(p t) c -> p t c", t=TILES)
            x_rows = d["x"].rearrange("(p t) c -> p t c", t=TILES)
            for m in range(PAIRS):
                wait_from(sp, cells.done, 2 * (m - 1))
                sp.dma_start(own[m % 2][:, :, :], t1[:, 2 * m:2 * m + 2, 0:C]).then_inc(own_in[m % 2], 16)
                sp.dma_start(own_x[m % 2][:, :, :], x_rows[:, 2 * m:2 * m + 2, :]).then_inc(own_in[m % 2], 16)
            sp.wait_ge(stored, 32)

        @block.gpsimd
        def _(pool):
            nc.gpsimd.memset(eg[:, :, :, :], 0.0).then_inc(eg0, 1)
            pool.wait_ge(eg0, 1)
            pool.wait_ge(stored, 32)
            gather_all(k, pool, lambda t, s: eg[:, t, s, :], k.e_dram, gathered)

        @block.scalar
        def _(act):
            def pick(m, parity):
                wait_from(act, cells.turned, m * 2 - 2)
                for jj in range(2):
                    nc.scalar.activation(acc[2 * parity + jj][:, 0:C],
                                         k.x[:, one(m * 2 + jj), :].rearrange("p a c -> p (a c)"),
                                         ACT.Copy).then_inc(picked, 1)

            def copies(m):
                for jj in range(2):
                    cells.copy(act, jj, m * 2 + jj)

            def gates(m):
                for jj in range(2):
                    cells.squash(act, jj, m * 2 + jj)
                for jj in range(2):
                    cells.tanh(act, jj, m * 2 + jj)

            def step(g, b):
                m = g * 2
                if not isinstance(g, int) or g > 0:
                    copies(m - 1)
                act.wait_ge(shifted, g + 1)
                nc.scalar.activation(prob[b][:, :, :, :], logit[b][:, :, :, :], ACT.Exp).then_inc(exped, 1)
                pick(m, 0)
                if not isinstance(g, int) or g > 0:
                    gates(m - 1)
                pick(m + 1, 1)
                copies(m)
                gates(m)

            act.wait_ge(k.plain, QUAD * SLOTS * QUADS)
            by_quads(act, step)
            copies(PAIRS - 1)
            gates(PAIRS - 1)

        @block.vector
        def _(dve_):
            nc.vector.tensor_copy(e_pack[:, :, :], k.e6[:, :, 0:HEADS]).then_inc(packed, 1)
            nc.vector.tensor_copy(e_col[:, :, :], k.e6[:, :, :].rearrange("p t c -> p c t")).then_inc(packed, 1)
            nc.vector.tensor_scalar(far[:, :, :], k.val[:, :, :], 0.0, FAR, ALU.is_le, ALU.mult).then_inc(packed, 1)
            plain_sums(k, dve_, QUADS // 2, QUADS)
            dve_.wait_ge(packed, 3)
            dve_.wait_ge(k.plain, QUAD * SLOTS * QUADS)

            def wide(x):
                return x.rearrange("p t (c o) -> p t c o", o=1).broadcast_to([P, QUAD, HEADS, SLOTS])

            def over_heads(x, g):
                return x[:, bass.ts(g, QUAD), :].rearrange("p t (o s) -> p t o s", o=1).broadcast_to(
                    [P, QUAD, HEADS, SLOTS])

            def softmax(g, b):
                link = Link(dve_, dve, g * 6)
                dve_.wait_ge(gathered[b], (g - b) * (QUAD_GATHERS // 2) + QUAD_GATHERS)
                lg, pr = logit[b][:, :, :, :], prob[b][:, :, :, :]
                link(nc.vector.tensor_tensor(lg, eg[:, bass.ts(g, QUAD), :, :].rearrange("p t s c -> p t c s"),
                                             over_heads(far, g), ALU.add))
                link(nc.vector.tensor_reduce(top[:, :, :], lg, AX_X, ALU.max))
                nc.vector.tensor_tensor(lg, lg, wide(top[:, :, :]), ALU.subtract).then_inc(shifted, 1)
                dve_.wait_ge(exped, g + 1)
                link(nc.vector.tensor_reduce(den[:, :, :], pr, AX_X, ALU.add))
                link(nc.vector.reciprocal(rden[:, :, :], den[:, :, :]))
                link(nc.vector.tensor_tensor(weight[:, :, :, :], pr, wide(rden[:, :, :]), ALU.mult))
                link(nc.vector.tensor_tensor(weight[:, :, :, :], weight[:, :, :, :], over_heads(k.val, g), ALU.mult))

            def sums(g, pair):
                m = g * 2 + pair
                wait_from(dve_, cells.turned, m * 2 - 2)
                for s in range(SLOTS):
                    for jj in range(2):
                        j = 2 * pair + jj
                        t = g * QUAD + j
                        if s > 0:
                            dve_.wait_ge(rounds, m * ROUNDS + (2 * s + jj - 1))
                        row = k.g[:, one(t), s, 0:C].rearrange("p a c -> p (a c)")
                        for h in range(1, 1 + HEADS):
                            w = weight[:, j, h - 1, s:s + 1]
                            to = acc[j][:, h * C:(h + 1) * C]
                            if s == 0:
                                ins = nc.vector.tensor_scalar(to, row, w, None, ALU.mult)
                            else:
                                ins = nc.vector.scalar_tensor_tensor(to, row, w, to, ALU.mult, ALU.add)
                        ins.then_inc(rounds, 1)

            def gates(m, parity):
                cells.inner(dve_, m * 2, 2)
                cells.blend(dve_, m * 2, [
                    (own[parity][:, jj, :], own_x[parity][:, jj, :],
                     k.x[:, one(m * 2 + jj), :].rearrange("p a c -> p (a c)"), k.dcol[:, one(m * 2 + jj)])
                    for jj in range(2)])

            def step(g, b):
                softmax(g, b)
                sums(g, 0)
                if not isinstance(g, int) or g > 0:
                    gates(g * 2 - 1, 1)
                sums(g, 1)
                gates(g * 2, 0)

            by_quads(dve_, step)
            gates(PAIRS - 1, 1)

        @block.tensor
        def _(pe):
            pe.wait_ge(cells.loaded, 16 * 3)

            def pair_step(m, parity):
                pe.wait_ge(rounds, m * ROUNDS + ROUNDS)
                pe.wait_ge(own_in[parity], (m - parity) * 16 + 32)
                pe.wait_ge(picked, m * 2 + 2)
                for jj in range(2):
                    cells.turn(jj, acc[2 * parity + jj], own[parity][:, jj, :])
                for jj in range(2):
                    cells.product(pe, jj, m * 2 + jj)

            def step(g, b):
                for pair in range(2):
                    pair_step(g * 2 + pair, pair)

            by_quads(pe, step)


def dense_attend(k, d):
    nc = k.nc
    st = ExitStack()
    with st:
        rows_sb = k.sb("d2_rows", [P, NODES], stack=st)
        e_wide = [[k.sb(f"d2_e{n}_{half}", [P, NODES], stack=st) for half in range(2)] for n in range(2)]
        att = [k.sb(f"d2_att{i}", [P, NODES], stack=st) for i in range(HEADS)]
        blank = k.sem("d2_blank")
        positive = k.sb("d2_pos", [P, NODES], U8, stack=st)
        negative = k.sb("d2_neg", [P, NODES], U8, stack=st)
        h = k.sb("d2_h", [P, TILES, C], stack=st)
        top = k.sb("d2_top", [P, HEADS], stack=st)
        minus_top = k.sb("d2_minus_top", [P, HEADS], stack=st)
        carrier = k.sb("d2_carrier", [P, 2], stack=st)
        den = k.sb("d2_den", [P, HEADS], stack=st)
        rden = k.sb("d2_rden", [P, HEADS], stack=st)
        sums = k.sb("d2_sums", [P, BANK], stack=st)
        acc = k.ps("d2_acc", [P, BANK], st)
        own, x1 = k.sb("d2_own_h", [P, C], stack=st), k.sb("d2_x", [P, C], stack=st)
        turning = Turning(k, st, "d2", calls=1 + HEADS)
        cells = Cells(k, st, "d2_gru", 1, [k.ps("d2_bank_s", [P, BANK], st)], [k.ps("d2_bank_h", [P, 512], st)],
                      [k.ps("d2_bank_g", [P, 2, BANK], st)])
        x_in = k.sem("d2_x_in")
        table_in, loaded, finished = k.sem("d2_table_in"), k.sem("d2_loaded"), k.sem("d2_finished")
        e_in = [k.sem(f"d2_e_in{n}") for n in range(2)]
        e_used = k.sem("d2_e_used")
        undiag, ready, dve = k.sem("d2_undiag"), k.sem("d2_ready"), k.sem("d2_dve")
        topped, exped, summed = k.sem("d2_topped"), k.sem("d2_exped"), k.sem("d2_summed")
        rows = d["adj"].rearrange("(p t) j -> t p j", t=TILES)
        block = st.enter_context(nc.Block())

        @block.sync
        def _(sp):
            t1 = k.t1_dram.rearrange("(p t) c -> p t c", t=TILES)
            x_rows = d["x"].rearrange("(p t) c -> p t c", t=TILES)
            with flagged(k, sp) as (t, rank):
                sp.wait_ge(finished, rank + 1)
                sp.sem_inc(k.paced, 1)
                sp.dma_start(rows_sb[:, :], rows[one(t)].rearrange("a p j -> p (a j)")).then_inc(loaded, 16)
                for n in range(HEADS):
                    if n == 2:
                        sp.wait_ge(e_used, rank * HEADS + 1)
                        sp.sem_inc(k.paced, 1)
                    if n == 1:
                        sp.dma_start(h[:, :, :], t1[:, :, 0:C]).then_inc(table_in, 16)
                    for half in range(2):
                        c = n + HEADS * half
                        sp.dma_start(e_wide[n % 2][half][:, :],
                                     k.ecol_dram[c:c + 1, :].broadcast_to([P, NODES])).then_inc(e_in[n % 2], 16)
                sp.dma_start(x1[:, :], x_rows[:, one(t), :].rearrange("p a c -> p (a c)")).then_inc(x_in, 16)

        @block.vector
        def _(dve_):
            dve_.sem_inc(finished, 1)
            with flagged(k, dve_) as (t, rank):
                dve_.wait_ge(loaded, rank * 16 + 16)
                diag = rows_sb[:, :].rearrange("p (q t) -> p q t", t=TILES)[:, :, one(t)]
                nc.vector.tensor_tensor(diag, diag, k.not_ident[:, :].rearrange("p (q o) -> p q o", o=1),
                                        ALU.mult).then_inc(undiag, 1)
                dve_.wait_ge(undiag, rank + 1)
                link = Link(dve_, dve, rank * (2 + 4 * HEADS))
                link(nc.vector.tensor_scalar(positive[:, :], rows_sb[:, :], 0.0, None, ALU.is_gt))
                link(nc.vector.tensor_scalar(negative[:, :], rows_sb[:, :], 0.0, None, ALU.is_lt))
                for n in range(HEADS):
                    a = att[n][:, :]
                    dve_.wait_ge(blank, rank * HEADS + (n + 1))
                    dve_.sem_inc(k.paced, 1)
                    dve_.wait_ge(e_in[n % 2], rank * (64 if n != 1 else 32) + (32 if n < 2 else 64))
                    for half, mask in enumerate((positive, negative)):
                        nc.vector.memset(carrier[:, half:half + 1], 0.0)
                        link(nc.vector.copy_predicated(a, mask[:, :], e_wide[n % 2][half][:, :]))
                    dve_.sem_inc(e_used, 1)
                    link(nc.vector.tensor_reduce(top[:, n:n + 1], a, AX_X, ALU.max))
                    nc.vector.tensor_scalar(minus_top[:, n:n + 1], top[:, n:n + 1], -1.0, None,
                                            ALU.mult).then_inc(topped, 1)
                for n in range(HEADS):
                    dve_.wait_ge(exped, rank * HEADS + (n + 1))
                    link(nc.vector.reciprocal(rden[:, n:n + 1], den[:, n:n + 1]))
                dve_.wait_ge(turning.used, turning.done(rank, HEADS))
                nc.vector.tensor_copy(sums[:, 0:C], acc[:, 0:C])
                for n in range(HEADS):
                    nc.vector.tensor_scalar(sums[:, (n + 1) * C:(n + 2) * C], acc[:, (n + 1) * C:(n + 2) * C],
                                            rden[:, n:n + 1], None, ALU.mult)
                dve_.wait_ge(table_in, rank * 16 + 16)
                nc.vector.tensor_copy(own[:, :], h[:, one(t), :].rearrange("p a c -> p (a c)")).then_inc(summed, 1)
                cells.inner(dve_, rank)
                dve_.wait_ge(x_in, rank * 16 + 16)
                cells.blend(dve_, rank, [(own[:, :], x1[:, :], k.x[:, one(t), :].rearrange("p a c -> p (a c)"),
                                          k.dcol[:, one(t)])])
                dve_.wait_ge(cells.done, rank + 1)
                dve_.sem_inc(finished, 1)

        @block.gpsimd
        def _(pool):
            with flagged(k, pool) as (t, rank):
                pool.wait_ge(finished, rank + 1)
                pool.sem_inc(k.paced, 1)
                for n in range(HEADS):
                    nc.gpsimd.memset(att[n][:, :], NEG_INF).then_inc(blank, 1)
                for n in range(HEADS):
                    pool.wait_ge(exped, rank * HEADS + (n + 1))
                    nc.gpsimd.tensor_tensor(att[n][:, :], att[n][:, :], rows_sb[:, :], ALU.mult).then_inc(ready, 1)

        @block.scalar
        def _(act):
            cells.load(act, d)
            turning.start(act)
            with flagged(k, act) as (t, rank):
                turning.copy(act, rank, 0)
                for n in range(HEADS + 1):
                    if n < HEADS:
                        act.wait_ge(topped, rank * HEADS + (n + 1))
                        nc.scalar.activation(att[n][:, :], att[n][:, :], ACT.Exp, bias=minus_top[:, n:n + 1],
                                             accum_out=den[:, n:n + 1]).then_inc(exped, 1)
                    if n > 0:
                        turning.copy(act, rank, n)
                cells.copy(act, 0, rank)
                cells.squash(act, 0, rank)
                cells.tanh(act, 0, rank)

        @block.tensor
        def _(pe):
            pe.wait_ge(cells.loaded, 16 * 3)
            with flagged(k, pe) as (t, rank):
                pe.wait_ge(undiag, rank + 1)
                pe.wait_ge(table_in, rank * 16 + 16)
                turning.multiply(pe, rank, 0, rows_sb[:, :], lambda b: h[:, b, :], acc[:, 0:C])
                for n in range(HEADS):
                    pe.wait_ge(ready, rank * HEADS + (n + 1))
                    turning.multiply(pe, rank, n + 1, att[n][:, :], lambda b: h[:, b, :],
                                     acc[:, (n + 1) * C:(n + 2) * C])
                pe.wait_ge(summed, rank + 1)
                cells.turn(0, sums, own[:, :])
                cells.product(pe, 0, rank)


def ffn_weights(k, d):
    nc = k.nc
    st = ExitStack()
    with st:
        wt = k.sb("ffn_wt_in", [P, C], stack=st)
        w_scaled = k.sb("ffn_w_scaled", [P, C], stack=st)
        ln_w, ln_b = k.sb("ffn_ln_w", [P, 1], stack=st), k.sb("ffn_ln_b", [P, 1], stack=st)
        b_row = k.sb("ffn_b_in", [1, C], stack=st)
        ln_b3 = k.sb("ffn_ln_b3", [P, 3], stack=st)
        bias3 = k.sb("ffn_bias3", [3, C], stack=st)
        mean_row = k.sb("ffn_ones_mean", [P, P], stack=st)
        bank = k.ps("ffn_w_bank", [P, 512], st)
        bank_b = k.ps("ffn_b_bank", [3, 512], st)
        w_in, scaled, averaged = k.sem("ffn_w_in"), k.sem("ffn_w_scaled_s"), k.sem("ffn_averaged")
        rsd, ready, dve = k.sem("ln1_rstd"), k.sem("ln1_var"), k.sem("ln1_dve")
        block = st.enter_context(nc.Block())

        @block.sync
        def _(sp):
            for to, of in ((wt, "ffn_wt"), (ln_w, "ln_w"), (ln_b, "ln_b"), (b_row, "ffn_b")):
                sp.dma_start(to[:, :], d[of]).then_inc(w_in, 16)

        @block.tensor
        def _(pe):
            pe.wait_ge(w_in, 64)
            pe.wait_ge(scaled, 3)
            nc.tensor.matmul(bank[:, 0:C], mean_row[:, :], w_scaled[:, :], start=True, stop=True).then_inc(averaged, 1)
            nc.tensor.matmul(bank_b[:, 0:C], ln_b3[:, :], wt[:, :], start=True, stop=False)
            nc.tensor.matmul(bank_b[:, 0:C], k.ones[0:1, 0:3], b_row[:, :], start=False, stop=True).then_inc(averaged, 1)

        @block.gpsimd
        def _(pool):
            pool.wait_ge(ready, 1)
            for q in range(4):
                ts = slice(q * TILES // 4, (q + 1) * TILES // 4)
                nc.gpsimd.tensor_tensor(k.rstd[:, ts], k.var[:, ts], k.minus_half[:, ts], ALU.pow).then_inc(rsd, 1)

        @block.vector
        def _(dve_):
            dve_.wait_ge(w_in, 64)
            nc.vector.tensor_scalar(w_scaled[:, :], wt[:, :], ln_w[:, 0:1], None, ALU.mult).then_inc(scaled, 1)
            nc.vector.memset(mean_row[:, :], 1.0 / C).then_inc(scaled, 1)
            nc.vector.tensor_scalar(ln_b3[:, :], k.ones[:, 0:3], ln_b[:, 0:1], None, ALU.mult).then_inc(scaled, 1)
            link = Link(dve_, dve)
            layer_stats(k, dve_, link, k.x, ready)
            dve_.wait_ge(averaged, 2)
            nc.vector.tensor_tensor(k.ffn_wc[:, :], w_scaled[:, :], bank[:, 0:C], ALU.subtract)
            link(nc.vector.tensor_copy(bias3[:, :], bank_b[:, 0:C]))
            three_parts(k, link, "ffn_bias", bias3[:, :], k.ffn_bias[:, :], st)
            normalise(k, dve_, k.x, k.f0, rsd)


def normalise(k, eng, x, to, rsd):
    for t in range(TILES):
        if t % (TILES // 4) == 0:
            eng.wait_ge(rsd, t // (TILES // 4) + 1)
        k.nc.vector.tensor_scalar(to[:, t, :], x[:, t, :], k.mean[:, t:t + 1], k.rstd[:, t:t + 1],
                                  ALU.subtract, ALU.mult)


def feed_forward(k):
    nc = k.nc
    st = ExitStack()
    with st:
        act_out = [k.sb(f"ffn_silu{i}", [P, QUAD, C], stack=st) for i in range(QUADS)]
        diag = [k.sb(f"ffn_diag{i}", [P, QUAD, C], stack=st) for i in range(QUADS)]
        tanh = [k.sb(f"ffn_tanh{i}", [P, QUAD, C], stack=st) for i in range(2)]
        blend = [k.sb(f"ffn_blend{i}", [P, QUAD, C], stack=st) for i in range(2)]
        turned_sb = [k.sb(f"ffn_turned{i}", [P, BANK], stack=st) for i in range(2)]
        stats = [k.sb(f"ffn_stats{i}", [P, QUAD, 6], stack=st) for i in range(2)]
        dif = k.sb("ffn_dif", [P, QUAD], stack=st)
        sq = k.sb("ffn_sq", [P, QUAD], stack=st)
        both = k.sb("ffn_both", [P, QUAD], stack=st)
        var = [k.sb(f"ffn_var{i}", [P, QUAD], stack=st) for i in range(4)]
        rstd = [k.sb(f"ffn_rstd{i}", [P, QUAD], stack=st) for i in range(4)]
        s_own_diag = k.sem("ffn_s_own_diag")
        bank_t = [k.ps(f"ffn_bank_t{i}", [P, BANK], st) for i in range(4)]
        bank_z = [k.ps(f"ffn_bank_z{i}", [P, BANK], st) for i in range(4)]
        s_tanh, s_blend, s_silu, s_var, s_rstd, s_diag, s_turn, s_copy, s_z, dve = (
            k.sem("ffn_s_tanh"), k.sem("ffn_s_blend"), k.sem("ffn_s_silu"), k.sem("ffn_s_var"), k.sem("ffn_s_rstd"),
            k.sem("ffn_s_diag"), k.sem("ffn_s_turn"), k.sem("ffn_s_copy"), k.sem("ffn_s_z"), k.sem("ffn_dve"))
        ITEMS = ITERS * QUADS
        LINKS = 3
        block = st.enter_context(nc.Block())

        def schedule(eng, stages):
            def step(s, base):
                for stage, lag in stages:
                    j = s - lag
                    if base is not None or 0 <= j < ITEMS:
                        stage(j, base)
            last = ITEMS + max(lag for _, lag in stages)
            head = 2 * QUADS
            tail = ITEMS - QUADS
            for s in range(0, head):
                step(s, None)
            with eng.Fori(head // QUADS, tail // QUADS) as it:
                base = it * QUADS
                for g in range(QUADS):
                    step(g, base)
            for s in range(tail, last + 1):
                step(s, None)

        def at(j, base, n):
            return (j + n) if base is None else base + (j + n)

        def wait(eng, sem, j, base, n):
            if base is not None or j + n >= 1:
                eng.wait_ge(sem, at(j, base, n))

        def source(j, base):
            if base is None and j < QUADS:
                return k.f0[:, j * QUAD:(j + 1) * QUAD, :]
            return bank_z[j % 4][:, :].rearrange("p (q c) -> p q c", q=QUAD)

        T_TANH, T_SILU, T_BLEND, T_STATS, T_RSTD, T_DIAG, T_OWN_DIAG = 0, 1, 0, 2, 2, 3, 4
        T_TURN, T_COPY, T_PRODUCT = 5, 6, 6

        @block.scalar
        def _(act):
            def do_tanh(j, base):
                if base is not None or j >= QUADS:
                    wait(act, s_z, j, base, 1 - QUADS)
                wait(act, s_blend, j, base, -1)
                nc.scalar.activation(tanh[j % 2][:, :, :], source(j, base), ACT.Tanh).then_inc(s_tanh, 1)

            def do_silu(j, base):
                wait(act, s_blend, j, base, 1)
                wait(act, s_turn, j, base, 1 - QUADS)
                nc.scalar.activation(act_out[j % QUADS][:, :, :], blend[j % 2][:, :, :], ACT.Silu).then_inc(s_silu, 1)

            def do_copy(j, base):
                wait(act, s_turn, j, base, 1)
                wait(act, s_z, j, base, -1)
                nc.scalar.activation(turned_sb[j % 2][:, :], bank_t[j % 4][:, :], ACT.Copy).then_inc(s_copy, 1)

            def do_own_diag(j, base):
                wait(act, s_rstd, j, base, 1)
                wait(act, s_turn, j, base, 1 - QUADS)
                q = QUAD - 1
                nc.scalar.activation(diag[j % QUADS][:, q, :], k.ident[:, :], ACT.Copy,
                                     scale=rstd[j % 4][:, q:q + 1]).then_inc(s_own_diag, 1)

            schedule(act, [(do_copy, T_COPY), (do_tanh, T_TANH), (do_own_diag, T_OWN_DIAG), (do_silu, T_SILU)])

        @block.vector
        def _(dve_):
            def do_blend(j, base):
                wait(dve_, s_tanh, j, base, 1)
                wait(dve_, s_silu, j, base, -1)
                nc.vector.scalar_tensor_tensor(blend[j % 2][:, :, :], tanh[j % 2][:, :, :], 0.01, source(j, base),
                                               ALU.mult, ALU.add).then_inc(s_blend, 1)

            def do_moments(j, base):
                wait(dve_, s_silu, j, base, 1)
                stats_ = stats[j % 2]
                for q in range(QUAD):
                    ins = nc.vector.bn_stats(stats_[:, q, :], act_out[j % QUADS][:, q, :])
                ins.then_inc(dve, 1)

            def do_var(j, base):
                stats_ = stats[j % 2]
                n = at(j, base, 0) * LINKS
                dve_.wait_ge(dve, n + 1)
                nc.vector.tensor_tensor(dif[:, :], stats_[:, :, 1], stats_[:, :, 4], ALU.subtract).then_inc(dve, 1)
                nc.vector.scalar_tensor_tensor(both[:, :], stats_[:, :, 2], C * EPS, stats_[:, :, 5],
                                               ALU.add, ALU.add)
                dve_.wait_ge(dve, n + 2)
                nc.vector.scalar_tensor_tensor(sq[:, :], dif[:, :], 0.25, dif[:, :], ALU.mult, ALU.mult).then_inc(dve, 1)
                dve_.wait_ge(dve, n + 3)
                wait(dve_, s_rstd, j, base, -3)
                nc.vector.scalar_tensor_tensor(var[j % 4][:, :], both[:, :], 1.0 / C, sq[:, :],
                                               ALU.mult, ALU.add).then_inc(s_var, 1)

            schedule(dve_, [(do_moments, T_STATS), (do_blend, T_BLEND), (do_var, T_STATS)])
            for g in range(QUADS):
                dve_.wait_ge(s_z, ITEMS - QUADS + g + 1)
                xg = k.x[:, g * QUAD:(g + 1) * QUAD, :]
                nc.vector.tensor_tensor(xg, xg, bank_z[g % 4][:, :].rearrange("p (q c) -> p q c", q=QUAD),
                                        ALU.add).then_inc(s_blend, 1)

        @block.gpsimd
        def _(pool):
            ident = k.ident[:, :].rearrange("p (o c) -> p o c", o=1).broadcast_to([P, QUAD - 1, C])

            def do_rstd(j, base):
                wait(pool, s_var, j, base, 1)
                wait(pool, s_diag, j, base, -3)
                wait(pool, s_own_diag, j, base, -3)
                nc.gpsimd.tensor_tensor(rstd[j % 4][:, :], var[j % 4][:, :], k.minus_half[:, 0:QUAD], ALU.pow).then_inc(s_rstd, 1)

            def do_diag(j, base):
                wait(pool, s_rstd, j, base, 1)
                wait(pool, s_turn, j, base, 1 - QUADS)
                nc.gpsimd.tensor_tensor(diag[j % QUADS][:, 0:QUAD - 1, :], ident,
                                        rstd[j % 4][:, 0:QUAD - 1].rearrange("p (q o) -> p q o", o=1).broadcast_to(
                                            [P, QUAD - 1, C]),
                                        ALU.mult).then_inc(s_diag, 1)

            schedule(pool, [(do_rstd, T_RSTD), (do_diag, T_DIAG)])

        @block.tensor
        def _(pe):
            bias = k.ffn_bias[:, :].rearrange("p (o c) -> p o c", o=1).broadcast_to([3, QUAD, C])

            def do_turn(j, base):
                wait(pe, s_diag, j, base, 1)
                wait(pe, s_own_diag, j, base, 1)
                wait(pe, s_copy, j, base, -3)
                for q in range(QUAD):
                    mm = nc.tensor.matmul(bank_t[j % 4][:, q * C:(q + 1) * C], act_out[j % QUADS][:, q, :],
                                          diag[j % QUADS][:, q, :], start=True, stop=True)
                mm.then_inc(s_turn, 1)

            def do_product(j, base):
                wait(pe, s_copy, j, base, 1)
                wait(pe, s_blend, j, base, QUADS - 3)
                nc.tensor.matmul(bank_z[j % 4][:, :], k.ones_bf[0:3, :], bias, start=True, stop=False)
                for q in range(QUAD):
                    out = bank_z[j % 4][:, q * C:(q + 1) * C]
                    mm = nc.tensor.matmul(out, turned_sb[j % 2][:, q * C:(q + 1) * C], k.ffn_wc[:, :],
                                          start=False, stop=(q == QUAD - 1))
                mm.then_inc(s_z, 1)

            schedule(pe, [(do_turn, T_TURN), (do_product, T_PRODUCT)])


def poly_weights(k, d):
    nc = k.nc
    st = ExitStack()
    with st:
        w1t, bk = k.sb("poly_w1t", [KPOLY, C], stack=st), k.sb("poly_bk", [KPOLY, C], stack=st)
        bank = k.ps("poly_w_bank", [P, 512], st)
        w_in, made, ready, rsd, dve = (
            k.sem("poly_w_in"), k.sem("poly_w_made"), k.sem("ln2_var"), k.sem("ln2_rstd"), k.sem("ln2_dve"))
        block = st.enter_context(nc.Block())

        @block.sync
        def _(sp):
            sp.dma_start(k.poly_w1[:, 0:KPOLY], d["w1"]).then_inc(w_in, 16)
            sp.dma_start(w1t[:, :], d["w1t"]).then_inc(w_in, 16)
            sp.dma_start(bk[:, :], d["bk"]).then_inc(w_in, 16)
            sp.dma_start(k.poly_w2[:, :, :], d["w2"]).then_inc(w_in, 16)

        @block.tensor
        def _(pe):
            pe.wait_ge(w_in, 64)
            nc.tensor.matmul(bank[:, 0:C], w1t[:, :], bk[:, :], start=True, stop=True).then_inc(made, 1)

        @block.gpsimd
        def _(pool):
            pool.wait_ge(ready, 1)
            nc.gpsimd.tensor_tensor(k.rstd[:, :], k.var[:, :], k.minus_half[:, :], ALU.pow).then_inc(rsd, 1)

        @block.vector
        def _(dve_):
            layer_stats(k, dve_, Link(dve_, dve), k.x, ready)
            dve_.wait_ge(made, 1)
            nc.vector.tensor_copy(k.poly_w1[:, KPOLY:], bank[:, 0:C])
            dve_.wait_ge(rsd, 1)


def poly(k):
    nc = k.nc
    st = ExitStack()
    with st:
        SLOTS_SHARE = 2 * QUAD * SLOTS * C // TILES
        h4 = [k.sb(f"poly_h{i}", [P, QUAD, C], stack=st) for i in range(2)]
        h4t = [k.sb(f"poly_ht{i}", [P, BANK], stack=st) for i in range(2)]
        node = [k.sb(f"poly_node{i}", [P, KPOLY], stack=st) for i in range(2)]
        sums = [k.sb(f"poly_sums{i}", [P, 4, C], stack=st) for i in range(2)]
        zeros = k.sb("poly_zeros", [P, SLOTS_SHARE], stack=st)
        seeded, pool_link = k.sem("poly_seeded"), k.sem("poly_pool_link")
        bank_t = [k.ps(f"poly_bank_t{i}", [P, BANK], st) for i in range(2)]
        bank_n = [k.ps(f"poly_bank_n{i}", [P, 512], st) for i in range(2)]
        bank_w = [k.ps(f"poly_bank_w{i}", [P, BANK], st) for i in range(4)]
        normed, turned, copied, noded, put, wide, summed, done, stored, zeroed = (
            k.sem("poly_normed"), k.sem("poly_turned"), k.sem("poly_copied"), k.sem("poly_noded"), k.sem("poly_put"),
            k.sem("poly_wide"), k.sem("poly_summed"), k.sem("poly_done"), k.sem("poly_stored"), k.sem("poly_zeroed"))
        QUAD_WIDE = QUAD * 4
        STEPS = KPOLY - 4
        block = st.enter_context(nc.Block())

        @block.sync
        def _(sp):
            y_rows = k.y_dram.rearrange("(p t) c -> p t c", t=TILES)
            for i in range(QUADS // 2):
                sp.wait_ge(done, 2 * QUAD * (i + 1) + 2)
                ts = slice(2 * QUAD * i, 2 * QUAD * (i + 1))
                sp.dma_start(y_rows[:, ts, :], k.y[:, ts, :]).then_inc(stored, 16)
            sp.wait_ge(stored, 16 * (QUADS // 2))

        @block.gpsimd
        def _(pool):
            with pool.Fori(0, QUADS // 2) as i:
                for jj in range(2 * QUAD):
                    t = i * (2 * QUAD) + jj
                    part = sums[jj % 2]
                    pool.wait_ge(summed, t * STEPS + 2 * STEPS)
                    nc.gpsimd.tensor_tensor(part[:, 0:2, :], part[:, 0:2, :], part[:, 2:4, :],
                                            ALU.add).then_inc(pool_link, 1)
                    pool.wait_ge(pool_link, t + 1)
                    nc.gpsimd.tensor_tensor(k.y[:, one(t), :].rearrange("p a c -> p (a c)"), part[:, 0, :],
                                            part[:, 1, :], ALU.add).then_inc(done, 1)

        @block.scalar
        def _(act):
            act.sem_inc(wide, 2 * QUAD_WIDE)
            act.sem_inc(seeded, 1)
            with act.Fori(0, QUADS // 2) as i:
                for b in range(2):
                    act.wait_ge(turned, i * 2 + (b + 3))
                    act.wait_ge(wide, i * (2 * QUAD_WIDE) + (b + 1) * QUAD_WIDE)
                    nc.scalar.activation(h4t[b][:, :], bank_t[b][:, :], ACT.Copy).then_inc(copied, 1)
                for jj in range(2 * QUAD):
                    t = i * (2 * QUAD) + jj
                    act.wait_ge(noded, t + 1)
                    nc.scalar.activation(k.z[:, one(t), :].rearrange("p a c -> p (a c)"),
                                         bank_n[jj % 2][:, KPOLY:KPOLY + C], ACT.Copy)
                    act.wait_ge(done, t + 1)
                    nc.scalar.activation(node[jj % 2][:, :], bank_n[jj % 2][:, 0:KPOLY], ACT.Copy).then_inc(put, 1)
                    act.wait_ge(put, t + 3)
                    act.wait_ge(wide, t * 4 + (1 + 2 * QUAD_WIDE))
                    for c in range(4):
                        ins = nc.scalar.activation(sums[jj % 2][:, c, :], bank_w[0][:, c * C:(c + 1) * C], ACT.Copy,
                                                   scale=node[jj % 2][:, c:c + 1])
                    ins.then_inc(seeded, 1)

        @block.vector
        def _(dve_):
            slots = k.yg[:, :, :, :, :].rearrange("p a q s c -> p (a q s c)")
            nc.vector.memset(zeros[:, :], 0.0).then_inc(zeroed, 1)
            dve_.wait_ge(zeroed, 1)
            dve_.sem_inc(turned, 2)
            dve_.sem_inc(done, 2)
            dve_.sem_inc(summed, STEPS)
            with dve_.Fori(0, QUADS // 2) as i:
                for b in range(2):
                    dve_.wait_ge(turned, i * 2 + (b + 1))
                    for j in range(QUAD):
                        t = i * (2 * QUAD) + (b * QUAD + j)
                        ins = nc.vector.tensor_scalar(h4[b][:, j, :], k.x[:, one(t), :], k.mean[:, one(t)],
                                                      k.rstd[:, one(t)], ALU.subtract, ALU.mult)
                    ins.then_inc(normed, 1)
                for jj in range(2 * QUAD):
                    t = i * (2 * QUAD) + jj
                    values, part = node[jj % 2], sums[jj % 2]
                    nc.vector.tensor_copy(slots[:, bass.ts(t, SLOTS_SHARE)], zeros[:, :])
                    dve_.wait_ge(seeded, t + 2)
                    for m in range(4, KPOLY):
                        n, c = m // 4, m % 4
                        if c == 0:
                            dve_.wait_ge(wide, t * 4 + (n + 1 + 2 * QUAD_WIDE))
                        product, w, to = bank_w[n][:, c * C:(c + 1) * C], values[:, m:m + 1], part[:, c, :]
                        if n > 1:
                            dve_.wait_ge(summed, t * STEPS + (STEPS + m - 7))
                        nc.vector.scalar_tensor_tensor(to, product, w, to, ALU.mult, ALU.add).then_inc(summed, 1)

        @block.tensor
        def _(pe):
            pe.sem_inc(copied, 2)
            pe.sem_inc(put, 2)
            with pe.Fori(0, QUADS // 2) as i:
                for b in range(2):
                    pe.wait_ge(normed, i * 2 + (b + 1))
                    pe.wait_ge(copied, i * 2 + (b + 1))
                    for j in range(QUAD):
                        mm = nc.tensor.transpose(bank_t[b][:, j * C:(j + 1) * C], h4[b][:, j, :], k.ident[:, :])
                    mm.then_inc(turned, 1)
                for jj in range(2 * QUAD):
                    b, j = jj // QUAD, jj % QUAD
                    t = i * (2 * QUAD) + jj
                    if j == 0:
                        pe.wait_ge(copied, i * 2 + (b + 3))
                    lhs = h4t[b][:, j * C:(j + 1) * C]
                    pe.wait_ge(put, t + 1)
                    nc.tensor.matmul(bank_n[jj % 2][:, 0:KPOLY + C], lhs, k.poly_w1[:, :], start=True,
                                     stop=True).then_inc(noded, 1)
                    for n in range(4):
                        if n == 0:
                            pe.wait_ge(seeded, t + 1)
                        else:
                            pe.wait_ge(summed, t * STEPS + 4 * n)
                        nc.tensor.matmul(bank_w[n][:, :], lhs, k.poly_w2[:, 4 * n:4 * n + 4, :], start=True,
                                         stop=True).then_inc(wide, 1)



def spread_and_mix(k, d, out):
    nc = k.nc
    st = ExitStack()
    with st:
        router = k.sb("router", [P, EXPERTS], stack=st)
        w1, w2 = k.sb("moe_w1", [P, EXPERTS, C], stack=st), k.sb("moe_w2", [P, EXPERTS, C], stack=st)
        b1, b2 = k.sb("moe_b1", [P, EXPERTS], stack=st), k.sb("moe_b2", [3, EXPERTS * C], BF16, stack=st)
        b2_rows = k.sb("moe_b2_rows", [3, EXPERTS * C], stack=st)
        number_i, number_f = k.sb("moe_number_i", [P, EXPERTS], I32, stack=st), k.sb("moe_number", [P, EXPERTS], stack=st)
        rows_sb = k.sb("d3_rows", [P, NODES], stack=st)
        stats = k.sb("moe_stats", [P, QUAD, 6], stack=st)
        dif, sq, both = (k.sb(f"moe_{n}", [P, QUAD], stack=st) for n in ("dif", "sq", "both"))
        mean, var, rstd = ([k.sb(f"moe_{n}{i}", [P, QUAD], stack=st) for i in range(2)] for n in ("mean", "var", "rstd"))
        h4 = [k.sb(f"moe_h{i}", [P, QUAD, C], stack=st) for i in range(2)]
        h4t = [k.sb(f"moe_ht{i}", [P, BANK], stack=st) for i in range(2)]
        wide = [P, QUAD, EXPERTS]
        logit, prob, sorted_p, mask = (k.sb(f"moe_{n}", wide, stack=st) for n in ("logit", "prob", "sorted", "mask"))
        share = [k.sb(f"moe_share{i}", wide, stack=st) for i in range(2)]
        index = k.sb("moe_index", wide, U32, stack=st)
        index_f = k.sb("moe_index_f", [P, QUAD, 2], stack=st)
        top, den, rden = (k.sb(f"moe_{n}", [P, QUAD], stack=st) for n in ("top", "den", "rden"))
        hidden = [k.sb(f"moe_hidden{i}", [P, BANK], stack=st) for i in range(2)]
        bank_1 = [k.ps(f"moe_bank_1{i}", [P, BANK], st) for i in range(2)]
        bank_2 = [k.ps(f"moe_bank_2{i}", [P, BANK], st) for i in range(4)]
        bank_t = k.ps("moe_bank_t", [P, BANK], st)
        bank_s = k.ps("moe_bank_small", [P, BANK], st)
        acc = bank_s[:, 0:C]
        bank_l = bank_s[:, 2 * C:2 * C + QUAD * EXPERTS].rearrange("p (q e) -> p q e", q=QUAD)

        turning = Turning(k, st, "d3", calls=1, banks=bank_1)
        loaded, free, undiag = k.sem("d3_loaded"), k.sem("d3_free"), k.sem("d3_undiag")
        gathered = [k.sem(f"y_gathered{i}") for i in range(2)]
        rounds, w_in, numbered = k.sem("z_rounds"), k.sem("moe_w_in"), k.sem("moe_numbered")
        var_made, rstd_made, split, settled = (
            k.sem("moe_var_made"), k.sem("moe_rstd_made"), k.sem("moe_b2_split"), k.sem("moe_settled"))
        normed, turned, copied, routed, shifted, exped = (
            k.sem("moe_normed"), k.sem("moe_turned"), k.sem("moe_copied"), k.sem("moe_routed"),
            k.sem("moe_shifted"), k.sem("moe_exped"))
        first, gelued, second, mixed = k.sem("moe_first"), k.sem("moe_gelued"), k.sem("moe_second"), k.sem("moe_mixed")
        stored = k.sem("out_stored")
        rows = d["adj"].rearrange("(p t) j -> t p j", t=TILES)
        out_rows = out.rearrange("(p t) c -> p t c", t=TILES)
        ROUNDS = QUAD * (SLOTS + 1)
        MIXES = QUAD * EXPERTS
        WEIGHTS = 5
        block = st.enter_context(nc.Block())

        @block.sync
        def _(sp):
            loads = [(router[:, :], d["router_t"]), (w1[:, :, :], d["e_w1"]), (w2[:, :, :], d["e_w2"]),
                     (b1[:, :], d["e_b1"]), (b2_rows[:, :], d["e_b2"].broadcast_to([3, EXPERTS * C]))]
            assert len(loads) == WEIGHTS
            for to, of in loads:
                sp.dma_start(to, of).then_inc(w_in, 16)
            with flagged(k, sp) as (t, rank):
                sp.wait_ge(free, rank + 1)
                sp.sem_inc(k.paced, 1)
                sp.dma_start(rows_sb[:, :], rows[one(t)].rearrange("a p j -> p (a j)")).then_inc(loaded, 16)
            for g in range(QUADS):
                sp.wait_ge(mixed, MIXES * (g + 1))
                ts = slice(g * QUAD, (g + 1) * QUAD)
                sp.dma_start(out_rows[:, ts, :], k.x[:, ts, :]).then_inc(stored, 16)
            sp.wait_ge(stored, 16 * QUADS)

        @block.gpsimd
        def _(pool):
            nc.gpsimd.iota(number_i[:, :], pattern=[[1, EXPERTS]], base=0, channel_multiplier=0).then_inc(numbered, 1)
            pool.wait_ge(numbered, 1)
            nc.gpsimd.tensor_copy(number_f[:, :], number_i[:, :]).then_inc(numbered, 1)

            def power(g):
                pool.wait_ge(var_made, g + 1)
                nc.gpsimd.tensor_tensor(rstd[g % 2][:, :], var[g % 2][:, :], k.minus_half[:, 0:QUAD],
                                        ALU.pow).then_inc(rstd_made, 1)

            for g in range(QUADS):
                if g >= 2:
                    pool.wait_ge(gathered[g % 2], QUAD_GATHERS * (g // 2))
                    pool.wait_ge(rounds, ROUNDS * (g - 1))
                for j in range(QUAD):
                    for s in range(SLOTS):
                        gather(nc, k.yg[:, g % 2, j, s, :], k.y_dram,
                               k.idx[:, g * QUAD + j, s:s + 1]).then_inc(gathered[g % 2], 16)
                    if g >= 1 and j == 1:
                        power(g - 1)
            power(QUADS - 1)

        @block.vector
        def _(dve_):
            dve_.sem_inc(free, 1)
            with flagged(k, dve_) as (t, rank):
                z = k.z[:, one(t), :].rearrange("p a c -> p (a c)")
                dve_.wait_ge(loaded, rank * 16 + 16)
                diag = rows_sb[:, :].rearrange("p (q t) -> p q t", t=TILES)[:, :, one(t)]
                nc.vector.tensor_tensor(diag, diag, k.not_ident[:, :].rearrange("p (q o) -> p q o", o=1),
                                        ALU.mult).then_inc(undiag, 1)
                dve_.wait_ge(turning.used, turning.done(rank, 0))
                nc.vector.tensor_tensor(z, acc, z, ALU.add).then_inc(free, 1)
            nc.vector.drain()
            dve_.wait_ge(w_in, 16 * WEIGHTS)
            three_parts(k, Link(dve_, split), "moe_b2", b2_rows[:, :], b2[:, :], st)
            dve_.sem_inc(split, 1)
            dve_.wait_ge(numbered, 2)
            links_per_quad = 20

            def sums(g, b):
                dve_.wait_ge(gathered[b], (g - b) * (QUAD_GATHERS // 2) + QUAD_GATHERS)
                for s in range(-1, SLOTS):
                    for j in range(QUAD):
                        n = (s + 1) * QUAD + j
                        t = g * QUAD + j
                        to = k.z[:, one(t), :].rearrange("p a c -> p (a c)")
                        if s < 0:
                            row, w = k.y[:, one(t), :].rearrange("p a c -> p (a c)"), k.dcol[:, one(t)]
                        else:
                            row, w = k.yg[:, b, j, s, :], k.val[:, one(t), s]
                            dve_.wait_ge(rounds, g * ROUNDS + (n - 3))
                        nc.vector.scalar_tensor_tensor(to, row, w, to, ALU.mult, ALU.add).then_inc(rounds, 1)
                dve_.wait_ge(rounds, g * ROUNDS + ROUNDS)

            def statistics(g, b, link):
                xg = k.x[:, bass.ts(g, QUAD), :]
                link(nc.vector.scalar_tensor_tensor(xg, k.z[:, bass.ts(g, QUAD), :], 0.0, xg, ALU.max, ALU.add))
                dve_.sem_inc(k.paced, 1)
                for j in range(QUAD):
                    ins = nc.vector.bn_stats(stats[:, j, :], k.x[:, one(g * QUAD + j), :])
                link(ins)
                nc.vector.tensor_tensor(dif[:, :], stats[:, :, 1], stats[:, :, 4], ALU.subtract)
                nc.vector.tensor_tensor(mean[b][:, :], stats[:, :, 1], stats[:, :, 4], ALU.add)
                link(nc.vector.scalar_tensor_tensor(both[:, :], stats[:, :, 2], C * EPS, stats[:, :, 5],
                                                    ALU.add, ALU.add))
                nc.vector.tensor_scalar(mean[b][:, :], mean[b][:, :], 0.5, None, ALU.mult)
                link(nc.vector.scalar_tensor_tensor(sq[:, :], dif[:, :], 0.25, dif[:, :], ALU.mult, ALU.mult))
                nc.vector.scalar_tensor_tensor(var[b][:, :], both[:, :], 1.0 / C, sq[:, :],
                                               ALU.mult, ALU.add).then_inc(var_made, 1)

            def mix(g, b):
                for e in range(EXPERTS):
                    dve_.wait_ge(second, g * EXPERTS + (e + 1))
                    for j in range(QUAD):
                        n = e * QUAD + j
                        xt = k.x[:, one(g * QUAD + j), :].rearrange("p a c -> p (a c)")
                        if e > 0:
                            dve_.wait_ge(mixed, g * MIXES + (n - 3))
                        nc.vector.scalar_tensor_tensor(xt, bank_2[e % 4][:, j * C:(j + 1) * C],
                                                       share[b][:, j, e:e + 1], xt, ALU.mult, ALU.add).then_inc(mixed, 1)

            def norm(g, b, link):
                dve_.wait_ge(rstd_made, g + 1)
                for j in range(QUAD):
                    ins = nc.vector.tensor_scalar(h4[b][:, j, :], k.x[:, one(g * QUAD + j), :].rearrange("p a c -> p (a c)"),
                                                  mean[b][:, j:j + 1], rstd[b][:, j:j + 1], ALU.subtract, ALU.mult)
                ins.then_inc(normed, 1)
                dve_.wait_ge(normed, g + 1)
                xg = k.x[:, bass.ts(g, QUAD), :]
                link(nc.vector.tensor_tensor(xg, xg, h4[b][:, :, :], ALU.add))

            def route(g, b, link):
                def wide_of(x):
                    return x.rearrange("p (t o) -> p t o", o=1).broadcast_to(wide)

                dve_.wait_ge(routed, g + 1)
                link(nc.vector.tensor_copy(logit[:, :, :], bank_l))
                link(nc.vector.tensor_reduce(top[:, :], logit[:, :, :], AX_X, ALU.max))
                nc.vector.tensor_tensor(prob[:, :, :], logit[:, :, :], wide_of(top[:, :]),
                                        ALU.subtract).then_inc(shifted, 1)
                dve_.wait_ge(exped, g + 1)
                link(nc.vector.tensor_reduce(den[:, :], prob[:, :, :], AX_X, ALU.add))
                link(nc.vector.reciprocal(rden[:, :], den[:, :]))
                link(nc.vector.tensor_tensor(prob[:, :, :], prob[:, :, :], wide_of(rden[:, :]), ALU.mult))
                dve_.sem_inc(k.paced, 1)
                for j in range(QUAD):
                    ins = nc.vector.max(sorted_p[:, j, :], prob[:, j, :])
                link(ins)
                dve_.sem_inc(k.paced, 1)
                for j in range(QUAD):
                    ins = nc.vector.max_index(index[:, j, :], sorted_p[:, j, :], prob[:, j, :])
                link(nc.vector.tensor_tensor(den[:, :], sorted_p[:, :, 0], sorted_p[:, :, 1], ALU.add))
                nc.vector.tensor_copy(index_f[:, :, :], index[:, :, 0:2])
                link(nc.vector.tensor_scalar(den[:, :], den[:, :], 1e-12, None, ALU.max))
                link(nc.vector.reciprocal(rden[:, :], den[:, :]))
                number = number_f[:, :].rearrange("p (o e) -> p o e", o=1).broadcast_to(wide)
                nc.vector.tensor_tensor(share[b][:, :, :], number, wide_of(index_f[:, :, 0]), ALU.is_equal)
                link(nc.vector.tensor_tensor(mask[:, :, :], number, wide_of(index_f[:, :, 1]), ALU.is_equal))
                link(nc.vector.tensor_tensor(mask[:, :, :], mask[:, :, :], share[b][:, :, :], ALU.add))
                link(nc.vector.tensor_tensor(mask[:, :, :], mask[:, :, :], prob[:, :, :], ALU.mult))
                link(nc.vector.tensor_tensor(share[b][:, :, :], mask[:, :, :], wide_of(rden[:, :]), ALU.mult))

            def step(g, b):
                link = Link(dve_, settled, g * links_per_quad)
                sums(g, b)
                statistics(g, b, link)
                if not isinstance(g, int) or g > 0:
                    mix(g - 1, 1 - b)
                norm(g, b, link)
                route(g, b, link)
                while link.n < links_per_quad:
                    link.n += 1
                    dve_.sem_inc(settled, 1)

            by_quads(dve_, step)
            mix(QUADS - 1, 1)

        @block.tensor
        def _(pe):
            with flagged(k, pe) as (t, rank):
                pe.wait_ge(undiag, rank + 1)
                turning.multiply(pe, rank, 0, rows_sb[:, :], lambda b: k.y[:, b, :], acc)
            pe.wait_ge(w_in, 16 * WEIGHTS)

            def turn(g, b):
                pe.wait_ge(normed, g + 1)
                for j in range(QUAD):
                    mm = nc.tensor.transpose(bank_t[:, j * C:(j + 1) * C], h4[b][:, j, :], k.ident[:, :])
                mm.then_inc(turned, 1)
                pe.wait_ge(copied, g + 1)
                for j in range(QUAD):
                    mm = nc.tensor.matmul(bank_l[:, j, :], h4t[b][:, j * C:(j + 1) * C], router[:, :],
                                          start=True, stop=True)
                mm.then_inc(routed, 1)

            def experts(g, b):
                for e in range(EXPERTS + 1):
                    if e < EXPERTS:
                        wait_from(pe, gelued, g * EXPERTS + (e - 1))
                        nc.tensor.matmul(bank_1[e % 2][:, :], w1[:, e, :], h4t[b][:, :],
                                         start=True, stop=True).then_inc(first, 1)
                    if e >= 1:
                        m = e - 1
                        pe.wait_ge(gelued, g * EXPERTS + (m + 1))
                        wait_from(pe, mixed, g * MIXES + QUAD * (m - 3))
                        bias = b2[:, m * C:(m + 1) * C].rearrange("p (o c) -> p o c", o=1).broadcast_to([3, QUAD, C])
                        nc.tensor.matmul(bank_2[m % 4][:, :], k.ones_bf[0:3, :], bias, start=True, stop=False)
                        for j in range(QUAD):
                            mm = nc.tensor.matmul(bank_2[m % 4][:, j * C:(j + 1) * C],
                                                  hidden[m % 2][:, j * C:(j + 1) * C], w2[:, m, :],
                                                  start=False, stop=(j == QUAD - 1))
                        mm.then_inc(second, 1)

            def step(g, b):
                if not isinstance(g, int) or g > 0:
                    experts(g - 1, 1 - b)
                turn(g, b)

            pe.wait_ge(split, 8)
            by_quads(pe, step)
            experts(QUADS - 1, 1)

        @block.scalar
        def _(act):
            turning.start(act)
            with flagged(k, act) as (t, rank):
                turning.copy(act, rank, 0)
            act.wait_ge(w_in, 16 * WEIGHTS)

            def gelus(g):
                for e in range(EXPERTS):
                    act.wait_ge(first, g * EXPERTS + (e + 1))
                    wait_from(act, second, g * EXPERTS + (e - 1))
                    nc.scalar.activation(hidden[e % 2][:, :], bank_1[e % 2][:, :], ACT.Gelu,
                                         bias=b1[:, e:e + 1]).then_inc(gelued, 1)

            def step(g, b):
                if not isinstance(g, int) or g > 0:
                    gelus(g - 1)
                act.wait_ge(turned, g + 1)
                nc.scalar.activation(h4t[b][:, :], bank_t[:, :], ACT.Copy).then_inc(copied, 1)
                act.wait_ge(shifted, g + 1)
                nc.scalar.activation(prob[:, :, :], prob[:, :, :], ACT.Exp).then_inc(exped, 1)

            by_quads(act, step)
            gelus(QUADS - 1)


def program(nc, d, out):
    stack = ExitStack()
    with stack:
        k = Core(nc, stack)
        k.t1_dram = nc.dram_tensor("t1_rows", (NODES, WIDE), F32).ap()
        k.e_dram = nc.dram_tensor("e_rows", (NODES, HEADS), F32).ap()
        k.ecol_dram = nc.dram_tensor("e_columns", (2 * HEADS, NODES), F32).ap()
        k.y_dram = nc.dram_tensor("y_rows", (NODES, C), F32).ap()
        k.ident = k.sb("ident", [P, P])
        k.not_ident = k.sb("not_ident", [P, P])
        k.ones = k.sb("ones", [P, P])
        k.ones_bf = k.sb("ones_bf", [P, P], BF16)
        k.of_three = k.sb("of_three", [P, 3])
        k.tiny = k.sb("tiny", [P, 1])
        k.minus_half = k.sb("minus_half", [P, TILES])
        k.mean, k.var, k.rstd = k.sb("mean", [P, TILES]), k.sb("var", [P, TILES]), k.sb("rstd", [P, TILES])
        k.dif, k.sq = k.sb("dif", [P, TILES]), k.sb("sq", [P, TILES])
        k.stats = k.sb("stats", [P, TILES, 6])
        k.stats_s, k.stats_n = k.sem("stats_s"), 0
        k.dcol = k.sb("dcol", [P, TILES])
        k.val = k.sb("val", [P, TILES, SLOTS])
        k.idx = k.sb("idx", [P, TILES, SLOTS], U32)
        k.e6 = k.sb("e6", [P, TILES, 2 * HEADS])
        k.tiles_left = k.sb("tiles_left", [1, TILES])
        k.order = k.sb("order", [1, TILES], I32)
        k.count = k.sb("count", [1, 1], I32)
        k.after_flagged = k.sem("after_flagged")
        k.paced = k.sem("paced")
        k.gathered = k.sem("gathered")
        k.plain = k.sem("plain_sums")
        with ExitStack() as gnn:
            k.ww = k.sb("ww", [P, HEADS, 3 * C], stack=gnn)
            k.gru_bias = [k.sb(f"gru_bias{i}", [6, BANK], BF16, stack=gnn) for i in range(2)]
            k.x = k.sb("x", [P, TILES, C], stack=gnn)
            with ExitStack() as gat:
                k.g = k.sb("g", [P, TILES, SLOTS, WIDE], stack=gat)
                extract(k, d)
                dense_logits(k, d)
                attend(k, d)
            dense_attend(k, d)
            k.ffn_wc = k.sb("ffn_wc", [P, C], stack=gnn)
            k.ffn_bias = k.sb("ffn_bias", [3, C], BF16, stack=gnn)
            with ExitStack() as ffn:
                k.f0 = k.sb("f0", [P, TILES, C], stack=ffn)
                ffn_weights(k, d)
                feed_forward(k)
            with ExitStack() as gnn2:
                k.z = k.sb("z", [P, TILES, C], stack=gnn2)
                k.y = k.sb("y", [P, TILES, C], stack=gnn2)
                k.yg = k.sb("yg", [P, 2, QUAD, SLOTS, C], stack=gnn2)
                with ExitStack() as poly_stack:
                    k.poly_w1 = k.sb("poly_w1", [P, KPOLY + C], stack=poly_stack)
                    k.poly_w2 = k.sb("poly_w2", [P, KPOLY, C], stack=poly_stack)
                    poly_weights(k, d)
                    poly(k)
                spread_and_mix(k, d, out)


def kernel(**inputs):
    import numpy as _np
    import concourse.bacc as _bacc
    from concourse import mybir as _mybir
    from concourse.bass_utils import run_bass_kernel_spmd as _run

    nc = _bacc.Bacc("TRN2", target_bir_lowering=False, num_devices=1)
    arrays = lay_out(inputs)
    d = {}
    for name, a in arrays.items():
        d[name] = nc.dram_tensor(f"in_{name}", a.shape, _mybir.dt.from_np(a.dtype), kind="ExternalInput").ap()
    out = nc.dram_tensor("out_0", (NODES, C), F32, kind="ExternalOutput").ap()
    program(nc, d, out)
    r = _run(nc, [{f"in_{n}": a for n, a in arrays.items()}], core_ids=[0])
    return r.results[0]["out_0"]


def lay_out(inputs):
    import numpy as np

    i = {n: np.asarray(a) for n, a in inputs.items()}
    row = lambda a: a.reshape(1, -1)
    laid = {
        "x": i["x"],
        "adj": i["adj"],
        "gat_wt": i["L0_gnn_gat_W"].transpose(2, 0, 1),
        "gat_at": i["L0_gnn_gat_a"].reshape(HEADS, 2, C).transpose(2, 1, 0).reshape(C, 2 * HEADS),
        "wih_e": i["L0_gnn_edge_Wih"].T,
        "whh_e": i["L0_gnn_edge_Whh"].T,
        "wih_n": i["L0_gnn_node_Wih"].T,
        "whh_n": i["L0_gnn_node_Whh"].T,
        "bih_e": row(i["L0_gnn_edge_bih"]),
        "bhh_e": row(i["L0_gnn_edge_bhh"]),
        "bih_n": row(i["L0_gnn_node_bih"]),
        "bhh_n": row(i["L0_gnn_node_bhh"]),
        "ln_w": i["L0_ffn_ln_w"].reshape(C, 1),
        "ln_b": i["L0_ffn_ln_b"].reshape(C, 1),
        "ffn_wt": i["L0_ffn_W"].T,
        "ffn_b": row(i["L0_ffn_b"]),
        "w1": i["L1_gnn_W1"],
        "w1t": i["L1_gnn_W1"].T,
        "w2": i["L1_gnn_W2"].transpose(1, 0, 2),
        "bk": i["L1_gnn_b"],
        "router_t": i["L1_ffn_router_w"].T,
        "e_w1": i["L1_ffn_w1"].transpose(1, 0, 2),
        "e_b1": i["L1_ffn_b1"].T,
        "e_w2": i["L1_ffn_w2"].transpose(1, 0, 2),
        "e_b2": row(i["L1_ffn_b2"]),
    }
    return {n: np.ascontiguousarray(a) for n, a in laid.items()}
```
